# Optimizing a Trainium2 kernel written in Bass

```python
import numpy as np
import jax
import jax.numpy as jnp

def _softmax(x, axis=-1):
    return jax.nn.softmax(x, axis=axis)

def _gelu(x):
    return jax.nn.gelu(x, approximate=True)

def _silu(x):
    return jax.nn.silu(x)

def _sigmoid(x):
    return jax.nn.sigmoid(x)

def _layernorm(x, axis=-1, eps=1e-05):
    m = jnp.mean(x, axis=axis, keepdims=True)
    v = jnp.var(x, axis=axis, keepdims=True)
    return (x - m) / jnp.sqrt(v + eps)

def _scatter_add(tgt, idx, src, axis=0):
    return tgt.at[idx].add(src)

def _segment_sum(src, seg, n):
    return jax.ops.segment_sum(src, seg, n)
kernel_name = 'mk_vit_tower_d1_tok_img1024_r4_604493'

def setup_inputs(seed: int=0):
    np.random.seed(seed)
    _w = jnp.asarray

    def _rec_inputs():
        import jax
        import jax.numpy as jnp
        _rk = jax.random.key(seed)
        x = jax.random.uniform(jax.random.fold_in(_rk, 1), (8, 3, 256, 256), jnp.float32, 0.0, 1)
        return x
    x = _rec_inputs()

    def _L0_tok_setup():
        import jax, jax.numpy as jnp
        import numpy as np
        _GRAY_W = (0.2989, 0.587, 0.114)
        key = jax.random.key(seed)
        x = jax.random.uniform(key, (32, 3, 256, 256), dtype=jnp.float32)
        sx = jnp.array([[-3.0, 0.0, 3.0], [-10.0, 0.0, 10.0], [-3.0, 0.0, 3.0]], dtype=jnp.float32)
        scharr = jnp.stack([sx, sx.T])[:, None, :, :]
        return {'x': x, 'scharr': scharr}
    _L0_tok_all = _L0_tok_setup()
    _L0_tok_in = {k: v for k, v in _L0_tok_all.items() if k in ('scharr',)}
    del _L0_tok_all

    def _L0_attn_setup():
        import jax, jax.numpy as jnp
        import numpy as np
        HIDDEN = 256
        HEADS = 16
        key = jax.random.key(seed)
        ks = jax.random.split(key, 7)
        s = 1.0 / np.sqrt(HIDDEN)
        return {'x': jax.random.normal(ks[0], (4, 1024, HIDDEN), dtype=jnp.float32), 'Wq': jax.random.uniform(ks[1], (HIDDEN, HIDDEN), jnp.float32, -s, s), 'bq': jax.random.uniform(ks[2], (HIDDEN,), jnp.float32, -s, s), 'Wk': jax.random.uniform(ks[3], (HIDDEN, HIDDEN), jnp.float32, -s, s), 'bk': jax.random.uniform(ks[4], (HIDDEN,), jnp.float32, -s, s), 'Wv': jax.random.uniform(ks[5], (HIDDEN, HIDDEN), jnp.float32, -s, s), 'bv': jax.random.uniform(ks[6], (HIDDEN,), jnp.float32, -s, s)}
    _L0_attn_all = _L0_attn_setup()
    _L0_attn_in = {k: v for k, v in _L0_attn_all.items() if k in ('Wq', 'bq', 'Wk', 'bk', 'Wv', 'bv')}
    del _L0_attn_all

    def _L0_ffn_setup():
        import jax, jax.numpy as jnp
        import numpy as np
        TOP_K = 2
        EPS = 1e-09
        key = jax.random.key(seed)
        ks = jax.random.split(key, 6)
        B, T, D, H, E = (4, 512, 256, 512, 8)
        x = jax.random.normal(ks[0], (B, T, D), dtype=jnp.float32)
        Wg = jax.random.normal(ks[1], (E, D), dtype=jnp.float32) * 0.02
        W1 = jax.random.normal(ks[2], (E, 2 * H, D), dtype=jnp.float32) * 0.02
        b1 = jax.random.normal(ks[3], (E, 2 * H), dtype=jnp.float32) * 0.02
        Wo = jax.random.normal(ks[4], (D, H), dtype=jnp.float32) * 0.02
        bo = jax.random.normal(ks[5], (D,), dtype=jnp.float32) * 0.02
        return {'x': x, 'Wg': Wg, 'W1': W1, 'b1': b1, 'Wo': Wo, 'bo': bo}
    _L0_ffn_all = _L0_ffn_setup()
    _L0_ffn_in = {k: v for k, v in _L0_ffn_all.items() if k in ('Wg', 'W1', 'b1', 'Wo', 'bo')}
    del _L0_ffn_all
    return {'x': x, 'L0_tok_scharr': _L0_tok_in['scharr'], 'L0_attn_Wq': _L0_attn_in['Wq'], 'L0_attn_bq': _L0_attn_in['bq'], 'L0_attn_Wk': _L0_attn_in['Wk'], 'L0_attn_bk': _L0_attn_in['bk'], 'L0_attn_Wv': _L0_attn_in['Wv'], 'L0_attn_bv': _L0_attn_in['bv'], 'L0_ffn_Wg': _L0_ffn_in['Wg'], 'L0_ffn_W1': _L0_ffn_in['W1'], 'L0_ffn_b1': _L0_ffn_in['b1'], 'L0_ffn_Wo': _L0_ffn_in['Wo'], 'L0_ffn_bo': _L0_ffn_in['bo']}

def reference(x, L0_tok_scharr, L0_attn_Wq, L0_attn_bq, L0_attn_Wk, L0_attn_bk, L0_attn_Wv, L0_attn_bv, L0_ffn_Wg, L0_ffn_W1, L0_ffn_b1, L0_ffn_Wo, L0_ffn_bo):
    import jax
    import jax.numpy as jnp

    def _L0_tok_ref(x, scharr):
        import jax, jax.numpy as jnp
        import numpy as np
        _GRAY_W = (0.2989, 0.587, 0.114)
        w = jnp.asarray(_GRAY_W, dtype=x.dtype)
        gray = jnp.einsum('bchw,c->bhw', x, w)[:, None]
        edges = jax.lax.conv_general_dilated(gray, scharr, window_strides=(1, 1), padding='SAME', dimension_numbers=('NCHW', 'OIHW', 'NCHW'))
        abs_edges = jnp.sqrt(jnp.square(edges))
        edge = abs_edges.sum(axis=1) / 2
        return edge

    def _L0_attn_ref(x, Wq, bq, Wk, bk, Wv, bv):
        import jax, jax.numpy as jnp
        import numpy as np
        HIDDEN = 256
        HEADS = 16
        batch, len_, hidden = x.shape
        xh = x.reshape(batch, HEADS, len_ // HEADS, hidden)
        q = jnp.einsum('bhcd,ed->bhce', xh, Wq) + bq
        k = jnp.einsum('bhcd,ed->bhce', xh, Wk) + bk
        v = jnp.einsum('bhcd,ed->bhce', xh, Wv) + bv
        score = jax.nn.softmax(jnp.einsum('bhce,bhke->bhck', q, k), axis=-1)
        out = jnp.einsum('bhck,bhke->bhce', score, v)
        return out.reshape(batch, len_, hidden)

    def _L0_ffn_ref(x, Wg, W1, b1, Wo, bo):
        import jax, jax.numpy as jnp
        import numpy as np
        TOP_K = 2
        EPS = 1e-09
        E = Wg.shape[0]
        gate_logits = jnp.einsum('btd,ed->bte', x, Wg)
        gate_scores = jax.nn.softmax(gate_logits, axis=-1)
        topk_val, topk_idx = jax.lax.top_k(gate_scores, TOP_K)
        topk_val = topk_val / (topk_val.sum(axis=-1, keepdims=True) + EPS)
        comb = (jax.nn.one_hot(topk_idx, E, dtype=x.dtype) * topk_val[..., None]).sum(axis=-2)
        out = jnp.zeros_like(x)
        for e in range(E):
            h = jnp.einsum('btd,hd->bth', x, W1[e]) + b1[e]
            a, b = jnp.split(h, 2, axis=-1)
            g = a * jax.nn.sigmoid(b)
            eo = jnp.einsum('bth,dh->btd', g, Wo) + bo
            out = out + eo * comb[..., e:e + 1]
        return out
    h = _L0_tok_ref(x, L0_tok_scharr)
    h = h + _L0_attn_ref(_layernorm(h, axis=-1), L0_attn_Wq, L0_attn_bq, L0_attn_Wk, L0_attn_bk, L0_attn_Wv, L0_attn_bv)
    h = h + _L0_ffn_ref(_layernorm(h, axis=-1), L0_ffn_Wg, L0_ffn_W1, L0_ffn_b1, L0_ffn_Wo, L0_ffn_bo)
    return h

_drawn_inputs = setup_inputs


def setup_inputs(seed=0):
    import zlib

    import numpy as np

    out = dict(_drawn_inputs(seed))
    spreads = {}
    factors = {'L0_attn_bq': 3.052,
     'L0_attn_bk': 8.0,
     'L0_attn_bv': 4.179,
     'L0_ffn_Wg': 3.466,
     'L0_ffn_W1': 3.042,
     'L0_ffn_b1': 8.0,
     'L0_ffn_Wo': 3.039,
     'L0_ffn_bo': 7.611}
    for name, (base, spread) in spreads.items():
        noise = np.random.default_rng([zlib.crc32(name.encode()), seed]).standard_normal(out[name].shape)
        drawn = base * np.exp(spread * noise) if base else spread * noise
        out[name] = jnp.asarray(drawn.astype(out[name].dtype))
    for name, factor in factors.items():
        out[name] = (out[name] * factor).astype(out[name].dtype)
    return out
```

```python
from contextlib import ExitStack

import concourse.bass as bass
from concourse import mybir

F32 = mybir.dt.float32
F32R = mybir.dt.float32r
BF16 = mybir.dt.bfloat16
I32 = mybir.dt.int32
U32 = mybir.dt.uint32
ALU = mybir.AluOpType
ACT = mybir.ActivationFunctionType
AX = mybir.AxisListType

P = 128
IMAGES, CHANNELS, SIZE = 8, 3, 256
D = 256
KD = D // P
TILES_IN_IMAGE = SIZE // P
TILES = IMAGES * TILES_IN_IMAGE
HEAD = SIZE // 16
EXPERTS, TOP = 8, 2
H = 512
KH = H // P
REGION = IMAGES * SIZE + P
MAX_TILES = (IMAGES * SIZE * TOP + EXPERTS * (P - 1)) // P
LEAST_TILES = IMAGES * SIZE * TOP // P
ROWS = (EXPERTS + 1) * REGION
EPS_LN, EPS_TOP = 1e-5, 1e-9
GRAY = (0.2989, 0.587, 0.114)
NEVER = -3.0e38

C_ID, C_MASK, C_IOTA, C_BASE, C_SEL, C_TILE = 0, 128, 256, 264, 272, 274
C_UP = C_TILE + MAX_TILES
C_DOWN, C_BEFORE = C_UP + P, C_UP + 2 * P
C_ALL = C_UP + 3 * P


def shape_constants():
    import numpy as np
    c = np.zeros((P, C_ALL), np.float32)
    r = np.arange(P)
    c[:, C_ID:C_ID + P] = np.eye(P)
    c[:, C_UP:C_UP + P] = r[:, None] == r[None, :] - 1
    c[:, C_DOWN:C_DOWN + P] = r[:, None] == r[None, :] + 1
    c[:, C_MASK:C_MASK + P] = np.where(r[:, None] // HEAD == r[None, :] // HEAD, 0.0, NEVER)
    c[:, C_BEFORE:C_BEFORE + P] = r[:, None] < r[None, :]
    c[:, C_IOTA:C_IOTA + EXPERTS] = np.arange(EXPERTS)
    c[:, C_BASE:C_BASE + EXPERTS] = np.arange(EXPERTS) * REGION
    c[:9, C_SEL] = [1, 1, 1, 0, 0, 0, 1, 1, 1]
    c[:9, C_SEL + 1] = [0, 0, 0, 1, 1, 1, 0, 0, 0]
    c[:, C_TILE:C_TILE + MAX_TILES] = np.arange(MAX_TILES)
    return c


def build(nc, x, scharr, wqT, wkT, wvT, bq, bk, bv, wgT, w1T, b1, woT, bo, consts, zeros, out):
    ctx = ExitStack()
    with ctx:
        _build(nc, ctx, x, scharr, wqT, wkT, wvT, bq, bk, bv, wgT, w1T, b1, woT, bo, consts, zeros, out)


def _build(nc, ctx, x, scharr, wqT, wkT, wvT, bq, bk, bv, wgT, w1T, b1, woT, bo, consts, zeros, out):
    ds = bass.ds

    def sb(name, shape, dt=F32):
        return ctx.enter_context(nc.sbuf_tensor(name, shape, dt))

    def sem(name):
        return ctx.enter_context(nc.semaphore(name))

    rows_in = nc.dram_tensor("rows_in", (ROWS, D), F32, kind="Internal").ap()
    rows_gated = nc.dram_tensor("rows_gated", (MAX_TILES * P, H), F32, kind="Internal").ap()
    resid = nc.dram_tensor("resid", (TILES * P, D), F32, kind="Internal").ap()

    WE = KD * 2 * H
    w1_hi = sb("w1_hi", [P, EXPERTS * WE], F32R)
    w1_lo = sb("w1_lo", [P, EXPERTS * WE], F32R)
    LAST = (EXPERTS - 1) * WE
    GW = SIZE + 2
    gray_hi = w1_lo[:, LAST:LAST + 2 * GW].rearrange("p (t c) -> p t c", t=2)
    gray_lo = w1_lo[:, LAST + 2 * GW:LAST + 4 * GW].rearrange("p (t c) -> p t c", t=2)
    halo_in = w1_lo[0:9, LAST + 4 * GW:LAST + 4 * GW + 2 * SIZE].rearrange("p (t c) -> p t c", t=2)
    halo_w = w1_hi[0:9, LAST:LAST + 4 * P].rearrange("p (t k o) -> p t k o", t=2, k=2)
    front_w = sb("front_w", [P, 6 * 2 * P + 2 * 2 * KD * D], F32R)
    band = front_w[:, 0:12 * P].rearrange("p (g q o) -> p g q o", g=2, q=6)
    wqk = front_w[:, 12 * P:].rearrange("p (w g k e) -> p w g k e", w=2, g=2, k=KD)
    wv = w1_hi[:, LAST + 4 * P:LAST + 4 * P + 2 * KD * D].rearrange("p (g k e) -> p g k e", g=2, k=KD)
    wqkv = [wqk[:, 0], wqk[:, 1], wv]
    wo_h = front_w[:, 0:2 * KH * D].rearrange("p (g k e) -> p g k e", g=2, k=KH)
    shared = sb("shared", [P, EXPERTS * 2 * H])
    xs_img = shared[:, 0:3072].rearrange("p (b c t w) -> p b c t w", b=2, c=3, t=2)
    gray = shared[:, 3072:3584].rearrange("p (t w) -> p t w", t=2)
    xn1 = shared[:, 4096:4608].rearrange("p (t w) -> p t w", t=2)
    stage = shared[:, 4608:6656].rearrange("p (b w) -> p b w", b=2)
    stage_qkv = shared[:, 6656:8192].rearrange("p (w k e) -> p w k e", w=3, k=KD)
    edge = shared[:, 6656:7680].rearrange("p (t k w) -> p t k w", t=2, k=2)
    b1_all = shared[:, :]
    NB = 4
    top1 = shared[:, 0:NB * H].rearrange("p (b h) -> p b h", b=NB)
    top2 = shared[:, NB * H:2 * NB * H].rearrange("p (b h) -> p b h", b=NB)
    res_in = shared[:, 2 * NB * H:2 * NB * H + NB * D].rearrange("p (b d) -> p b d", b=NB)
    result = shared[:, 2 * NB * H + NB * D:2 * NB * H + 2 * NB * D].rearrange("p (b d) -> p b d", b=NB)
    work = sb("work", [P, 5888])
    h_all = work[:, 0:2048].rearrange("p (b t w) -> p b t w", b=4, t=2)
    xn2 = work[:, 2048:3072].rearrange("p (b t w) -> p b t w", b=2, t=2)
    xn2T = work[:, 3072:3584].rearrange("p (k n) -> p k n", k=KD)
    qT = work[:, 3584:4096].rearrange("p (k n) -> p k n", k=KD)
    kT = work[:, 4096:4608].rearrange("p (k n) -> p k n", k=KD)
    v_sb = work[:, 4608:5120].rearrange("p (t w) -> p t w", t=2)
    masked = work[:, 5120:5376].rearrange("p (t w) -> p t w", t=2)
    probs = work[:, 5376:5632].rearrange("p (t w) -> p t w", t=2)
    probsT = work[:, 5632:5888].rearrange("p (t w) -> p t w", t=2)
    band_raw = work[:, 2048:2048 + 6 * P].rearrange("p (q o) -> p q o", q=6)
    early = work[:, 2816:2816 + 3 * P]
    wo_raw = work[:, 4608:4608 + KH * D].rearrange("p (k e) -> p k e", k=KH)
    e_in = work[:, 0:2 * D].rearrange("p (b d) -> p b d", b=2)
    e_b = work[:, 512:512 + 2 * H].rearrange("p (b h) -> p b h", b=2)
    e_sig = work[:, 1536:1536 + 2 * H].rearrange("p (b h) -> p b h", b=2)
    e_a = work[:, 2560:2560 + 2 * H].rearrange("p (b h) -> p b h", b=2)
    e_out = work[:, 3584:3584 + 2 * H].rearrange("p (b h) -> p b h", b=2)
    xT = sb("xT", [P, 2 * KD * SIZE], F32R)
    xT_f = xT[:, :].rearrange("p (g k n) -> p g k n", g=2, k=KD)
    xT_e = xT[:, :].rearrange("p (b g k n) -> p b g k n", b=2, g=2, k=KD)

    sumT = [a.rearrange("p (g k t) -> p g k t", g=2, k=KH) for a in (front_w[:, 2 * KH * D:2 * KH * D + 2 * H], xT[:, :])]
    cst = sb("cst", [P, C_UP])
    ident = cst[:, C_ID:C_ID + P]
    before = sb("before", [P, P], BF16)
    ones = sb("ones", [P, P], BF16)
    bv_all = sb("bv_all", [P, D])
    bo_all = sb("bo_all", [P, D])
    bqk = sb("bqk", [P, 2 * KD])
    wg_sb = sb("wg_sb", [P, KD, EXPERTS])
    taps = sb("taps", [P, 18])
    htap = sb("htap", [9, 4, 6])
    htap_r = sb("htap_r", [9, 6], F32R)
    stats = sb("stats", [P, 2, 2, 6])
    mv = sb("mv", [P, 2, 2, 2])
    vare = sb("vare", [P, 2, 2])
    rstd = sb("rstd", [P, 2, 2])
    neg_half = sb("neg_half", [P, 2])
    smax = sb("smax", [P, 2])
    nsmax = sb("nsmax", [P, 2])
    ssum = sb("ssum", [P, 2])
    srec = sb("srec", [P, 2])
    gmax = sb("gmax", [P, 2])
    logit = sb("logit", [P, 2, EXPERTS])
    gexp = sb("gexp", [P, 2, EXPERTS])
    gsum = sb("gsum", [P, 2])
    grec = sb("grec", [P, 2])
    gprob = sb("gprob", [P, 2, EXPERTS])
    best = sb("best", [P, 2, 8])
    best_at = sb("best_at", [P, 2, 8], U32)
    best_f = sb("best_f", [P, 2, TOP])
    chosen_all = sb("chosen_all", [P, TILES, TOP, EXPERTS], BF16)
    hit = sb("hit", [P, 2, EXPERTS], BF16)
    earlier = sb("earlier", [P, 3, EXPERTS], BF16)
    den = sb("den", [P, 2])
    weight = sb("weight", [P, TILES * TOP])
    wsum = sb("wsum", [P, 2])
    place = sb("place", [P, 2, EXPERTS])
    placed = sb("placed", [P, 2, TOP, EXPERTS])
    place_f = sb("place_f", [P, 2, TOP])
    place_i = sb("place_i", [P, TILES, TOP], I32)
    gated_i = sb("gated_i", [P, TILES, TOP], I32)
    tiles_i = sb("tiles_i", [P, 2, EXPERTS], I32)
    tiles_f = sb("tiles_f", [P, EXPERTS])
    one8 = sb("one8", [P, EXPERTS])
    ends = sb("ends", [P, EXPERTS])
    shift = sb("shift", [P, EXPERTS])
    shifts = work[:, 4352:4352 + TILES * TOP * EXPERTS].rearrange("p (n e) -> p n e", e=EXPERTS)
    shift_of = work[:, 4320:4352]
    passed, passed_n = (work[0:1, 3072 + n * 512:3072 + n * 512 + MAX_TILES * EXPERTS].rearrange("p (j e) -> p j e", e=EXPERTS)
                        for n in range(2))
    expert_of, start_of, tiles_in, rows_before = (work[0:1, 4096 + n * 48:4096 + n * 48 + MAX_TILES] for n in range(4))
    tab_row = sb("tab_row", [1, MAX_TILES], I32)
    tab_w = sb("tab_w", [1, MAX_TILES], I32)
    tab_b = sb("tab_b", [1, MAX_TILES], I32)
    pad_f = sb("pad_f", [1, EXPERTS])
    pad_i = sb("pad_i", [1, EXPERTS], I32)

    bank = [ctx.enter_context(nc.psum_tensor(f"bank{i}", [P, 512], F32)) for i in range(8)]
    ps_conv = bank[0:2]
    ps_xT, ps_q, ps_k, ps_v, ps_s, ps_pv = bank[2:8]
    ps_rank, ps_xn2T, ps_gate, ps_pT = ps_q, ps_k, ps_s, ps_pv
    ps_et = bank[0:2]
    ps_a, ps_b = bank[2:4], bank[4:6]
    ps_ct = bank[6:8]
    ps_y = bank[0:2]

    S = {n: sem(n) for n in (
        "consts_in taps_in halo_taps_in qkv_in small_in regions_zeroed pads_set bf_set "
        "before_made bands_made bands_split halo_made qkv_hi qkv_split band_hi "
        "gray_first gray_made gray_hi_made gray_split halo_moved conv_done edge_made h_made "
        "mv1_made rstd1_made xn1_made xT_done xT_hi_made xT_split q_done k_done v_done q_made k_made v_made "
        "s_done masked_made probs_made pT_done pT_made pv_done srec_made h2_made mv2_made rstd2_made xn2_made "
        "xn2T_done xn2T_made gate_done logit_made gexp_made hits_made rank_done rank_read places_made "
        "res_made gated_places_made count_done tables_made padded b1_in wo_in wo_hi wo_split w1_hi_made w1_lo_made "
        "e_T e_hi e_split e_b_done e_a_done e_b_made e_sig_made e_a_read e_out_made "
        "c_first c_sum c_T c_hi c_split c_y c_out dve_step pool_step").split()}
    x_in = [sem(f"x_in{i}") for i in range(2)]
    stage_in = [sem(f"stage_in{i}") for i in range(2)]
    scattered = [sem(f"scattered{i}") for i in range(2)]
    res_stored = [sem(f"res_stored{i}") for i in range(4)]
    e_loaded = [sem(f"e_loaded{i}") for i in range(2)]
    e_stored = [sem(f"e_stored{i}") for i in range(2)]
    c_loaded = [sem(f"c_loaded{i}") for i in range(NB)]
    c_res = [sem(f"c_res{i}") for i in range(NB)]
    c_stored = [sem(f"c_stored{i}") for i in range(NB)]

    block = ctx.enter_context(nc.Block())

    STEPS = IMAGES + 3
    CHUNKS = EXPERTS * KD
    FREE_CHUNKS = CHUNKS - KD

    def chunks_of(step):
        return range(2 * step, min(2 * step + 2, FREE_CHUNKS)) if step < IMAGES else \
            range(FREE_CHUNKS, CHUNKS) if step == IMAGES else range(0)

    def live(u):
        return 0 <= u < IMAGES

    def three(k_range):
        return [(g, f, k) for k in k_range for g, f in ((0, 0), (0, 1), (1, 0))]

    def w1_chunk(c):
        return w1T[(c % KD) * P:(c % KD + 1) * P, c // KD, :]

    def weight_of(t, k):
        return weight[:, ds(TOP * t + k, 1)]

    @block.sync
    def _(sp):
        def load_image(u):
            if u >= 2:
                sp.wait_ge(S["gray_made"], u - 1)
            sp.dma_start(xs_img[:, u % 2], x[u].rearrange("c (t p) w -> p c t w", p=P)).then_inc(x_in[u % 2], 16)

        sp.dma_start(cst[:, :], consts[:, 0:C_UP]).then_inc(S["consts_in"], 16)
        sp.dma_start(early, consts[:, C_UP:C_ALL]).then_inc(S["consts_in"], 16)
        load_image(0)
        sp.dma_start(stage_qkv[:, 0], wqT.rearrange("(k p) e -> p k e", p=P)).then_inc(S["qkv_in"], 16)
        sp.dma_start(stage_qkv[:, 1], wkT.rearrange("(k p) e -> p k e", p=P)).then_inc(S["qkv_in"], 16)
        sp.dma_start(stage_qkv[:, 2], wvT.rearrange("(k p) e -> p k e", p=P)).then_inc(S["qkv_in"], 16)
        load_image(1)
        for n in range(MAX_TILES - LEAST_TILES):
            r = EXPERTS * REGION + n * P
            sp.dma_start(rows_in[r:r + P, :], zeros).then_inc(S["regions_zeroed"], 16)

        def halo(u):
            sp.wait_ge(S["gray_split"], u + 1)
            if u >= 1:
                sp.wait_ge(S["conv_done"], 2 * u)
            for t, row in ((0, 0), (1, P - 1)):
                for half, parts in ((gray_hi, (0, 3)), (gray_lo, (6,))):
                    src = half[row:row + 1, 1 - t, 0:SIZE]
                    wide = bass.AP(tensor=src.tensor, offset=src.offset, ap=[list(src.ap[0]), [1, 3], [1, SIZE]]).bitcast(F32)
                    for p0 in parts:
                        sp.dma_start(halo_in[p0:p0 + 3, t, :].bitcast(F32), wide).then_inc(S["halo_moved"], 16)

        halo(0)
        for s in range(STEPS):
            if live(s + 2):
                load_image(s + 2)
            if live(s + 1):
                halo(s + 1)
            if live(s - 3):
                u = s - 3
                sp.wait_ge(S["res_made"], 2 * (u + 1))
                sp.dma_start(resid[u * SIZE:(u + 1) * SIZE, :].rearrange("(t p) w -> p t w", p=P),
                             h_all[:, u % 4]).then_inc(res_stored[u % 4], 16)
            if s == IMAGES:
                sp.wait_ge(S["xT_done"], IMAGES)
                sp.wait_ge(S["qkv_split"], 3)
                sp.wait_ge(S["w1_lo_made"], CHUNKS)
                sp.dma_start(b1_all, b1.rearrange("e h -> (e h)").partition_broadcast(P)).then_inc(S["b1_in"], 16)
        sp.wait_ge(S["pv_done"], IMAGES)
        sp.dma_start(wo_raw, woT.rearrange("(k p) e -> p k e", p=P)).then_inc(S["wo_in"], 16)
        sp.wait_ge(S["tables_made"], 1)
        for e in range(EXPERTS):
            r = sp.value_load(pad_i[0:1, e:e + 1], min_val=0, max_val=ROWS - P)
            sp.dma_start(rows_in[ds(r, P), :], zeros).then_inc(S["padded"], 16)
        for n in range(2):
            sp.wait_ge(scattered[n], 16 * 4 * IMAGES // 2)
        sp.wait_ge(S["regions_zeroed"], 16 * (MAX_TILES - LEAST_TILES))
        sp.wait_ge(S["padded"], 16 * EXPERTS)
        for n in range(4):
            sp.wait_ge(res_stored[n], 16 * IMAGES // 4)

        def load_rows(j, p):
            r = sp.value_load(tab_row[0:1, ds(j, 1)], min_val=0, max_val=ROWS - P)
            sp.dma_start(e_in[:, p, :], rows_in[ds(r, P), :]).then_inc(e_loaded[p], 16)

        def store_rows(j, p):
            sp.wait_ge(S["e_out_made"], j + 1)
            sp.dma_start(rows_gated[ds(j * P, P), :], e_out[:, p, :]).then_inc(e_stored[p], 16)

        load_rows(0, 0)
        load_rows(1, 1)
        LOOPED = (MAX_TILES - 3) // 2
        with sp.Fori(0, LOOPED) as i:
            for p in range(2):
                sp.wait_ge(S["e_T"], 2 * i + p + 1)
                load_rows(2 * i + p + 2, p)
                store_rows(2 * i + p, p)
        for j in range(2 * LOOPED, MAX_TILES):
            if j + 2 < MAX_TILES:
                sp.wait_ge(S["e_T"], j + 1)
                load_rows(j + 2, j % 2)
            store_rows(j, j % 2)

        sp.wait_ge(S["e_a_read"], MAX_TILES)
        for b in range(NB):
            sp.dma_start(res_in[:, b, :], resid[b * P:(b + 1) * P, :]).then_inc(c_res[b], 16)
        with sp.Fori(0, TILES // NB - 1) as i:
            for b in range(NB):
                t = NB * i + b
                sp.wait_ge(S["c_out"], t + 1)
                sp.dma_start(out[ds(t * P, P), :], result[:, b, :]).then_inc(c_stored[b], 16)
                sp.dma_start(res_in[:, b, :], resid[ds((t + NB) * P, P), :]).then_inc(c_res[b], 16)
        for b in range(NB):
            t = TILES - NB + b
            sp.wait_ge(S["c_out"], t + 1)
            sp.dma_start(out[t * P:(t + 1) * P, :], result[:, b, :]).then_inc(c_stored[b], 16)
        for b in range(NB):
            sp.wait_ge(c_stored[b], 16 * TILES // NB)

    @block.scalar
    def _(act):
        act.dma_start(taps[:, :], scharr.rearrange("k o a b -> (k o a b)").partition_broadcast(P)).then_inc(S["taps_in"], 16)
        for c in range(3):
            with nc.allow_non_contiguous_dma(reason="18 values"):
                act.dma_start(htap[3 * c:3 * c + 3, 0, :], scharr.rearrange("k o a b -> b (k o a)")).then_inc(S["halo_taps_in"], 16)
        act.dma_start(bv_all[:, :], bv.partition_broadcast(P)).then_inc(S["small_in"], 16)
        act.dma_start(bo_all[:, :], bo.partition_broadcast(P)).then_inc(S["small_in"], 16)
        with nc.allow_non_contiguous_dma(reason="256 values each"):
            act.dma_start(bqk[:, 0:KD], bq.rearrange("(k p) -> p k", p=P)).then_inc(S["small_in"], 16)
            act.dma_start(bqk[:, KD:2 * KD], bk.rearrange("(k p) -> p k", p=P)).then_inc(S["small_in"], 16)
            act.dma_start(wg_sb[:, :, :], wgT.rearrange("(k p) e -> p k e", p=P)).then_inc(S["small_in"], 16)

        def gray_first(u):
            act.wait_ge(x_in[u % 2], 16 * (u // 2 + 1))
            if u >= 1:
                act.wait_ge(S["gray_split"], u)
            act.activation(gray, xs_img[:, u % 2, 0], ACT.Copy, scale=GRAY[0]).then_inc(S["gray_first"], 1)

        def gray_high(u):
            act.wait_ge(S["gray_made"], u + 1)
            if u >= 1:
                act.wait_ge(S["conv_done"], 2 * u)
            act.activation(gray_hi[:, :, 1:1 + SIZE], gray, ACT.Copy).then_inc(S["gray_hi_made"], 1)

        def edges(u, t):
            act.wait_ge(S["conv_done"], 2 * u + t + 1)
            if u >= 1:
                act.wait_ge(S["h_made"], 2 * u + t - 1)
            else:
                act.wait_ge(S["qkv_split"], 3)
            act.activation(edge[:, t], ps_conv[t][:, :].rearrange("p (k w) -> p k w", k=2), ACT.Abs).then_inc(S["edge_made"], 1)

        def split_high(c):
            act.wait_ge(stage_in[c % 2], 16 * (c // 2 + 1))
            if c >= FREE_CHUNKS:
                act.wait_ge(S["v_done"], IMAGES)
            act.activation(w1_hi[:, c * 2 * H:(c + 1) * 2 * H], stage[:, c % 2, :], ACT.Copy)\
               .then_inc(S["w1_hi_made"], 1)

        gray_first(0)
        act.wait_ge(S["bands_made"], 6)
        act.activation(band[:, 0], band_raw, ACT.Copy).then_inc(S["band_hi"], 1)
        gray_high(0)
        act.wait_ge(S["qkv_in"], 48)
        for w in range(3):
            act.activation(wqkv[w][:, 0], stage_qkv[:, w], ACT.Copy).then_inc(S["qkv_hi"], 1)
        act.wait_ge(S["small_in"], 80)

        for s in range(STEPS):
            if live(s - 1):
                u = s - 1
                act.wait_ge(S["xT_done"], u + 1)
                if u >= 1:
                    act.wait_ge(S["v_done"], u)
                act.activation(xT_f[:, 0], ps_xT[:, :].rearrange("p (k n) -> p k n", k=KD), ACT.Copy)\
                   .then_inc(S["xT_hi_made"], 1)
            if live(s - 2):
                u = s - 2
                act.wait_ge(S["pT_done"], u + 1)
                if u >= 1:
                    act.wait_ge(S["pv_done"], u)
                act.activation(probsT, ps_pT[:, 0:2 * P].rearrange("p (t n) -> p t n", t=2), ACT.Copy)\
                   .then_inc(S["pT_made"], 1)
            if live(s + 1):
                gray_first(s + 1)
            if live(s - 3):
                u = s - 3
                act.wait_ge(S["logit_made"], u + 1)
                act.activation(gexp[:, :, :], logit[:, :, :], ACT.Exp).then_inc(S["gexp_made"], 1)
            if live(s):
                edges(s, 0)
            if live(s - 1):
                u = s - 1
                for n, (done, made, ps, dst) in enumerate((("q_done", "q_made", ps_q, qT), ("k_done", "k_made", ps_k, kT))):
                    act.wait_ge(S[done], u + 1)
                    if u >= 1:
                        act.wait_ge(S["s_done"], u)
                    for m in range(KD):
                        act.activation(dst[:, m], ps[:, m * SIZE:(m + 1) * SIZE], ACT.Identity,
                                       bias=bqk[:, n * KD + m:n * KD + m + 1]).then_inc(S[made], 1)
            if live(s):
                edges(s, 1)
            for c in chunks_of(s)[0:1]:
                split_high(c)
            if live(s + 1):
                gray_high(s + 1)
            if live(s - 1):
                u = s - 1
                act.wait_ge(S["masked_made"], u + 1)
                if u >= 1:
                    act.wait_ge(S["pT_done"], u)
                    act.wait_ge(S["srec_made"], u)
                for t in range(2):
                    act.activation(probs[:, t], masked[:, t], ACT.Exp, bias=nsmax[:, t:t + 1],
                                   accum_out=ssum[:, t:t + 1]).then_inc(S["probs_made"], 1)
            if live(s - 2):
                u = s - 2
                act.wait_ge(S["xn2T_done"], u + 1)
                if u >= 1:
                    act.wait_ge(S["gate_done"], u)
                act.activation(xn2T, ps_xn2T[:, :].rearrange("p (k n) -> p k n", k=KD), ACT.Copy)\
                   .then_inc(S["xn2T_made"], 1)
            for c in chunks_of(s)[1:2]:
                split_high(c)

        act.wait_ge(S["wo_in"], 16)
        act.wait_ge(S["v_done"], IMAGES)
        act.activation(wo_h[:, 0], wo_raw, ACT.Copy).then_inc(S["wo_hi"], 1)

        def e_high(j, p, first=False):
            act.wait_ge(S["e_T"], j + 1)
            if not first:
                act.wait_ge(S["e_a_done"], j - 1)
            act.activation(xT_e[:, p, 0], ps_et[p][:, 0:KD * P].rearrange("p (k n) -> p k n", k=KD), ACT.Copy)\
               .then_inc(S["e_hi"], 1)

        def e_sigmoid(j, p, first=False):
            act.wait_ge(S["e_b_made"], j + 1)
            if not first:
                act.wait_ge(S["e_out_made"], j - 1)
            act.activation(e_sig[:, p], e_b[:, p], ACT.Sigmoid).then_inc(S["e_sig_made"], 1)

        e_high(0, 0, True)
        e_high(1, 1, True)
        e_sigmoid(0, 0, True)
        e_high(2, 0)
        e_sigmoid(1, 1, True)
        with act.Fori(1, MAX_TILES // 2) as i:
            e_high(2 * i + 1, 1)
            e_sigmoid(2 * i, 0)
            e_high(2 * i + 2, 0)
            e_sigmoid(2 * i + 1, 1)
        e_sigmoid(MAX_TILES - 1, 0)

        def c_high(t, p, first=False):
            act.wait_ge(S["c_T"], t + 1)
            if not first:
                act.wait_ge(S["c_y"], t - 1)
            act.activation(sumT[p][:, 0], ps_ct[p][:, :].rearrange("p (k n) -> p k n", k=KH), ACT.Copy)\
               .then_inc(S["c_hi"], 1)

        def c_first(t, b, at16):
            act.wait_ge(c_loaded[b], at16)
            act.activation(top1[:, b], top1[:, b], ACT.Copy, scale=weight_of(t, 0)).then_inc(S["c_first"], 1)

        c_first(0, 0, 32)
        for t in range(NB):
            c_first(t + 1, (t + 1) % NB, 32 * ((t + 1) // NB + 1))
            c_high(t, t % 2, t < 2)
        with act.Fori(1, TILES // NB - 1) as i:
            for b in range(NB):
                t = NB * i + b
                c_first(t + 1, (b + 1) % NB, 32 * i + 32 * ((b + 1) // NB + 1))
                c_high(t, b % 2)
        for t in range(TILES - NB, TILES):
            if t + 1 < TILES:
                c_first(t + 1, (t + 1) % NB, 32 * ((t + 1) // NB + 1))
            c_high(t, t % 2)


    @block.gpsimd
    def _(pool):
        def split_low(c):
            pool.wait_ge(S["w1_hi_made"], c + 1)
            cols = slice(c * 2 * H, (c + 1) * 2 * H)
            pool.tensor_tensor(w1_lo[:, cols], stage[:, c % 2, :], w1_hi[:, cols].bitcast(F32), ALU.subtract)\
                .then_inc(S["w1_lo_made"], 1)
            if c + 2 < CHUNKS:
                pool.wait_ge(S["w1_lo_made"], c + 1)
                pool.dma_start(stage[:, c % 2, :], w1_chunk(c + 2)).then_inc(stage_in[c % 2], 16)

        steps = 0

        def inverse_deviation(norm, u, moments, made):
            nonlocal steps
            pool.wait_ge(S[moments], u + 1)
            pool.tensor_scalar(vare[:, norm], mv[:, norm, :, 1], EPS_LN, None, ALU.add).then_inc(S["pool_step"], 1)
            steps += 1
            pool.wait_ge(S["pool_step"], steps)
            pool.tensor_tensor(rstd[:, norm], vare[:, norm], neg_half[:, :], ALU.pow).then_inc(S[made], 1)

        for c in range(2):
            pool.dma_start(stage[:, c, :], w1_chunk(c)).then_inc(stage_in[c], 16)
        pool.memset(neg_half[:, :], -0.5).then_inc(S["pool_step"], 1)
        steps += 1
        pool.wait_ge(S["pool_step"], steps)

        for s in range(STEPS):
            for c in chunks_of(s)[0:1]:
                split_low(c)
            if live(s):
                inverse_deviation(0, s, "mv1_made", "rstd1_made")
            if live(s - 2):
                inverse_deviation(1, s - 2, "mv2_made", "rstd2_made")
            for c in chunks_of(s)[1:2]:
                split_low(c)
            if live(s - 3):
                u = s - 3
                pool.wait_ge(S["places_made"], u + 1)
                for t in range(2):
                    for k in range(TOP):
                        pool.indirect_dma_start(
                            rows_in, bass.IndirectOffsetOnAxis(ap=place_i[:, 2 * u + t, k:k + 1], axis=0),
                            xn2[:, u % 2, t, :], None).then_inc(scattered[u % 2], 16)

        pool.wait_ge(S["gated_places_made"], 1)
        pool.wait_ge(S["e_a_read"], MAX_TILES)
        for p in range(2):
            pool.wait_ge(e_stored[p], 16 * ((MAX_TILES + 1 - p) // 2))
        for t in range(TILES):
            if t >= NB:
                pool.wait_ge(S["c_T"], t - NB + 1)
            for k, rows in enumerate((top1, top2)):
                pool.indirect_dma_start(
                    rows[:, t % NB, :], None, rows_gated,
                    bass.IndirectOffsetOnAxis(ap=gated_i[:, t, k:k + 1], axis=0)).then_inc(c_loaded[t % NB], 16)

    @block.vector
    def _(dve):
        steps = 0

        def step(ins):
            nonlocal steps
            steps += 1
            ins.then_inc(S["dve_step"], 1)
            dve.wait_ge(S["dve_step"], steps)

        for half in (gray_hi, gray_lo):
            for col in (0, GW - 1):
                dve.memset(half[:, :, col:col + 1].bitcast(F32), 0.0)
        dve.memset(ones[:, :], 1.0)
        dve.memset(one8[:, :], 1.0)
        dve.memset(earlier[:, :, :], 0.0)
        step(dve.memset(halo_w.bitcast(F32), 0.0))

        dve.wait_ge(S["taps_in"], 16)
        step(dve.tensor_scalar(taps[:, :], taps[:, :], 0.5, None, ALU.mult))
        dve.wait_ge(S["consts_in"], 32)
        for dy, diagonal in ((0, early[:, 0:P]), (1, ident), (2, early[:, P:2 * P])):
            for k in range(2):
                for dx in range(3):
                    w = taps[:, 9 * k + 3 * dy + dx:9 * k + 3 * dy + dx + 1]
                    b = band_raw[:, 3 * k + dx, :]
                    if dy == 0:
                        last = dve.tensor_scalar(b, diagonal, w, None, ALU.mult)
                    else:
                        last = dve.scalar_tensor_tensor(b, diagonal, w, b, ALU.mult, ALU.add)
                    if dy == 2:
                        last.then_inc(S["bands_made"], 1)
            if dy < 2:
                step(last)
        dve.wait_ge(S["halo_taps_in"], 48)
        step(dve.tensor_scalar(htap[:, 1], htap[:, 0], 0.5, None, ALU.mult))
        step(dve.tensor_copy(htap_r[:, :], htap[:, 1]))
        step(dve.tensor_tensor(htap[:, 2], htap[:, 1], htap_r[:, :].bitcast(F32), ALU.subtract))
        step(dve.tensor_scalar(htap[:, 2], htap[:, 2], cst[0:9, C_SEL + 1:C_SEL + 2], None, ALU.mult))
        step(dve.scalar_tensor_tensor(htap[:, 3], htap_r[:, :].bitcast(F32), cst[0:9, C_SEL:C_SEL + 1], htap[:, 2],
                                      ALU.mult, ALU.add))
        for t, dy, col in ((0, 2, P - 1), (1, 0, 0)):
            dve.tensor_copy(halo_w[:, t, :, col], htap[:, 3, dy:6:3]).then_inc(S["halo_made"], 1)
        dve.tensor_copy(before[:, :], early[:, 2 * P:3 * P]).then_inc(S["before_made"], 1)

        def gray_rest(u):
            dve.wait_ge(x_in[u % 2], 16 * (u // 2 + 1))
            dve.wait_ge(S["gray_first"], u + 1)
            step(dve.scalar_tensor_tensor(gray, xs_img[:, u % 2, 1], GRAY[1], gray, ALU.mult, ALU.add))
            dve.scalar_tensor_tensor(gray, xs_img[:, u % 2, 2], GRAY[2], gray, ALU.mult, ALU.add)\
               .then_inc(S["gray_made"], 1)

        def gray_low(u):
            dve.wait_ge(S["gray_hi_made"], u + 1)
            dve.tensor_tensor(gray_lo[:, :, 1:1 + SIZE], gray, gray_hi[:, :, 1:1 + SIZE].bitcast(F32), ALU.subtract)\
               .then_inc(S["gray_split"], 1)

        gray_rest(0)
        dve.wait_ge(S["band_hi"], 1)
        dve.tensor_tensor(band[:, 1], band_raw, band[:, 0].bitcast(F32), ALU.subtract).then_inc(S["bands_split"], 1)
        gray_low(0)
        for w in range(3):
            dve.wait_ge(S["qkv_hi"], w + 1)
            dve.tensor_tensor(wqkv[w][:, 1], stage_qkv[:, w], wqkv[w][:, 0].bitcast(F32), ALU.subtract)\
               .then_inc(S["qkv_split"], 1)
        dve.wait_ge(S["small_in"], 80)

        def moments(norm, rows, made):
            for t in range(2):
                last = dve.bn_stats(stats[:, norm, t, :], rows[:, t, :])
            step(last)
            for t in range(2):
                last = dve.bn_aggr(mv[:, norm, t, :], stats[:, norm, t, :])
            last.then_inc(S[made], 1)

        def normalise(norm, dst, rows, u, have, made):
            dve.wait_ge(S[have], u + 1)
            for t in range(2):
                last = dve.tensor_scalar(dst[:, t, :], rows[:, t, :], mv[:, norm, t, 0:1], rstd[:, norm, t:t + 1],
                                         ALU.subtract, ALU.mult)
            last.then_inc(S[made], 1)

        def edges(u, t):
            dve.wait_ge(S["edge_made"], 2 * u + t + 1)
            if u >= 4:
                dve.wait_ge(res_stored[u % 4], 16 * (u // 4))
            dve.tensor_tensor(h_all[:, u % 4, t], edge[:, t, 0], edge[:, t, 1], ALU.add).then_inc(S["h_made"], 1)

        def topk_logits(u):
            dve.wait_ge(S["gate_done"], u + 1)
            ps = ps_gate[:, 0:2 * EXPERTS].rearrange("p (t e) -> p t e", t=2)
            step(dve.tensor_reduce(gmax[:, :], ps, AX.X, ALU.max))
            dve.tensor_tensor(logit[:, :, :], ps, gmax[:, :].unsqueeze(2).broadcast_to([P, 2, EXPERTS]), ALU.subtract)\
               .then_inc(S["logit_made"], 1)

        def topk_hits(u):
            dve.wait_ge(S["gexp_made"], u + 1)
            step(dve.tensor_reduce(gsum[:, :], gexp[:, :, :], AX.X, ALU.add))
            step(dve.reciprocal(grec[:, :], gsum[:, :]))
            step(dve.tensor_tensor(gprob[:, :, :], gexp[:, :, :], grec[:, :].unsqueeze(2).broadcast_to([P, 2, EXPERTS]), ALU.mult))
            for t in range(2):
                last = dve.max(best[:, t, :], gprob[:, t, :])
            step(last)
            for t in range(2):
                last = dve.max_index(best_at[:, t, :], best[:, t, :], gprob[:, t, :])
            step(last)
            step(dve.tensor_copy(best_f[:, :, :], best_at[:, :, 0:TOP]))
            chosen = chosen_all[:, 2 * u:2 * u + 2]
            iota = cst[:, C_IOTA:C_IOTA + EXPERTS].unsqueeze(1).unsqueeze(1).broadcast_to([P, 2, TOP, EXPERTS])
            step(dve.tensor_tensor(chosen[:, :, :, :], iota, best_f[:, :, :].unsqueeze(3).broadcast_to([P, 2, TOP, EXPERTS]), ALU.is_equal))
            if u >= 1:
                dve.wait_ge(S["rank_done"], u)
                dve.tensor_copy(earlier[:, 0, :], earlier[:, 2, :])
            step(dve.tensor_tensor(hit[:, :, :], chosen[:, :, 0, :], chosen[:, :, 1, :], ALU.add))
            step(dve.tensor_tensor(earlier[:, 1, :], earlier[:, 0, :], hit[:, 0, :], ALU.add))
            dve.tensor_tensor(earlier[:, 2, :], earlier[:, 1, :], hit[:, 1, :], ALU.add).then_inc(S["hits_made"], 1)
            step(dve.tensor_tensor(den[:, :], best[:, :, 0], best[:, :, 1], ALU.add))
            step(dve.tensor_scalar(den[:, :], den[:, :], EPS_TOP, None, ALU.add))
            step(dve.reciprocal(den[:, :], den[:, :]))
            w = weight[:, 2 * TOP * u:2 * TOP * (u + 1)].rearrange("p (t k) -> p t k", t=2)
            step(dve.tensor_tensor(w, best[:, :, 0:TOP], den[:, :].unsqueeze(2).broadcast_to([P, 2, TOP]), ALU.mult))
            step(dve.tensor_tensor(wsum[:, :], w[:, :, 0], w[:, :, 1], ALU.add))

        def topk_places(u):
            dve.wait_ge(S["rank_done"], u + 1)
            base = cst[:, C_BASE:C_BASE + EXPERTS].unsqueeze(1).broadcast_to([P, 2, EXPERTS])
            dve.tensor_tensor(place[:, :, :], ps_rank[:, 0:2 * EXPERTS].rearrange("p (t e) -> p t e", t=2), base, ALU.add)\
               .then_inc(S["rank_read"], 1)
            dve.wait_ge(S["rank_read"], u + 1)
            step(dve.tensor_tensor(placed[:, :, :, :], chosen_all[:, 2 * u:2 * u + 2],
                                   place[:, :, :].unsqueeze(2).broadcast_to([P, 2, TOP, EXPERTS]), ALU.mult))
            step(dve.tensor_reduce(place_f[:, :, :], placed[:, :, :, :], AX.X, ALU.add))
            dve.tensor_copy(place_i[:, 2 * u:2 * u + 2, :], place_f[:, :, :])\
               .then_inc(S["places_made"], 1)

        for s in range(STEPS):
            if live(s - 1):
                u = s - 1
                dve.wait_ge(S["xT_hi_made"], u + 1)
                dve.tensor_tensor(xT_f[:, 1], ps_xT[:, :].rearrange("p (k n) -> p k n", k=KD),
                                  xT_f[:, 0].bitcast(F32), ALU.subtract).then_inc(S["xT_split"], 1)
            if live(s + 1):
                gray_rest(s + 1)
            if live(s - 3):
                topk_logits(s - 3)
            if live(s):
                edges(s, 0)
            if live(s - 3):
                topk_hits(s - 3)
            if live(s):
                edges(s, 1)
                dve.wait_ge(S["h_made"], 2 * (s + 1))
                moments(0, h_all[:, s % 4], "mv1_made")
            if live(s - 2):
                u = s - 2
                dve.wait_ge(S["probs_made"], 2 * (u + 1))
                dve.reciprocal(srec[:, :], ssum[:, :]).then_inc(S["srec_made"], 1)
                dve.wait_ge(S["srec_made"], u + 1)
                dve.wait_ge(S["pv_done"], u + 1)
                for t in range(2):
                    dve.scalar_tensor_tensor(h_all[:, u % 4, t], ps_pv[:, t * D:(t + 1) * D], srec[:, t:t + 1],
                                             h_all[:, u % 4, t], ALU.mult, ALU.add).then_inc(S["h2_made"], 1)
                dve.wait_ge(S["h2_made"], 2 * (u + 1))
                moments(1, h_all[:, u % 4], "mv2_made")
            if live(s):
                if s >= 1:
                    dve.wait_ge(S["xT_done"], s)
                normalise(0, xn1, h_all[:, s % 4], s, "rstd1_made", "xn1_made")
            if live(s - 1):
                u = s - 1
                dve.wait_ge(S["v_done"], u + 1)
                if u >= 1:
                    dve.wait_ge(S["pv_done"], u)
                dve.tensor_tensor(v_sb, ps_v[:, :].rearrange("p (t e) -> p t e", t=2),
                                  bv_all[:, :].unsqueeze(1).broadcast_to([P, 2, D]), ALU.add).then_inc(S["v_made"], 1)
            if live(s - 2):
                u = s - 2
                if u >= 2:
                    dve.wait_ge(scattered[u % 2], 64 * (u // 2))
                normalise(1, xn2[:, u % 2], h_all[:, u % 4], u, "rstd2_made", "xn2_made")
            if live(s + 1):
                gray_low(s + 1)
            if live(s - 1):
                u = s - 1
                dve.wait_ge(S["s_done"], u + 1)
                if u >= 1:
                    dve.wait_ge(S["probs_made"], 2 * u)
                for t in range(2):
                    last = dve.tensor_tensor_reduce(masked[:, t], ps_s[:, t * P:(t + 1) * P], cst[:, C_MASK:C_MASK + P],
                                                    1.0, NEVER, ALU.add, ALU.max, smax[:, t:t + 1])
                step(last)
                dve.tensor_scalar(nsmax[:, :], smax[:, :], -1.0, None, ALU.mult).then_inc(S["masked_made"], 1)
            if live(s - 3):
                u = s - 3
                topk_places(u)
                for t in range(2):
                    dve.scalar_tensor_tensor(h_all[:, u % 4, t], bo_all[:, :], wsum[:, t:t + 1], h_all[:, u % 4, t],
                                             ALU.mult, ALU.add).then_inc(S["res_made"], 1)

        dve.wait_ge(S["count_done"], 1)
        rows_of_expert = ps_rank[:, 0:EXPERTS]
        dve.tensor_tensor(pad_f[:, :], rows_of_expert[0:1], cst[0:1, C_BASE:C_BASE + EXPERTS], ALU.add)
        step(dve.tensor_scalar(tiles_i[:, 0], rows_of_expert, float(P - 1), None, ALU.add))
        dve.tensor_copy(pad_i[:, :], pad_f[:, :])
        step(dve.tensor_scalar(tiles_i[:, 1], tiles_i[:, 0], P.bit_length() - 1, None, ALU.logical_shift_right))
        step(dve.tensor_copy(tiles_f[:, :], tiles_i[:, 1]))
        step(dve.tensor_tensor_scan(ends[:, :], one8[:, :], tiles_f[:, :], 0.0, ALU.mult, ALU.add))
        whole = [1, MAX_TILES, EXPERTS]
        tile_no = cst[0:1, C_TILE:C_TILE + MAX_TILES]
        step(dve.tensor_tensor(passed, tile_no.unsqueeze(2).broadcast_to(whole),
                               ends[0:1, :].unsqueeze(1).broadcast_to(whole), ALU.is_ge))
        step(dve.tensor_tensor(passed_n, passed, tiles_f[0:1, :].unsqueeze(1).broadcast_to(whole), ALU.mult))
        step(dve.tensor_reduce(expert_of, passed, AX.X, ALU.add))
        step(dve.tensor_reduce(start_of, passed_n, AX.X, ALU.add))
        step(dve.tensor_tensor(tiles_in, tile_no, start_of, ALU.subtract))
        step(dve.tensor_scalar(rows_before, tiles_in, float(P), None, ALU.mult))
        dve.scalar_tensor_tensor(tab_row[:, :], expert_of, float(REGION), rows_before, ALU.mult, ALU.add)
        dve.tensor_scalar(tab_w[:, :], expert_of, float(EXPERTS - 1), float(WE), ALU.min, ALU.mult)
        dve.tensor_scalar(tab_b[:, :], expert_of, float(EXPERTS - 1), float(2 * H), ALU.min, ALU.mult)\
           .then_inc(S["tables_made"], 1)
        dve.wait_ge(S["tables_made"], 1)

        step(dve.tensor_tensor(shift[:, :], ends[:, :], tiles_f[:, :], ALU.subtract))
        step(dve.scalar_tensor_tensor(shift[:, :], shift[:, :], float(P), cst[:, C_BASE:C_BASE + EXPERTS], ALU.mult, ALU.subtract))
        each = [P, TILES * TOP, EXPERTS]
        step(dve.tensor_tensor(shifts, chosen_all[:, :, :, :].rearrange("p t k e -> p (t k) e"),
                               shift[:, :].unsqueeze(1).broadcast_to(each), ALU.mult))
        step(dve.tensor_reduce(shift_of, shifts, AX.X, ALU.add))
        dve.tensor_tensor(gated_i[:, :, :].rearrange("p t k -> p (t k)"), place_i[:, :, :].rearrange("p t k -> p (t k)"),
                          shift_of, ALU.add).then_inc(S["gated_places_made"], 1)

        dve.wait_ge(S["wo_hi"], 1)
        dve.tensor_tensor(wo_h[:, 1], wo_raw, wo_h[:, 0].bitcast(F32), ALU.subtract).then_inc(S["wo_split"], 1)

        dve.wait_ge(S["b1_in"], 16)

        def e_low(j, p):
            dve.wait_ge(S["e_hi"], j + 1)
            dve.tensor_tensor(xT_e[:, p, 1], ps_et[p][:, 0:KD * P].rearrange("p (k n) -> p k n", k=KD),
                              xT_e[:, p, 0].bitcast(F32), ALU.subtract).then_inc(S["e_split"], 1)

        def e_gate(j, p, stored, first=False):
            off = dve.value_load(tab_b[0:1, ds(j, 1)], min_val=0, max_val=(EXPERTS - 1) * 2 * H)
            dve.wait_ge(S["e_b_done"], j + 1)
            if not first:
                dve.wait_ge(S["e_sig_made"], j - 1)
            dve.tensor_tensor(e_b[:, p], ps_b[p][:, :], b1_all[:, ds(off + H, H)], ALU.add).then_inc(S["e_b_made"], 1)
            dve.wait_ge(S["e_a_done"], j + 1)
            dve.tensor_tensor(e_a[:, p], ps_a[p][:, :], b1_all[:, ds(off, H)], ALU.add).then_inc(S["e_a_read"], 1)
            dve.wait_ge(S["e_a_read"], j + 1)
            dve.wait_ge(S["e_sig_made"], j + 1)
            if not first:
                dve.wait_ge(e_stored[p], stored)
            dve.tensor_tensor(e_out[:, p], e_a[:, p], e_sig[:, p], ALU.mult).then_inc(S["e_out_made"], 1)

        e_low(0, 0)
        e_low(1, 1)
        e_gate(0, 0, 0, True)
        e_low(2, 0)
        e_gate(1, 1, 0, True)
        with dve.Fori(1, MAX_TILES // 2) as i:
            e_low(2 * i + 1, 1)
            e_gate(2 * i, 0, 16 * i)
            e_low(2 * i + 2, 0)
            e_gate(2 * i + 1, 1, 16 * i)
        e_gate(MAX_TILES - 1, 0, 16 * (MAX_TILES // 2))

        def c_sum(t, b, loaded):
            dve.wait_ge(c_loaded[b], loaded)
            dve.wait_ge(S["c_first"], t + 1)
            dve.scalar_tensor_tensor(top2[:, b], top2[:, b], weight_of(t, 1), top1[:, b], ALU.mult, ALU.add)\
               .then_inc(S["c_sum"], 1)

        def c_low(t, p):
            dve.wait_ge(S["c_hi"], t + 1)
            dve.tensor_tensor(sumT[p][:, 1], ps_ct[p][:, :].rearrange("p (k n) -> p k n", k=KH),
                              sumT[p][:, 0].bitcast(F32), ALU.subtract).then_inc(S["c_split"], 1)

        def c_result(t, b, turn, first=False):
            dve.wait_ge(S["c_y"], t + 1)
            dve.wait_ge(c_res[b], turn)
            if not first:
                dve.wait_ge(c_stored[b], turn - 16)
            dve.tensor_tensor(result[:, b], ps_y[b % 2][:, 0:D], res_in[:, b], ALU.add).then_inc(S["c_out"], 1)

        c_sum(0, 0, 32)
        for t in range(NB + 1):
            c_sum(t + 1, (t + 1) % NB, 32 * ((t + 1) // NB + 1))
            c_low(t, t % 2)
            if t >= 1:
                c_result(t - 1, t - 1, 16, True)
        with dve.Fori(1, TILES // NB - 1) as i:
            for b in range(NB):
                t = NB * i + b + 1
                c_sum(t + 1, (b + 2) % NB, 32 * i + 32 * ((b + 2) // NB + 1))
                c_low(t, (b + 1) % 2)
                c_result(t - 1, b, 16 * i + 16)
        for t in range(TILES - NB + 1, TILES):
            if t + 1 < TILES:
                c_sum(t + 1, (t + 1) % NB, 32 * ((t + 1) // NB + 1))
            c_low(t, t % 2)
            c_result(t - 1, (t - 1) % NB, 16 * ((t - 1) // NB + 1))
        c_result(TILES - 1, NB - 1, 16 * (TILES // NB))

    @block.tensor
    def _(pe):
        def conv(u, t):
            pe.wait_ge(S["gray_split"], u + 1)
            if u >= 1:
                pe.wait_ge(S["edge_made"], 2 * u + t - 1)
            for k in range(2):
                dst = ps_conv[t][:, k * SIZE:(k + 1) * SIZE]
                for n, (g, f, dx) in enumerate(three(range(3))):
                    pe.matmul(dst, band[:, g, 3 * k + dx, :], (gray_hi, gray_lo)[f][:, t, dx:dx + SIZE],
                              start=(n == 0), stop=False)
                if t == 0 and k == 0:
                    pe.wait_ge(S["halo_moved"], 16 * 6 * (u + 1))
                last = pe.matmul(dst, halo_w[:, t, k, :], halo_in[:, t, :], start=False, stop=True)
            last.then_inc(S["conv_done"], 1)

        def project(u, w, ps, done):
            for m in range(KD):
                for n, (g, f, k) in enumerate(three(range(KD))):
                    last = pe.matmul(ps[:, m * SIZE:(m + 1) * SIZE], wqkv[w][:, g, k, m * P:(m + 1) * P],
                                     xT_f[:, f, k, :], start=(n == 0), stop=(n == 3 * KD - 1))
            last.then_inc(S[done], 1)

        pe.wait_ge(S["consts_in"], 32)
        pe.wait_ge(S["bands_split"], 1)
        pe.wait_ge(S["halo_made"], 2)
        for s in range(STEPS):
            if live(s - 1):
                u = s - 1
                pe.wait_ge(S["xn1_made"], u + 1)
                if u >= 1:
                    pe.wait_ge(S["xT_split"], u)
                for k in range(KD):
                    for t in range(2):
                        last = pe.transpose(ps_xT[:, k * SIZE + t * P:k * SIZE + (t + 1) * P],
                                            xn1[:, t, k * P:(k + 1) * P], ident)
                last.then_inc(S["xT_done"], 1)
            if live(s - 2):
                u = s - 2
                pe.wait_ge(S["probs_made"], 2 * (u + 1))
                if u >= 1:
                    pe.wait_ge(S["h2_made"], 2 * u)
                for t in range(2):
                    last = pe.transpose(ps_pT[:, t * P:(t + 1) * P], probs[:, t], ident)
                last.then_inc(S["pT_done"], 1)
            if live(s - 3):
                u = s - 3
                pe.wait_ge(S["xn2T_made"], u + 1)
                pe.wait_ge(S["masked_made"], min(u + 2, IMAGES))
                for t in range(2):
                    for k in range(KD):
                        last = pe.matmul(ps_gate[:, t * EXPERTS:(t + 1) * EXPERTS], xn2T[:, k, t * P:(t + 1) * P],
                                         wg_sb[:, k, :], start=(k == 0), stop=(k == KD - 1))
                last.then_inc(S["gate_done"], 1)
            if live(s):
                conv(s, 0)
            if live(s - 1):
                u = s - 1
                pe.wait_ge(S["xT_split"], u + 1)
                pe.wait_ge(S["qkv_split"], 3)
                if u >= 3:
                    pe.wait_ge(S["rank_read"], u - 2)
                project(u, 0, ps_q, "q_done")
                if u >= 2:
                    pe.wait_ge(S["xn2T_made"], u - 1)
                project(u, 1, ps_k, "k_done")
            if live(s):
                conv(s, 1)
            if live(s - 2):
                u = s - 2
                pe.wait_ge(S["pT_made"], u + 1)
                pe.wait_ge(S["v_made"], u + 1)
                for t in range(2):
                    last = pe.matmul(ps_pv[:, t * D:(t + 1) * D], probsT[:, t], v_sb[:, t], start=True, stop=True)
                last.then_inc(S["pv_done"], 1)
            if live(s - 1):
                u = s - 1
                if u >= 1:
                    pe.wait_ge(S["v_made"], u)
                for t in range(2):
                    for n, (g, f, k) in enumerate(three(range(KD))):
                        last = pe.matmul(ps_v[:, t * D:(t + 1) * D], xT_f[:, g, k, t * P:(t + 1) * P],
                                         wv[:, f, k, :], start=(n == 0), stop=(n == 3 * KD - 1))
                last.then_inc(S["v_done"], 1)
                pe.wait_ge(S["q_made"], KD * (u + 1))
                pe.wait_ge(S["k_made"], KD * (u + 1))
                if u >= 2:
                    pe.wait_ge(S["logit_made"], u - 1)
                for t in range(2):
                    for m in range(KD):
                        last = pe.matmul(ps_s[:, t * P:(t + 1) * P], qT[:, m, t * P:(t + 1) * P],
                                         kT[:, m, t * P:(t + 1) * P], start=(m == 0), stop=(m == KD - 1))
                last.then_inc(S["s_done"], 1)
            if live(s - 3):
                u = s - 3
                pe.wait_ge(S["hits_made"], u + 1)
                pe.wait_ge(S["before_made"], 1)
                pe.matmul(ps_rank[:, 0:2 * EXPERTS], before[:, :], hit[:, :, :].rearrange("p t e -> p (t e)"),
                          start=True, stop=False)
                pe.matmul(ps_rank[:, 0:2 * EXPERTS], ones[:, :], earlier[:, 0:2, :].rearrange("p t e -> p (t e)"),
                          start=False, stop=True).then_inc(S["rank_done"], 1)
            if live(s - 2):
                u = s - 2
                pe.wait_ge(S["xn2_made"], u + 1)
                if live(s - 1):
                    pe.wait_ge(S["k_made"], KD * s)
                for k in range(KD):
                    for t in range(2):
                        last = pe.transpose(ps_xn2T[:, k * SIZE + t * P:k * SIZE + (t + 1) * P],
                                            xn2[:, u % 2, t, k * P:(k + 1) * P], ident)
                last.then_inc(S["xn2T_done"], 1)
        pe.wait_ge(S["rank_read"], IMAGES)
        pe.matmul(ps_rank[:, 0:EXPERTS], ones[:, :], earlier[:, 2, :], start=True, stop=True).then_inc(S["count_done"], 1)

        def e_transpose(j, p, loaded, first=False):
            pe.wait_ge(e_loaded[p], loaded)
            if not first:
                pe.wait_ge(S["e_split"], j - 1)
            for k in range(KD):
                last = pe.transpose(ps_et[p][:, k * P:(k + 1) * P], e_in[:, p, k * P:(k + 1) * P], ident)
            last.then_inc(S["e_T"], 1)

        def weights_of(j):
            return pe.value_load(tab_w[0:1, ds(j, 1)], min_val=0, max_val=(EXPERTS - 1) * WE)

        def e_product(j, p, off, first=False):
            pe.wait_ge(S["e_split"], j + 1)
            for ps, col, done, read in ((ps_b[p], H, "e_b_done", "e_b_made"), (ps_a[p], 0, "e_a_done", "e_a_read")):
                if not first:
                    pe.wait_ge(S[read], j - 1)
                for n, (g, f, k) in enumerate(three(range(KD))):
                    last = pe.matmul(ps[:, :], xT_e[:, p, g, k, :], (w1_hi, w1_lo)[f][:, ds(off + k * 2 * H + col, H)],
                                     start=(n == 0), stop=(n == 3 * KD - 1))
                last.then_inc(S[done], 1)

        pe.wait_ge(S["tables_made"], 1)
        pe.wait_ge(S["w1_lo_made"], CHUNKS)
        e_transpose(0, 0, 16, True)
        e_transpose(1, 1, 16, True)
        e_product(0, 0, weights_of(0), True)
        e_transpose(2, 0, 32)
        e_product(1, 1, weights_of(1), True)
        with pe.Fori(1, MAX_TILES // 2) as i:
            off = [weights_of(2 * i + p) for p in range(2)]
            e_transpose(2 * i + 1, 1, 16 * i + 16)
            e_product(2 * i, 0, off[0])
            e_transpose(2 * i + 2, 0, 16 * i + 32)
            e_product(2 * i + 1, 1, off[1])
        e_product(MAX_TILES - 1, 0, weights_of(MAX_TILES - 1))

        def c_transpose(t, b, p, first=False):
            pe.wait_ge(S["c_sum"], t + 1)
            if not first:
                pe.wait_ge(S["c_split"], t - 1)
            for k in range(KH):
                last = pe.transpose(ps_ct[p][:, k * P:(k + 1) * P], top2[:, b, k * P:(k + 1) * P], ident)
            last.then_inc(S["c_T"], 1)

        def c_product(t, p, first=False):
            pe.wait_ge(S["c_split"], t + 1)
            if not first:
                pe.wait_ge(S["c_out"], t - 1)
            for n, (g, f, k) in enumerate(three(range(KH))):
                last = pe.matmul(ps_y[p][:, 0:D], sumT[p][:, g, k, :], wo_h[:, f, k, :],
                                 start=(n == 0), stop=(n == 3 * KH - 1))
            last.then_inc(S["c_y"], 1)

        pe.wait_ge(S["wo_split"], 1)
        c_transpose(0, 0, 0, True)
        for t in range(NB):
            c_transpose(t + 1, (t + 1) % NB, (t + 1) % 2, t + 1 < 2)
            c_product(t, t % 2, t < 2)
        with pe.Fori(1, TILES // NB - 1) as i:
            for b in range(NB):
                t = NB * i + b
                c_transpose(t + 1, (b + 1) % NB, (b + 1) % 2)
                c_product(t, b % 2)
        for t in range(TILES - NB, TILES):
            if t + 1 < TILES:
                c_transpose(t + 1, (t + 1) % NB, (t + 1) % 2)
            c_product(t, t % 2)


def kernel(x, L0_tok_scharr, L0_attn_Wq, L0_attn_bq, L0_attn_Wk, L0_attn_bk, L0_attn_Wv, L0_attn_bv,
           L0_ffn_Wg, L0_ffn_W1, L0_ffn_b1, L0_ffn_Wo, L0_ffn_bo):
    import numpy as np
    from concourse import bacc, mybir as mb
    from concourse.bass_utils import run_bass_kernel_spmd

    def laid(a, *axes):
        a = np.asarray(a)
        return np.ascontiguousarray(a.transpose(*axes) if axes else a)

    arrays = {
        "x": laid(x), "scharr": laid(L0_tok_scharr),
        "wqT": laid(L0_attn_Wq, 1, 0), "wkT": laid(L0_attn_Wk, 1, 0), "wvT": laid(L0_attn_Wv, 1, 0),
        "bq": laid(L0_attn_bq), "bk": laid(L0_attn_bk), "bv": laid(L0_attn_bv),
        "wgT": laid(L0_ffn_Wg, 1, 0), "w1T": laid(L0_ffn_W1, 2, 0, 1), "b1": laid(L0_ffn_b1),
        "woT": laid(L0_ffn_Wo, 1, 0), "bo": laid(L0_ffn_bo), "consts": shape_constants(), "zeros": np.zeros((P, D), np.float32),
    }
    nc = bacc.Bacc("TRN2", target_bir_lowering=False, num_devices=1)
    aps = {n: nc.dram_tensor(n, a.shape, mb.dt.from_np(a.dtype), kind="ExternalInput").ap() for n, a in arrays.items()}
    out = nc.dram_tensor("out", (TILES * P, D), mb.dt.float32, kind="ExternalOutput").ap()
    build(nc, out=out, **aps)
    r = run_bass_kernel_spmd(nc, [arrays], core_ids=[0])
    return r.results[0]["out"].reshape(IMAGES, SIZE, D)
```

```python
from contextlib import ExitStack

import concourse.bass as bass
from concourse import mybir

F32 = mybir.dt.float32
F32R = mybir.dt.float32r
BF16 = mybir.dt.bfloat16
I32 = mybir.dt.int32
U32 = mybir.dt.uint32
ALU = mybir.AluOpType
ACT = mybir.ActivationFunctionType
AX = mybir.AxisListType

P = 128
IMAGES, CHANNELS, SIZE = 8, 3, 256
D = 256
KD = D // P
TILES_IN_IMAGE = SIZE // P
TILES = IMAGES * TILES_IN_IMAGE
HEAD = SIZE // 16
EXPERTS, TOP = 8, 2
H = 512
KH = H // P
REGION = IMAGES * SIZE + P
MAX_TILES = (IMAGES * SIZE * TOP + EXPERTS * (P - 1)) // P
LEAST_TILES = IMAGES * SIZE * TOP // P
ROWS = (EXPERTS + 1) * REGION
EPS_LN, EPS_TOP = 1e-5, 1e-9
GRAY = (0.2989, 0.587, 0.114)
NEVER = -3.0e38

C_ID, C_MASK, C_IOTA, C_BASE, C_SEL, C_TILE = 0, 128, 256, 264, 272, 274
C_UP = C_TILE + MAX_TILES
C_DOWN, C_BEFORE = C_UP + P, C_UP + 2 * P
C_ALL = C_UP + 3 * P


def shape_constants():
    import numpy as np
    c = np.zeros((P, C_ALL), np.float32)
    r = np.arange(P)
    c[:, C_ID:C_ID + P] = np.eye(P)
    c[:, C_UP:C_UP + P] = r[:, None] == r[None, :] - 1
    c[:, C_DOWN:C_DOWN + P] = r[:, None] == r[None, :] + 1
    c[:, C_MASK:C_MASK + P] = np.where(r[:, None] // HEAD == r[None, :] // HEAD, 0.0, NEVER)
    c[:, C_BEFORE:C_BEFORE + P] = r[:, None] < r[None, :]
    c[:, C_IOTA:C_IOTA + EXPERTS] = np.arange(EXPERTS)
    c[:, C_BASE:C_BASE + EXPERTS] = np.arange(EXPERTS) * REGION
    c[:9, C_SEL] = [1, 1, 1, 0, 0, 0, 1, 1, 1]
    c[:9, C_SEL + 1] = [0, 0, 0, 1, 1, 1, 0, 0, 0]
    c[:, C_TILE:C_TILE + MAX_TILES] = np.arange(MAX_TILES)
    return c


def build(nc, x, scharr, wqT, wkT, wvT, bq, bk, bv, wgT, w1T, b1, woT, bo, consts, zeros, out):
    ctx = ExitStack()
    with ctx:
        _build(nc, ctx, x, scharr, wqT, wkT, wvT, bq, bk, bv, wgT, w1T, b1, woT, bo, consts, zeros, out)


def _build(nc, ctx, x, scharr, wqT, wkT, wvT, bq, bk, bv, wgT, w1T, b1, woT, bo, consts, zeros, out):
    ds = bass.ds

    def sb(name, shape, dt=F32):
        return ctx.enter_context(nc.sbuf_tensor(name, shape, dt))

    def sem(name):
        return ctx.enter_context(nc.semaphore(name))

    rows_in = nc.dram_tensor("rows_in", (ROWS, D), F32, kind="Internal").ap()
    rows_gated = nc.dram_tensor("rows_gated", (MAX_TILES * P, H), F32, kind="Internal").ap()
    resid = nc.dram_tensor("resid", (TILES * P, D), F32, kind="Internal").ap()

    WE = KD * 2 * H
    w1_hi = sb("w1_hi", [P, EXPERTS * WE], F32R)
    w1_lo = sb("w1_lo", [P, EXPERTS * WE], F32R)
    LAST = (EXPERTS - 1) * WE
    GW = SIZE + 2
    gray_hi = w1_lo[:, LAST:LAST + 2 * GW].rearrange("p (t c) -> p t c", t=2)
    gray_lo = w1_lo[:, LAST + 2 * GW:LAST + 4 * GW].rearrange("p (t c) -> p t c", t=2)
    halo_in = w1_lo[0:9, LAST + 4 * GW:LAST + 4 * GW + 2 * SIZE].rearrange("p (t c) -> p t c", t=2)
    halo_w = w1_hi[0:9, LAST:LAST + 4 * P].rearrange("p (t k o) -> p t k o", t=2, k=2)
    front_w = sb("front_w", [P, 6 * 2 * P + 2 * 2 * KD * D], F32R)
    band = front_w[:, 0:12 * P].rearrange("p (g q o) -> p g q o", g=2, q=6)
    wqk = front_w[:, 12 * P:].rearrange("p (w g k e) -> p w g k e", w=2, g=2, k=KD)
    wv = w1_hi[:, LAST + 4 * P:LAST + 4 * P + 2 * KD * D].rearrange("p (g k e) -> p g k e", g=2, k=KD)
    wqkv = [wqk[:, 0], wqk[:, 1], wv]
    wo_h = front_w[:, 0:2 * KH * D].rearrange("p (g k e) -> p g k e", g=2, k=KH)
    NS = 3
    shared = sb("shared", [P, EXPERTS * 2 * H])
    xs_img = shared[:, 0:3072].rearrange("p (b c t w) -> p b c t w", b=2, c=3, t=2)
    gray = shared[:, 3072:3584].rearrange("p (t w) -> p t w", t=2)
    xn1 = shared[:, 3584:4096].rearrange("p (t w) -> p t w", t=2)
    stage = shared[:, 4096:7168].rearrange("p (b w) -> p b w", b=NS)
    stage_qkv = shared[:, 6656:8192].rearrange("p (w k e) -> p w k e", w=3, k=KD)
    edge = shared[:, 7168:8192].rearrange("p (t k w) -> p t k w", t=2, k=2)
    b1_all = shared[:, :]
    NB = 4
    top1 = shared[:, 0:NB * H].rearrange("p (b h) -> p b h", b=NB)
    top2 = shared[:, NB * H:2 * NB * H].rearrange("p (b h) -> p b h", b=NB)
    res_in = shared[:, 2 * NB * H:2 * NB * H + NB * D].rearrange("p (b d) -> p b d", b=NB)
    result = shared[:, 2 * NB * H + NB * D:2 * NB * H + 2 * NB * D].rearrange("p (b d) -> p b d", b=NB)
    work = sb("work", [P, 5888])
    h_all = work[:, 0:2048].rearrange("p (b t w) -> p b t w", b=4, t=2)
    xn2 = work[:, 2048:3072].rearrange("p (b t w) -> p b t w", b=2, t=2)
    xn2T = work[:, 3072:3584].rearrange("p (k n) -> p k n", k=KD)
    qT = work[:, 3584:4096].rearrange("p (k n) -> p k n", k=KD)
    kT = work[:, 4096:4608].rearrange("p (k n) -> p k n", k=KD)
    v_sb = work[:, 4608:5120].rearrange("p (t w) -> p t w", t=2)
    masked = work[:, 5120:5376].rearrange("p (t w) -> p t w", t=2)
    probs = work[:, 5376:5632].rearrange("p (t w) -> p t w", t=2)
    probsT = work[:, 5632:5888].rearrange("p (t w) -> p t w", t=2)
    band_raw = work[:, 2048:2048 + 6 * P].rearrange("p (q o) -> p q o", q=6)
    early = work[:, 2816:2816 + 3 * P]
    wo_raw = work[:, 4608:4608 + KH * D].rearrange("p (k e) -> p k e", k=KH)
    e_in = work[:, 0:2 * D].rearrange("p (b d) -> p b d", b=2)
    e_b = work[:, 512:512 + 2 * H].rearrange("p (b h) -> p b h", b=2)
    e_sig = work[:, 1536:1536 + 2 * H].rearrange("p (b h) -> p b h", b=2)
    e_a = work[:, 2560:2560 + 2 * H].rearrange("p (b h) -> p b h", b=2)
    e_out = work[:, 3584:3584 + 2 * H].rearrange("p (b h) -> p b h", b=2)
    xT = sb("xT", [P, 2 * KD * SIZE], F32R)
    xT_f = xT[:, :].rearrange("p (g k n) -> p g k n", g=2, k=KD)
    xT_e = xT[:, :].rearrange("p (b g k n) -> p b g k n", b=2, g=2, k=KD)

    sumT = [a.rearrange("p (g k t) -> p g k t", g=2, k=KH) for a in (front_w[:, 2 * KH * D:2 * KH * D + 2 * H], xT[:, :])]
    cst = sb("cst", [P, C_UP])
    ident = cst[:, C_ID:C_ID + P]
    before = sb("before", [P, P], BF16)
    ones = sb("ones", [P, P], BF16)
    bv_all = sb("bv_all", [P, D])
    bo_all = sb("bo_all", [P, D])
    bqk = sb("bqk", [P, 2 * KD])
    wg_sb = sb("wg_sb", [P, KD, EXPERTS])
    taps = sb("taps", [P, 18])
    htap = sb("htap", [9, 4, 6])
    htap_r = sb("htap_r", [9, 6], F32R)
    stats = sb("stats", [P, 2, 2, 6])
    mv = sb("mv", [P, 2, 2, 2])
    vare = sb("vare", [P, 2, 2])
    rstd = sb("rstd", [P, 2, 2])
    neg_half = sb("neg_half", [P, 2])
    smax = sb("smax", [P, 2])
    nsmax = sb("nsmax", [P, 2])
    ssum = sb("ssum", [P, 2])
    srec = sb("srec", [P, 2])
    gmax = sb("gmax", [P, 2])
    logit = sb("logit", [P, 2, EXPERTS])
    gexp = sb("gexp", [P, 2, EXPERTS])
    gsum = sb("gsum", [P, 2])
    grec = sb("grec", [P, 2])
    gprob = sb("gprob", [P, 2, EXPERTS])
    best = sb("best", [P, 2, 8])
    best_at = sb("best_at", [P, 2, 8], U32)
    best_f = sb("best_f", [P, 2, TOP])
    chosen_all = sb("chosen_all", [P, TILES, TOP, EXPERTS], BF16)
    hit = sb("hit", [P, 2, EXPERTS], BF16)
    earlier = sb("earlier", [P, 3, EXPERTS], BF16)
    den = sb("den", [P, 2])
    weight = sb("weight", [P, TILES * TOP])
    wsum = sb("wsum", [P, 2])
    place = sb("place", [P, 2, EXPERTS])
    placed = sb("placed", [P, 2, TOP, EXPERTS])
    place_f = sb("place_f", [P, 2, TOP])
    place_i = sb("place_i", [P, TILES, TOP], I32)
    gated_i = sb("gated_i", [P, TILES, TOP], I32)
    tiles_i = sb("tiles_i", [P, 2, EXPERTS], I32)
    tiles_f = sb("tiles_f", [P, EXPERTS])
    one8 = sb("one8", [P, EXPERTS])
    ends = sb("ends", [P, EXPERTS])
    shift = sb("shift", [P, EXPERTS])
    shifts = work[:, 4352:4352 + TILES * TOP * EXPERTS].rearrange("p (n e) -> p n e", e=EXPERTS)
    shift_of = work[:, 4320:4352]
    passed, passed_n = (work[0:1, 3072 + n * 512:3072 + n * 512 + MAX_TILES * EXPERTS].rearrange("p (j e) -> p j e", e=EXPERTS)
                        for n in range(2))
    expert_of, start_of, tiles_in, rows_before = (work[0:1, 4096 + n * 48:4096 + n * 48 + MAX_TILES] for n in range(4))
    tab_row = sb("tab_row", [1, MAX_TILES], I32)
    tab_w = sb("tab_w", [1, MAX_TILES], I32)
    tab_b = sb("tab_b", [1, MAX_TILES], I32)
    pad_f = sb("pad_f", [1, EXPERTS])
    pad_i = sb("pad_i", [1, EXPERTS], I32)

    bank = [ctx.enter_context(nc.psum_tensor(f"bank{i}", [P, 512], F32)) for i in range(8)]
    ps_conv = bank[0:2]
    ps_xT, ps_q, ps_k, ps_v, ps_s, ps_pv = bank[2:8]
    ps_rank, ps_xn2T, ps_gate, ps_pT = ps_q, ps_k, ps_s, ps_pv
    ps_et = bank[0:2]
    ps_a, ps_b = bank[2:4], bank[4:6]
    ps_ct = bank[6:8]
    ps_y = bank[0:2]

    S = {n: sem(n) for n in (
        "consts_in taps_in halo_taps_in qkv_in small_in regions_zeroed pads_set bf_set "
        "before_made bands_made bands_split halo_made qkv_hi qkv_split band_hi "
        "gray_first gray_made gray_hi_made gray_split halo_moved conv_done edge_made h_made "
        "mv1_made rstd1_made xn1_made xT_done xT_hi_made xT_split q_done k_done v_done q_made k_made v_made "
        "s_done masked_made probs_made pT_done pT_made pv_done srec_made h2_made mv2_made rstd2_made xn2_made "
        "xn2T_done xn2T_made gate_done logit_made gexp_made hits_made rank_done rank_read places_made "
        "res_made gated_places_made count_done tables_made padded b1_in wo_in wo_hi wo_split w1_hi_made w1_lo_made "
        "e_T e_hi e_split e_b_done e_a_done e_b_made e_sig_made e_a_read e_out_made "
        "c_first c_sum c_T c_hi c_split c_y c_out dve_step pool_step").split()}
    x_in = [sem(f"x_in{i}") for i in range(2)]
    stage_in = [sem(f"stage_in{i}") for i in range(NS)]
    scattered = [sem(f"scattered{i}") for i in range(2)]
    res_stored = [sem(f"res_stored{i}") for i in range(4)]
    e_loaded = [sem(f"e_loaded{i}") for i in range(2)]
    e_stored = [sem(f"e_stored{i}") for i in range(2)]
    c_loaded = [sem(f"c_loaded{i}") for i in range(NB)]
    c_res = [sem(f"c_res{i}") for i in range(NB)]
    c_stored = [sem(f"c_stored{i}") for i in range(NB)]

    block = ctx.enter_context(nc.Block())

    STEPS = IMAGES + 3
    CHUNKS = EXPERTS * KD
    FREE_CHUNKS = CHUNKS - KD

    def chunk_at(step, slot):
        c = 2 * step + slot
        if c < FREE_CHUNKS:
            return c
        return {(IMAGES, 1): FREE_CHUNKS, (IMAGES + 1, 0): FREE_CHUNKS + 1}.get((step, slot))

    def live(u):
        return 0 <= u < IMAGES

    def three(k_range):
        return [(g, f, k) for k in k_range for g, f in ((0, 0), (0, 1), (1, 0))]

    def w1_chunk(c):
        return w1T[(c % KD) * P:(c % KD + 1) * P, c // KD, :]

    def weight_of(t, k):
        return weight[:, ds(TOP * t + k, 1)]

    @block.sync
    def _(sp):
        def load_image(u):
            if u >= 2:
                sp.wait_ge(S["gray_made"], u - 1)
            sp.dma_start(xs_img[:, u % 2], x[u].rearrange("c (t p) w -> p c t w", p=P)).then_inc(x_in[u % 2], 16)

        sp.dma_start(cst[:, :], consts[:, 0:C_UP]).then_inc(S["consts_in"], 16)
        sp.dma_start(early, consts[:, C_UP:C_ALL]).then_inc(S["consts_in"], 16)
        load_image(0)
        sp.dma_start(stage_qkv[:, 0], wqT.rearrange("(k p) e -> p k e", p=P)).then_inc(S["qkv_in"], 16)
        sp.dma_start(stage_qkv[:, 1], wkT.rearrange("(k p) e -> p k e", p=P)).then_inc(S["qkv_in"], 16)
        sp.dma_start(stage_qkv[:, 2], wvT.rearrange("(k p) e -> p k e", p=P)).then_inc(S["qkv_in"], 16)
        load_image(1)
        for n in range(MAX_TILES - LEAST_TILES):
            r = EXPERTS * REGION + n * P
            sp.dma_start(rows_in[r:r + P, :], zeros).then_inc(S["regions_zeroed"], 16)

        def load_chunk(c):
            if c == 2:
                sp.wait_ge(S["qkv_split"], 3)
            if c >= NS:
                sp.wait_ge(S["w1_lo_made"], c - NS + 1)
            sp.dma_start(stage[:, c % NS, :], w1_chunk(c)).then_inc(stage_in[c % NS], 16)

        load_chunk(0)
        load_chunk(1)

        def halo(u):
            sp.wait_ge(S["gray_split"], u + 1)
            if u >= 1:
                sp.wait_ge(S["conv_done"], 2 * u)
            for t, row in ((0, 0), (1, P - 1)):
                for half, parts in ((gray_hi, (0, 3)), (gray_lo, (6,))):
                    src = half[row:row + 1, 1 - t, 0:SIZE]
                    wide = bass.AP(tensor=src.tensor, offset=src.offset, ap=[list(src.ap[0]), [1, 3], [1, SIZE]]).bitcast(F32)
                    for p0 in parts:
                        sp.dma_start(halo_in[p0:p0 + 3, t, :].bitcast(F32), wide).then_inc(S["halo_moved"], 16)

        halo(0)
        for s in range(STEPS):
            if live(s + 2):
                load_image(s + 2)
            if live(s + 1):
                halo(s + 1)
            for c in (2 * s + 2, 2 * s + 3):
                if c < CHUNKS:
                    load_chunk(c)
            if live(s - 3):
                u = s - 3
                sp.wait_ge(S["res_made"], 2 * (u + 1))
                sp.dma_start(resid[u * SIZE:(u + 1) * SIZE, :].rearrange("(t p) w -> p t w", p=P),
                             h_all[:, u % 4]).then_inc(res_stored[u % 4], 16)
            if s == IMAGES:
                sp.wait_ge(S["xT_done"], IMAGES)
                sp.wait_ge(S["qkv_split"], 3)
                sp.wait_ge(S["w1_lo_made"], CHUNKS)
                sp.dma_start(b1_all, b1.rearrange("e h -> (e h)").partition_broadcast(P)).then_inc(S["b1_in"], 16)
        sp.wait_ge(S["pv_done"], IMAGES)
        sp.dma_start(wo_raw, woT.rearrange("(k p) e -> p k e", p=P)).then_inc(S["wo_in"], 16)
        sp.wait_ge(S["tables_made"], 1)
        for e in range(EXPERTS):
            r = sp.value_load(pad_i[0:1, e:e + 1], min_val=0, max_val=ROWS - P)
            sp.dma_start(rows_in[ds(r, P), :], zeros).then_inc(S["padded"], 16)
        for n in range(2):
            sp.wait_ge(scattered[n], 16 * 4 * IMAGES // 2)
        sp.wait_ge(S["regions_zeroed"], 16 * (MAX_TILES - LEAST_TILES))
        sp.wait_ge(S["padded"], 16 * EXPERTS)
        for n in range(4):
            sp.wait_ge(res_stored[n], 16 * IMAGES // 4)

        def load_rows(j, p):
            r = sp.value_load(tab_row[0:1, ds(j, 1)], min_val=0, max_val=ROWS - P)
            sp.dma_start(e_in[:, p, :], rows_in[ds(r, P), :]).then_inc(e_loaded[p], 16)

        def store_rows(j, p):
            sp.wait_ge(S["e_out_made"], j + 1)
            sp.dma_start(rows_gated[ds(j * P, P), :], e_out[:, p, :]).then_inc(e_stored[p], 16)

        load_rows(0, 0)
        load_rows(1, 1)
        sp.wait_ge(S["e_T"], 1)
        load_rows(2, 0)
        LOOPED = (MAX_TILES - 3) // 2
        with sp.Fori(0, LOOPED) as i:
            for p in range(2):
                sp.wait_ge(S["e_T"], 2 * i + p + 2)
                load_rows(2 * i + p + 3, 1 - p)
                store_rows(2 * i + p, p)
        for j in range(2 * LOOPED, MAX_TILES):
            store_rows(j, j % 2)

        sp.wait_ge(S["e_a_read"], MAX_TILES)
        for b in range(NB):
            sp.dma_start(res_in[:, b, :], resid[b * P:(b + 1) * P, :]).then_inc(c_res[b], 16)
        with sp.Fori(0, TILES // NB - 1) as i:
            for b in range(NB):
                t = NB * i + b
                sp.wait_ge(S["c_out"], t + 1)
                sp.dma_start(out[ds(t * P, P), :], result[:, b, :]).then_inc(c_stored[b], 16)
                sp.dma_start(res_in[:, b, :], resid[ds((t + NB) * P, P), :]).then_inc(c_res[b], 16)
        for b in range(NB):
            t = TILES - NB + b
            sp.wait_ge(S["c_out"], t + 1)
            sp.dma_start(out[t * P:(t + 1) * P, :], result[:, b, :]).then_inc(c_stored[b], 16)
        for b in range(NB):
            sp.wait_ge(c_stored[b], 16 * TILES // NB)

    @block.scalar
    def _(act):
        act.dma_start(taps[:, :], scharr.rearrange("k o a b -> (k o a b)").partition_broadcast(P)).then_inc(S["taps_in"], 16)
        for c in range(3):
            with nc.allow_non_contiguous_dma(reason="18 values"):
                act.dma_start(htap[3 * c:3 * c + 3, 0, :], scharr.rearrange("k o a b -> b (k o a)")).then_inc(S["halo_taps_in"], 16)
        act.dma_start(bv_all[:, :], bv.partition_broadcast(P)).then_inc(S["small_in"], 16)
        act.dma_start(bo_all[:, :], bo.partition_broadcast(P)).then_inc(S["small_in"], 16)
        with nc.allow_non_contiguous_dma(reason="256 values each"):
            act.dma_start(bqk[:, 0:KD], bq.rearrange("(k p) -> p k", p=P)).then_inc(S["small_in"], 16)
            act.dma_start(bqk[:, KD:2 * KD], bk.rearrange("(k p) -> p k", p=P)).then_inc(S["small_in"], 16)
            act.dma_start(wg_sb[:, :, :], wgT.rearrange("(k p) e -> p k e", p=P)).then_inc(S["small_in"], 16)

        def gray_first(u):
            act.wait_ge(x_in[u % 2], 16 * (u // 2 + 1))
            if u >= 1:
                act.wait_ge(S["gray_split"], u)
            act.activation(gray, xs_img[:, u % 2, 0], ACT.Copy, scale=GRAY[0]).then_inc(S["gray_first"], 1)

        def gray_high(u):
            act.wait_ge(S["gray_made"], u + 1)
            if u >= 1:
                act.wait_ge(S["conv_done"], 2 * u)
            act.activation(gray_hi[:, :, 1:1 + SIZE], gray, ACT.Copy).then_inc(S["gray_hi_made"], 1)

        def edges(u, t):
            act.wait_ge(S["conv_done"], 2 * u + t + 1)
            if u >= 1:
                act.wait_ge(S["h_made"], 2 * u + t - 1)
            else:
                act.wait_ge(S["qkv_split"], 3)
            act.activation(edge[:, t], ps_conv[t][:, :].rearrange("p (k w) -> p k w", k=2), ACT.Abs).then_inc(S["edge_made"], 1)

        def split_high(c):
            act.wait_ge(stage_in[c % NS], 16 * (c // NS + 1))
            if c >= FREE_CHUNKS:
                act.wait_ge(S["v_done"], IMAGES)
            act.activation(w1_hi[:, c * 2 * H:(c + 1) * 2 * H], stage[:, c % NS, :], ACT.Copy)\
               .then_inc(S["w1_hi_made"], 1)

        gray_first(0)
        act.wait_ge(S["bands_made"], 6)
        act.activation(band[:, 0], band_raw, ACT.Copy).then_inc(S["band_hi"], 1)
        gray_high(0)
        act.wait_ge(S["qkv_in"], 48)
        for w in range(3):
            act.activation(wqkv[w][:, 0], stage_qkv[:, w], ACT.Copy).then_inc(S["qkv_hi"], 1)
        act.wait_ge(S["small_in"], 80)

        for s in range(STEPS):
            if live(s - 1):
                u = s - 1
                act.wait_ge(S["xT_done"], u + 1)
                if u >= 1:
                    act.wait_ge(S["v_done"], u)
                act.activation(xT_f[:, 0], ps_xT[:, :].rearrange("p (k n) -> p k n", k=KD), ACT.Copy)\
                   .then_inc(S["xT_hi_made"], 1)
            if chunk_at(s, 0) is not None:
                split_high(chunk_at(s, 0))
            if live(s + 1):
                gray_first(s + 1)
            if live(s):
                edges(s, 0)
            if live(s - 2):
                u = s - 2
                act.wait_ge(S["pT_done"], u + 1)
                if u >= 1:
                    act.wait_ge(S["pv_done"], u)
                act.activation(probsT, ps_pT[:, 0:2 * P].rearrange("p (t n) -> p t n", t=2), ACT.Copy)\
                   .then_inc(S["pT_made"], 1)
            if live(s - 3):
                u = s - 3
                act.wait_ge(S["logit_made"], u + 1)
                act.activation(gexp[:, :, :], logit[:, :, :], ACT.Exp).then_inc(S["gexp_made"], 1)
            if live(s):
                edges(s, 1)
            if live(s + 1):
                gray_high(s + 1)
            if live(s - 1):
                u = s - 1
                for n, (done, made, ps, dst) in enumerate((("q_done", "q_made", ps_q, qT), ("k_done", "k_made", ps_k, kT))):
                    act.wait_ge(S[done], u + 1)
                    if u >= 1:
                        act.wait_ge(S["s_done"], u)
                    for m in range(KD):
                        act.activation(dst[:, m], ps[:, m * SIZE:(m + 1) * SIZE], ACT.Identity,
                                       bias=bqk[:, n * KD + m:n * KD + m + 1]).then_inc(S[made], 1)
            if chunk_at(s, 1) is not None:
                split_high(chunk_at(s, 1))
            if live(s - 1):
                u = s - 1
                act.wait_ge(S["masked_made"], u + 1)
                if u >= 1:
                    act.wait_ge(S["pT_done"], u)
                    act.wait_ge(S["srec_made"], u)
                for t in range(2):
                    act.activation(probs[:, t], masked[:, t], ACT.Exp, bias=nsmax[:, t:t + 1],
                                   accum_out=ssum[:, t:t + 1]).then_inc(S["probs_made"], 1)
            if live(s - 2):
                u = s - 2
                act.wait_ge(S["xn2T_done"], u + 1)
                if u >= 1:
                    act.wait_ge(S["gate_done"], u)
                act.activation(xn2T, ps_xn2T[:, :].rearrange("p (k n) -> p k n", k=KD), ACT.Copy)\
                   .then_inc(S["xn2T_made"], 1)

        act.wait_ge(S["wo_in"], 16)
        act.wait_ge(S["v_done"], IMAGES)
        act.activation(wo_h[:, 0], wo_raw, ACT.Copy).then_inc(S["wo_hi"], 1)

        def e_high(j, p, first=False):
            act.wait_ge(S["e_T"], j + 1)
            if not first:
                act.wait_ge(S["e_a_done"], j - 1)
            act.activation(xT_e[:, p, 0], ps_et[p][:, 0:KD * P].rearrange("p (k n) -> p k n", k=KD), ACT.Copy)\
               .then_inc(S["e_hi"], 1)

        def e_sigmoid(j, p, first=False):
            act.wait_ge(S["e_b_made"], j + 1)
            if not first:
                act.wait_ge(S["e_out_made"], j - 1)
            act.activation(e_sig[:, p], e_b[:, p], ACT.Sigmoid).then_inc(S["e_sig_made"], 1)

        e_high(0, 0, True)
        e_high(1, 1, True)
        e_sigmoid(0, 0, True)
        e_high(2, 0)
        e_sigmoid(1, 1, True)
        with act.Fori(1, MAX_TILES // 2) as i:
            e_high(2 * i + 1, 1)
            e_sigmoid(2 * i, 0)
            e_high(2 * i + 2, 0)
            e_sigmoid(2 * i + 1, 1)
        e_sigmoid(MAX_TILES - 1, 0)

        def c_high(t, p, first=False):
            act.wait_ge(S["c_T"], t + 1)
            if not first:
                act.wait_ge(S["c_y"], t - 1)
            act.activation(sumT[p][:, 0], ps_ct[p][:, :].rearrange("p (k n) -> p k n", k=KH), ACT.Copy)\
               .then_inc(S["c_hi"], 1)

        def c_first(t, b, at16):
            act.wait_ge(c_loaded[b], at16)
            act.activation(top1[:, b], top1[:, b], ACT.Copy, scale=weight_of(t, 0)).then_inc(S["c_first"], 1)

        c_first(0, 0, 32)
        for t in range(NB):
            c_first(t + 1, (t + 1) % NB, 32 * ((t + 1) // NB + 1))
            c_high(t, t % 2, t < 2)
        with act.Fori(1, TILES // NB - 1) as i:
            for b in range(NB):
                t = NB * i + b
                c_first(t + 1, (b + 1) % NB, 32 * i + 32 * ((b + 1) // NB + 1))
                c_high(t, b % 2)
        for t in range(TILES - NB, TILES):
            if t + 1 < TILES:
                c_first(t + 1, (t + 1) % NB, 32 * ((t + 1) // NB + 1))
            c_high(t, t % 2)


    @block.gpsimd
    def _(pool):
        def split_low(c):
            pool.wait_ge(S["w1_hi_made"], c + 1)
            cols = slice(c * 2 * H, (c + 1) * 2 * H)
            pool.tensor_tensor(w1_lo[:, cols], stage[:, c % NS, :], w1_hi[:, cols].bitcast(F32), ALU.subtract)\
                .then_inc(S["w1_lo_made"], 1)

        steps = 0

        def inverse_deviation(norm, u, moments, made):
            nonlocal steps
            pool.wait_ge(S[moments], u + 1)
            pool.tensor_scalar(vare[:, norm], mv[:, norm, :, 1], EPS_LN, None, ALU.add).then_inc(S["pool_step"], 1)
            steps += 1
            pool.wait_ge(S["pool_step"], steps)
            pool.tensor_tensor(rstd[:, norm], vare[:, norm], neg_half[:, :], ALU.pow).then_inc(S[made], 1)

        pool.memset(neg_half[:, :], -0.5).then_inc(S["pool_step"], 1)
        steps += 1
        pool.wait_ge(S["pool_step"], steps)

        def scatter(u):
            pool.wait_ge(S["places_made"], u + 1)
            for t in range(2):
                for k in range(TOP):
                    pool.indirect_dma_start(
                        rows_in, bass.IndirectOffsetOnAxis(ap=place_i[:, 2 * u + t, k:k + 1], axis=0),
                        xn2[:, u % 2, t, :], None).then_inc(scattered[u % 2], 16)

        for s in range(STEPS + 1):
            if live(s - 4):
                scatter(s - 4)
            if s >= 1 and chunk_at(s - 1, 1) is not None:
                split_low(chunk_at(s - 1, 1))
            if live(s - 2):
                inverse_deviation(1, s - 2, "mv2_made", "rstd2_made")
            if live(s):
                inverse_deviation(0, s, "mv1_made", "rstd1_made")
            if chunk_at(s, 0) is not None:
                split_low(chunk_at(s, 0))

        pool.wait_ge(S["gated_places_made"], 1)
        pool.wait_ge(S["e_a_read"], MAX_TILES)
        for p in range(2):
            pool.wait_ge(e_stored[p], 16 * ((MAX_TILES + 1 - p) // 2))
        for t in range(TILES):
            if t >= NB:
                pool.wait_ge(S["c_T"], t - NB + 1)
            for k, rows in enumerate((top1, top2)):
                pool.indirect_dma_start(
                    rows[:, t % NB, :], None, rows_gated,
                    bass.IndirectOffsetOnAxis(ap=gated_i[:, t, k:k + 1], axis=0)).then_inc(c_loaded[t % NB], 16)

    @block.vector
    def _(dve):
        steps = 0

        def mark(ins):
            nonlocal steps
            steps += 1
            ins.then_inc(S["dve_step"], 1)

        def settle():
            dve.wait_ge(S["dve_step"], steps)

        def step(ins):
            mark(ins)
            settle()

        for half in (gray_hi, gray_lo):
            for col in (0, GW - 1):
                dve.memset(half[:, :, col:col + 1].bitcast(F32), 0.0)
        dve.memset(ones[:, :], 1.0)
        dve.memset(one8[:, :], 1.0)
        dve.memset(earlier[:, :, :], 0.0)
        step(dve.memset(halo_w.bitcast(F32), 0.0))

        dve.wait_ge(S["taps_in"], 16)
        step(dve.tensor_scalar(taps[:, :], taps[:, :], 0.5, None, ALU.mult))
        dve.wait_ge(S["consts_in"], 32)
        for dy, diagonal in ((0, early[:, 0:P]), (1, ident), (2, early[:, P:2 * P])):
            for k in range(2):
                for dx in range(3):
                    w = taps[:, 9 * k + 3 * dy + dx:9 * k + 3 * dy + dx + 1]
                    b = band_raw[:, 3 * k + dx, :]
                    if dy == 0:
                        last = dve.tensor_scalar(b, diagonal, w, None, ALU.mult)
                    else:
                        last = dve.scalar_tensor_tensor(b, diagonal, w, b, ALU.mult, ALU.add)
                    if dy == 2:
                        last.then_inc(S["bands_made"], 1)
            if dy < 2:
                step(last)
        dve.wait_ge(S["halo_taps_in"], 48)
        step(dve.tensor_scalar(htap[:, 1], htap[:, 0], 0.5, None, ALU.mult))
        step(dve.tensor_copy(htap_r[:, :], htap[:, 1]))
        step(dve.tensor_tensor(htap[:, 2], htap[:, 1], htap_r[:, :].bitcast(F32), ALU.subtract))
        step(dve.tensor_scalar(htap[:, 2], htap[:, 2], cst[0:9, C_SEL + 1:C_SEL + 2], None, ALU.mult))
        step(dve.scalar_tensor_tensor(htap[:, 3], htap_r[:, :].bitcast(F32), cst[0:9, C_SEL:C_SEL + 1], htap[:, 2],
                                      ALU.mult, ALU.add))
        for t, dy, col in ((0, 2, P - 1), (1, 0, 0)):
            dve.tensor_copy(halo_w[:, t, :, col], htap[:, 3, dy:6:3]).then_inc(S["halo_made"], 1)
        dve.tensor_copy(before[:, :], early[:, 2 * P:3 * P]).then_inc(S["before_made"], 1)

        def gray_rest(u):
            dve.wait_ge(x_in[u % 2], 16 * (u // 2 + 1))
            dve.wait_ge(S["gray_first"], u + 1)
            step(dve.scalar_tensor_tensor(gray, xs_img[:, u % 2, 1], GRAY[1], gray, ALU.mult, ALU.add))
            dve.scalar_tensor_tensor(gray, xs_img[:, u % 2, 2], GRAY[2], gray, ALU.mult, ALU.add)\
               .then_inc(S["gray_made"], 1)

        def gray_low(u):
            dve.wait_ge(S["gray_hi_made"], u + 1)
            dve.tensor_tensor(gray_lo[:, :, 1:1 + SIZE], gray, gray_hi[:, :, 1:1 + SIZE].bitcast(F32), ALU.subtract)\
               .then_inc(S["gray_split"], 1)

        gray_rest(0)
        dve.wait_ge(S["band_hi"], 1)
        dve.tensor_tensor(band[:, 1], band_raw, band[:, 0].bitcast(F32), ALU.subtract).then_inc(S["bands_split"], 1)
        gray_low(0)
        for w in range(3):
            dve.wait_ge(S["qkv_hi"], w + 1)
            dve.tensor_tensor(wqkv[w][:, 1], stage_qkv[:, w], wqkv[w][:, 0].bitcast(F32), ALU.subtract)\
               .then_inc(S["qkv_split"], 1)
        dve.wait_ge(S["small_in"], 80)

        def sums(norm, rows, t):
            mark(dve.bn_stats(stats[:, norm, t, :], rows[:, t, :]))

        def moments(norm, made):
            settle()
            for t in range(2):
                last = dve.bn_aggr(mv[:, norm, t, :], stats[:, norm, t, :])
            last.then_inc(S[made], 1)

        def normalise(norm, dst, rows, u, have, made):
            dve.wait_ge(S[have], u + 1)
            for t in range(2):
                last = dve.tensor_scalar(dst[:, t, :], rows[:, t, :], mv[:, norm, t, 0:1], rstd[:, norm, t:t + 1],
                                         ALU.subtract, ALU.mult)
            last.then_inc(S[made], 1)

        def edge_sum(u, t):
            dve.wait_ge(S["edge_made"], 2 * u + t + 1)
            if u >= 4:
                dve.wait_ge(res_stored[u % 4], 16 * (u // 4))
            dve.tensor_tensor(h_all[:, u % 4, t], edge[:, t, 0], edge[:, t, 1], ALU.add).then_inc(S["h_made"], 1)

        def topk_logits(u):
            dve.wait_ge(S["gate_done"], u + 1)
            ps = ps_gate[:, 0:2 * EXPERTS].rearrange("p (t e) -> p t e", t=2)
            step(dve.tensor_reduce(gmax[:, :], ps, AX.X, ALU.max))
            dve.tensor_tensor(logit[:, :, :], ps, gmax[:, :].unsqueeze(2).broadcast_to([P, 2, EXPERTS]), ALU.subtract)\
               .then_inc(S["logit_made"], 1)

        def pairs(a, n):
            return a[:, :].unsqueeze(2).broadcast_to([P, 2, n])

        def top_sum(u):
            dve.wait_ge(S["gexp_made"], u + 1)
            mark(dve.tensor_reduce(gsum[:, :], gexp[:, :, :], AX.X, ALU.add))

        def top_reciprocal():
            settle()
            mark(dve.reciprocal(grec[:, :], gsum[:, :]))

        def top_softmax():
            settle()
            mark(dve.tensor_tensor(gprob[:, :, :], gexp[:, :, :], pairs(grec, EXPERTS), ALU.mult))

        def top_best():
            settle()
            for t in range(2):
                last = dve.max(best[:, t, :], gprob[:, t, :])
            mark(last)

        def top_which():
            settle()
            for t in range(2):
                last = dve.max_index(best_at[:, t, :], best[:, t, :], gprob[:, t, :])
            mark(last)
            mark(dve.tensor_tensor(den[:, :], best[:, :, 0], best[:, :, 1], ALU.add))

        def top_which_f():
            settle()
            mark(dve.tensor_copy(best_f[:, :, :], best_at[:, :, 0:TOP]))
            mark(dve.tensor_scalar(den[:, :], den[:, :], EPS_TOP, None, ALU.add))

        def top_chosen(u):
            settle()
            iota = cst[:, C_IOTA:C_IOTA + EXPERTS].unsqueeze(1).unsqueeze(1).broadcast_to([P, 2, TOP, EXPERTS])
            mark(dve.tensor_tensor(chosen_all[:, 2 * u:2 * u + 2], iota,
                                   best_f[:, :, :].unsqueeze(3).broadcast_to([P, 2, TOP, EXPERTS]), ALU.is_equal))
            mark(dve.reciprocal(den[:, :], den[:, :]))

        def top_hit(u):
            if u >= 1:
                dve.wait_ge(S["rank_done"], u)
                mark(dve.tensor_copy(earlier[:, 0, :], earlier[:, 2, :]))
            settle()
            mark(dve.tensor_tensor(hit[:, :, :], chosen_all[:, 2 * u:2 * u + 2, 0, :], chosen_all[:, 2 * u:2 * u + 2, 1, :], ALU.add))
            mark(dve.tensor_tensor(weights_at(u), best[:, :, 0:TOP], pairs(den, TOP), ALU.mult))

        def top_earlier():
            settle()
            mark(dve.tensor_tensor(earlier[:, 1, :], earlier[:, 0, :], hit[:, 0, :], ALU.add))

        def top_all(u):
            settle()
            dve.tensor_tensor(earlier[:, 2, :], earlier[:, 1, :], hit[:, 1, :], ALU.add).then_inc(S["hits_made"], 1)
            w = weights_at(u)
            mark(dve.tensor_tensor(wsum[:, :], w[:, :, 0], w[:, :, 1], ALU.add))

        def weights_at(u):
            return weight[:, 2 * TOP * u:2 * TOP * (u + 1)].rearrange("p (t k) -> p t k", t=2)

        def topk_places(u):
            dve.wait_ge(S["rank_done"], u + 1)
            base = cst[:, C_BASE:C_BASE + EXPERTS].unsqueeze(1).broadcast_to([P, 2, EXPERTS])
            dve.tensor_tensor(place[:, :, :], ps_rank[:, 0:2 * EXPERTS].rearrange("p (t e) -> p t e", t=2), base, ALU.add)\
               .then_inc(S["rank_read"], 1)
            dve.wait_ge(S["rank_read"], u + 1)
            step(dve.tensor_tensor(placed[:, :, :, :], chosen_all[:, 2 * u:2 * u + 2],
                                   place[:, :, :].unsqueeze(2).broadcast_to([P, 2, TOP, EXPERTS]), ALU.mult))
            step(dve.tensor_reduce(place_f[:, :, :], placed[:, :, :, :], AX.X, ALU.add))
            dve.tensor_copy(place_i[:, 2 * u:2 * u + 2, :], place_f[:, :, :])\
               .then_inc(S["places_made"], 1)

        for s in range(STEPS):
            new, old, gated = live(s), live(s - 2), live(s - 3)
            h_new, h_old, h_gated = (h_all[:, n % 4] for n in (s, s - 2, s - 3))
            if live(s - 1):
                u = s - 1
                dve.wait_ge(S["xT_hi_made"], u + 1)
                dve.tensor_tensor(xT_f[:, 1], ps_xT[:, :].rearrange("p (k n) -> p k n", k=KD),
                                  xT_f[:, 0].bitcast(F32), ALU.subtract).then_inc(S["xT_split"], 1)
            if live(s + 1):
                gray_rest(s + 1)
            if old:
                dve.wait_ge(S["probs_made"], 2 * (s - 1))
                dve.reciprocal(srec[:, :], ssum[:, :]).then_inc(S["srec_made"], 1)
            if new:
                edge_sum(s, 0)
            if gated:
                topk_logits(s - 3)
            if old:
                dve.wait_ge(S["srec_made"], s - 1)
                dve.wait_ge(S["pv_done"], s - 1)
                for t in range(2):
                    dve.scalar_tensor_tensor(h_old[:, t], ps_pv[:, t * D:(t + 1) * D], srec[:, t:t + 1],
                                             h_old[:, t], ALU.mult, ALU.add).then_inc(S["h2_made"], 1)
            if gated:
                top_sum(s - 3)
            if old:
                for t in range(2):
                    dve.wait_ge(S["h2_made"], 2 * (s - 2) + t + 1)
                    sums(1, h_old, t)
            if gated:
                top_reciprocal()
            if old:
                moments(1, "mv2_made")
            if gated:
                top_softmax()
            if new:
                edge_sum(s, 1)
            if live(s + 1):
                gray_low(s + 1)
            if gated:
                top_best()
            if new:
                dve.wait_ge(S["h_made"], 2 * (s + 1))
                for t in range(2):
                    sums(0, h_new, t)
            if gated:
                top_which()
            if new:
                moments(0, "mv1_made")
            if gated:
                top_which_f()
            if old:
                if s >= 4:
                    dve.wait_ge(scattered[s % 2], 64 * ((s - 2) // 2))
                normalise(1, xn2[:, s % 2], h_old, s - 2, "rstd2_made", "xn2_made")
            if gated:
                top_chosen(s - 3)
            if new:
                if s >= 1:
                    dve.wait_ge(S["xT_done"], s)
                normalise(0, xn1, h_new, s, "rstd1_made", "xn1_made")
            if gated:
                top_hit(s - 3)
            if gated:
                top_earlier()
            if live(s - 1):
                u = s - 1
                dve.wait_ge(S["v_done"], u + 1)
                if u >= 1:
                    dve.wait_ge(S["pv_done"], u)
                dve.tensor_tensor(v_sb, ps_v[:, :].rearrange("p (t e) -> p t e", t=2),
                                  bv_all[:, :].unsqueeze(1).broadcast_to([P, 2, D]), ALU.add).then_inc(S["v_made"], 1)
            if gated:
                top_all(s - 3)
            if live(s - 1):
                u = s - 1
                dve.wait_ge(S["s_done"], u + 1)
                if u >= 1:
                    dve.wait_ge(S["probs_made"], 2 * u)
                for t in range(2):
                    last = dve.tensor_tensor_reduce(masked[:, t], ps_s[:, t * P:(t + 1) * P], cst[:, C_MASK:C_MASK + P],
                                                    1.0, NEVER, ALU.add, ALU.max, smax[:, t:t + 1])
                step(last)
                dve.tensor_scalar(nsmax[:, :], smax[:, :], -1.0, None, ALU.mult).then_inc(S["masked_made"], 1)
            if gated:
                topk_places(s - 3)
                for t in range(2):
                    dve.scalar_tensor_tensor(h_gated[:, t], bo_all[:, :], wsum[:, t:t + 1], h_gated[:, t],
                                             ALU.mult, ALU.add).then_inc(S["res_made"], 1)

        dve.wait_ge(S["count_done"], 1)
        rows_of_expert = ps_rank[:, 0:EXPERTS]
        dve.tensor_tensor(pad_f[:, :], rows_of_expert[0:1], cst[0:1, C_BASE:C_BASE + EXPERTS], ALU.add)
        step(dve.tensor_scalar(tiles_i[:, 0], rows_of_expert, float(P - 1), None, ALU.add))
        dve.tensor_copy(pad_i[:, :], pad_f[:, :])
        step(dve.tensor_scalar(tiles_i[:, 1], tiles_i[:, 0], P.bit_length() - 1, None, ALU.logical_shift_right))
        step(dve.tensor_copy(tiles_f[:, :], tiles_i[:, 1]))
        step(dve.tensor_tensor_scan(ends[:, :], one8[:, :], tiles_f[:, :], 0.0, ALU.mult, ALU.add))
        whole = [1, MAX_TILES, EXPERTS]
        tile_no = cst[0:1, C_TILE:C_TILE + MAX_TILES]
        step(dve.tensor_tensor(passed, tile_no.unsqueeze(2).broadcast_to(whole),
                               ends[0:1, :].unsqueeze(1).broadcast_to(whole), ALU.is_ge))
        step(dve.tensor_tensor(passed_n, passed, tiles_f[0:1, :].unsqueeze(1).broadcast_to(whole), ALU.mult))
        step(dve.tensor_reduce(expert_of, passed, AX.X, ALU.add))
        step(dve.tensor_reduce(start_of, passed_n, AX.X, ALU.add))
        step(dve.tensor_tensor(tiles_in, tile_no, start_of, ALU.subtract))
        step(dve.tensor_scalar(rows_before, tiles_in, float(P), None, ALU.mult))
        dve.scalar_tensor_tensor(tab_row[:, :], expert_of, float(REGION), rows_before, ALU.mult, ALU.add)
        dve.tensor_scalar(tab_w[:, :], expert_of, float(EXPERTS - 1), float(WE), ALU.min, ALU.mult)
        dve.tensor_scalar(tab_b[:, :], expert_of, float(EXPERTS - 1), float(2 * H), ALU.min, ALU.mult)\
           .then_inc(S["tables_made"], 1)
        dve.wait_ge(S["tables_made"], 1)

        step(dve.tensor_tensor(shift[:, :], ends[:, :], tiles_f[:, :], ALU.subtract))
        step(dve.scalar_tensor_tensor(shift[:, :], shift[:, :], float(P), cst[:, C_BASE:C_BASE + EXPERTS], ALU.mult, ALU.subtract))
        each = [P, TILES * TOP, EXPERTS]
        step(dve.tensor_tensor(shifts, chosen_all[:, :, :, :].rearrange("p t k e -> p (t k) e"),
                               shift[:, :].unsqueeze(1).broadcast_to(each), ALU.mult))
        step(dve.tensor_reduce(shift_of, shifts, AX.X, ALU.add))
        dve.tensor_tensor(gated_i[:, :, :].rearrange("p t k -> p (t k)"), place_i[:, :, :].rearrange("p t k -> p (t k)"),
                          shift_of, ALU.add).then_inc(S["gated_places_made"], 1)

        dve.wait_ge(S["wo_hi"], 1)
        dve.tensor_tensor(wo_h[:, 1], wo_raw, wo_h[:, 0].bitcast(F32), ALU.subtract).then_inc(S["wo_split"], 1)

        dve.wait_ge(S["b1_in"], 16)

        def e_low(j, p):
            dve.wait_ge(S["e_hi"], j + 1)
            dve.tensor_tensor(xT_e[:, p, 1], ps_et[p][:, 0:KD * P].rearrange("p (k n) -> p k n", k=KD),
                              xT_e[:, p, 0].bitcast(F32), ALU.subtract).then_inc(S["e_split"], 1)

        def e_gate(j, p, stored, first=False):
            off = dve.value_load(tab_b[0:1, ds(j, 1)], min_val=0, max_val=(EXPERTS - 1) * 2 * H)
            dve.wait_ge(S["e_b_done"], j + 1)
            if not first:
                dve.wait_ge(S["e_sig_made"], j - 1)
            dve.tensor_tensor(e_b[:, p], ps_b[p][:, :], b1_all[:, ds(off + H, H)], ALU.add).then_inc(S["e_b_made"], 1)
            dve.wait_ge(S["e_a_done"], j + 1)
            dve.tensor_tensor(e_a[:, p], ps_a[p][:, :], b1_all[:, ds(off, H)], ALU.add).then_inc(S["e_a_read"], 1)
            dve.wait_ge(S["e_a_read"], j + 1)
            dve.wait_ge(S["e_sig_made"], j + 1)
            if not first:
                dve.wait_ge(e_stored[p], stored)
            dve.tensor_tensor(e_out[:, p], e_a[:, p], e_sig[:, p], ALU.mult).then_inc(S["e_out_made"], 1)

        e_low(0, 0)
        e_low(1, 1)
        e_gate(0, 0, 0, True)
        e_low(2, 0)
        e_gate(1, 1, 0, True)
        with dve.Fori(1, MAX_TILES // 2) as i:
            e_low(2 * i + 1, 1)
            e_gate(2 * i, 0, 16 * i)
            e_low(2 * i + 2, 0)
            e_gate(2 * i + 1, 1, 16 * i)
        e_gate(MAX_TILES - 1, 0, 16 * (MAX_TILES // 2))

        def c_sum(t, b, loaded):
            dve.wait_ge(c_loaded[b], loaded)
            dve.wait_ge(S["c_first"], t + 1)
            dve.scalar_tensor_tensor(top2[:, b], top2[:, b], weight_of(t, 1), top1[:, b], ALU.mult, ALU.add)\
               .then_inc(S["c_sum"], 1)

        def c_low(t, p):
            dve.wait_ge(S["c_hi"], t + 1)
            dve.tensor_tensor(sumT[p][:, 1], ps_ct[p][:, :].rearrange("p (k n) -> p k n", k=KH),
                              sumT[p][:, 0].bitcast(F32), ALU.subtract).then_inc(S["c_split"], 1)

        def c_result(t, b, turn, first=False):
            dve.wait_ge(S["c_y"], t + 1)
            dve.wait_ge(c_res[b], turn)
            if not first:
                dve.wait_ge(c_stored[b], turn - 16)
            dve.tensor_tensor(result[:, b], ps_y[b % 2][:, 0:D], res_in[:, b], ALU.add).then_inc(S["c_out"], 1)

        c_sum(0, 0, 32)
        for t in range(NB + 1):
            c_sum(t + 1, (t + 1) % NB, 32 * ((t + 1) // NB + 1))
            c_low(t, t % 2)
            if t >= 1:
                c_result(t - 1, t - 1, 16, True)
        with dve.Fori(1, TILES // NB - 1) as i:
            for b in range(NB):
                t = NB * i + b + 1
                c_sum(t + 1, (b + 2) % NB, 32 * i + 32 * ((b + 2) // NB + 1))
                c_low(t, (b + 1) % 2)
                c_result(t - 1, b, 16 * i + 16)
        for t in range(TILES - NB + 1, TILES):
            if t + 1 < TILES:
                c_sum(t + 1, (t + 1) % NB, 32 * ((t + 1) // NB + 1))
            c_low(t, t % 2)
            c_result(t - 1, (t - 1) % NB, 16 * ((t - 1) // NB + 1))
        c_result(TILES - 1, NB - 1, 16 * (TILES // NB))

    @block.tensor
    def _(pe):
        def conv(u, t):
            pe.wait_ge(S["gray_split"], u + 1)
            if u >= 1:
                pe.wait_ge(S["edge_made"], 2 * u + t - 1)
            for k in range(2):
                dst = ps_conv[t][:, k * SIZE:(k + 1) * SIZE]
                for n, (g, f, dx) in enumerate(three(range(3))):
                    pe.matmul(dst, band[:, g, 3 * k + dx, :], (gray_hi, gray_lo)[f][:, t, dx:dx + SIZE],
                              start=(n == 0), stop=False)
                if t == 0 and k == 0:
                    pe.wait_ge(S["halo_moved"], 16 * 6 * (u + 1))
                last = pe.matmul(dst, halo_w[:, t, k, :], halo_in[:, t, :], start=False, stop=True)
            last.then_inc(S["conv_done"], 1)

        def project(u, w, ps, done):
            for m in range(KD):
                for n, (g, f, k) in enumerate(three(range(KD))):
                    last = pe.matmul(ps[:, m * SIZE:(m + 1) * SIZE], wqkv[w][:, g, k, m * P:(m + 1) * P],
                                     xT_f[:, f, k, :], start=(n == 0), stop=(n == 3 * KD - 1))
            last.then_inc(S[done], 1)

        pe.wait_ge(S["consts_in"], 32)
        pe.wait_ge(S["bands_split"], 1)
        pe.wait_ge(S["halo_made"], 2)
        for s in range(STEPS):
            if live(s - 1):
                u = s - 1
                pe.wait_ge(S["xn1_made"], u + 1)
                if u >= 1:
                    pe.wait_ge(S["xT_split"], u)
                for k in range(KD):
                    for t in range(2):
                        last = pe.transpose(ps_xT[:, k * SIZE + t * P:k * SIZE + (t + 1) * P],
                                            xn1[:, t, k * P:(k + 1) * P], ident)
                last.then_inc(S["xT_done"], 1)
            if live(s):
                conv(s, 0)
            if live(s - 2):
                u = s - 2
                pe.wait_ge(S["probs_made"], 2 * (u + 1))
                if u >= 1:
                    pe.wait_ge(S["h2_made"], 2 * u)
                for t in range(2):
                    last = pe.transpose(ps_pT[:, t * P:(t + 1) * P], probs[:, t], ident)
                last.then_inc(S["pT_done"], 1)
            if live(s - 3):
                u = s - 3
                pe.wait_ge(S["xn2T_made"], u + 1)
                pe.wait_ge(S["masked_made"], min(u + 2, IMAGES))
                for t in range(2):
                    for k in range(KD):
                        last = pe.matmul(ps_gate[:, t * EXPERTS:(t + 1) * EXPERTS], xn2T[:, k, t * P:(t + 1) * P],
                                         wg_sb[:, k, :], start=(k == 0), stop=(k == KD - 1))
                last.then_inc(S["gate_done"], 1)
            if live(s - 2):
                u = s - 2
                pe.wait_ge(S["pT_made"], u + 1)
                pe.wait_ge(S["v_made"], u + 1)
                for t in range(2):
                    last = pe.matmul(ps_pv[:, t * D:(t + 1) * D], probsT[:, t], v_sb[:, t], start=True, stop=True)
                last.then_inc(S["pv_done"], 1)
            if live(s):
                conv(s, 1)
            if live(s - 1):
                u = s - 1
                pe.wait_ge(S["xT_split"], u + 1)
                pe.wait_ge(S["qkv_split"], 3)
                if u >= 3:
                    pe.wait_ge(S["rank_read"], u - 2)
                project(u, 0, ps_q, "q_done")
                if u >= 2:
                    pe.wait_ge(S["xn2T_made"], u - 1)
                project(u, 1, ps_k, "k_done")
                if u >= 1:
                    pe.wait_ge(S["v_made"], u)
                for t in range(2):
                    for n, (g, f, k) in enumerate(three(range(KD))):
                        last = pe.matmul(ps_v[:, t * D:(t + 1) * D], xT_f[:, g, k, t * P:(t + 1) * P],
                                         wqkv[2][:, f, k, :], start=(n == 0), stop=(n == 3 * KD - 1))
                last.then_inc(S["v_done"], 1)
                pe.wait_ge(S["q_made"], KD * (u + 1))
                pe.wait_ge(S["k_made"], KD * (u + 1))
                if u >= 2:
                    pe.wait_ge(S["logit_made"], u - 1)
                for t in range(2):
                    for m in range(KD):
                        last = pe.matmul(ps_s[:, t * P:(t + 1) * P], qT[:, m, t * P:(t + 1) * P],
                                         kT[:, m, t * P:(t + 1) * P], start=(m == 0), stop=(m == KD - 1))
                last.then_inc(S["s_done"], 1)
            if live(s - 3):
                u = s - 3
                pe.wait_ge(S["hits_made"], u + 1)
                pe.wait_ge(S["before_made"], 1)
                pe.matmul(ps_rank[:, 0:2 * EXPERTS], before[:, :], hit[:, :, :].rearrange("p t e -> p (t e)"),
                          start=True, stop=False)
                pe.matmul(ps_rank[:, 0:2 * EXPERTS], ones[:, :], earlier[:, 0:2, :].rearrange("p t e -> p (t e)"),
                          start=False, stop=True).then_inc(S["rank_done"], 1)
            if live(s - 2):
                u = s - 2
                pe.wait_ge(S["xn2_made"], u + 1)
                if live(s - 1):
                    pe.wait_ge(S["k_made"], KD * s)
                for k in range(KD):
                    for t in range(2):
                        last = pe.transpose(ps_xn2T[:, k * SIZE + t * P:k * SIZE + (t + 1) * P],
                                            xn2[:, u % 2, t, k * P:(k + 1) * P], ident)
                last.then_inc(S["xn2T_done"], 1)
        pe.wait_ge(S["rank_read"], IMAGES)
        pe.matmul(ps_rank[:, 0:EXPERTS], ones[:, :], earlier[:, 2, :], start=True, stop=True).then_inc(S["count_done"], 1)

        def e_transpose(j, p, loaded, first=False):
            pe.wait_ge(e_loaded[p], loaded)
            if not first:
                pe.wait_ge(S["e_split"], j - 1)
            for k in range(KD):
                last = pe.transpose(ps_et[p][:, k * P:(k + 1) * P], e_in[:, p, k * P:(k + 1) * P], ident)
            last.then_inc(S["e_T"], 1)

        def weights_of(j):
            return pe.value_load(tab_w[0:1, ds(j, 1)], min_val=0, max_val=(EXPERTS - 1) * WE)

        def e_product(j, p, off, first=False):
            pe.wait_ge(S["e_split"], j + 1)
            for ps, col, done, read in ((ps_b[p], H, "e_b_done", "e_b_made"), (ps_a[p], 0, "e_a_done", "e_a_read")):
                if not first:
                    pe.wait_ge(S[read], j - 1)
                for n, (g, f, k) in enumerate(three(range(KD))):
                    last = pe.matmul(ps[:, :], xT_e[:, p, g, k, :], (w1_hi, w1_lo)[f][:, ds(off + k * 2 * H + col, H)],
                                     start=(n == 0), stop=(n == 3 * KD - 1))
                last.then_inc(S[done], 1)

        pe.wait_ge(S["tables_made"], 1)
        pe.wait_ge(S["w1_lo_made"], CHUNKS)
        e_transpose(0, 0, 16, True)
        e_transpose(1, 1, 16, True)
        e_product(0, 0, weights_of(0), True)
        e_transpose(2, 0, 32)
        e_product(1, 1, weights_of(1), True)
        with pe.Fori(1, MAX_TILES // 2) as i:
            off = [weights_of(2 * i + p) for p in range(2)]
            e_transpose(2 * i + 1, 1, 16 * i + 16)
            e_product(2 * i, 0, off[0])
            e_transpose(2 * i + 2, 0, 16 * i + 32)
            e_product(2 * i + 1, 1, off[1])
        e_product(MAX_TILES - 1, 0, weights_of(MAX_TILES - 1))

        def c_transpose(t, b, p, first=False):
            pe.wait_ge(S["c_sum"], t + 1)
            if not first:
                pe.wait_ge(S["c_split"], t - 1)
            for k in range(KH):
                last = pe.transpose(ps_ct[p][:, k * P:(k + 1) * P], top2[:, b, k * P:(k + 1) * P], ident)
            last.then_inc(S["c_T"], 1)

        def c_product(t, p, first=False):
            pe.wait_ge(S["c_split"], t + 1)
            if not first:
                pe.wait_ge(S["c_out"], t - 1)
            for n, (g, f, k) in enumerate(three(range(KH))):
                last = pe.matmul(ps_y[p][:, 0:D], sumT[p][:, g, k, :], wo_h[:, f, k, :],
                                 start=(n == 0), stop=(n == 3 * KH - 1))
            last.then_inc(S["c_y"], 1)

        pe.wait_ge(S["wo_split"], 1)
        c_transpose(0, 0, 0, True)
        for t in range(NB):
            c_transpose(t + 1, (t + 1) % NB, (t + 1) % 2, t + 1 < 2)
            c_product(t, t % 2, t < 2)
        with pe.Fori(1, TILES // NB - 1) as i:
            for b in range(NB):
                t = NB * i + b
                c_transpose(t + 1, (b + 1) % NB, (b + 1) % 2)
                c_product(t, b % 2)
        for t in range(TILES - NB, TILES):
            if t + 1 < TILES:
                c_transpose(t + 1, (t + 1) % NB, (t + 1) % 2)
            c_product(t, t % 2)


def kernel(x, L0_tok_scharr, L0_attn_Wq, L0_attn_bq, L0_attn_Wk, L0_attn_bk, L0_attn_Wv, L0_attn_bv,
           L0_ffn_Wg, L0_ffn_W1, L0_ffn_b1, L0_ffn_Wo, L0_ffn_bo):
    import numpy as np
    from concourse import bacc, mybir as mb
    from concourse.bass_utils import run_bass_kernel_spmd

    def laid(a, *axes):
        a = np.asarray(a)
        return np.ascontiguousarray(a.transpose(*axes) if axes else a)

    arrays = {
        "x": laid(x), "scharr": laid(L0_tok_scharr),
        "wqT": laid(L0_attn_Wq, 1, 0), "wkT": laid(L0_attn_Wk, 1, 0), "wvT": laid(L0_attn_Wv, 1, 0),
        "bq": laid(L0_attn_bq), "bk": laid(L0_attn_bk), "bv": laid(L0_attn_bv),
        "wgT": laid(L0_ffn_Wg, 1, 0), "w1T": laid(L0_ffn_W1, 2, 0, 1), "b1": laid(L0_ffn_b1),
        "woT": laid(L0_ffn_Wo, 1, 0), "bo": laid(L0_ffn_bo), "consts": shape_constants(), "zeros": np.zeros((P, D), np.float32),
    }
    nc = bacc.Bacc("TRN2", target_bir_lowering=False, num_devices=1)
    aps = {n: nc.dram_tensor(n, a.shape, mb.dt.from_np(a.dtype), kind="ExternalInput").ap() for n, a in arrays.items()}
    out = nc.dram_tensor("out", (TILES * P, D), mb.dt.float32, kind="ExternalOutput").ap()
    build(nc, out=out, **aps)
    r = run_bass_kernel_spmd(nc, [arrays], core_ids=[0])
    return r.results[0]["out"].reshape(IMAGES, SIZE, D)
```

```python
from contextlib import ExitStack

import concourse.bass as bass
from concourse import mybir

F32 = mybir.dt.float32
F32R = mybir.dt.float32r
BF16 = mybir.dt.bfloat16
I32 = mybir.dt.int32
U32 = mybir.dt.uint32
ALU = mybir.AluOpType
ACT = mybir.ActivationFunctionType
AX = mybir.AxisListType

P = 128
IMAGES, CHANNELS, SIZE = 8, 3, 256
D = 256
KD = D // P
TILES_IN_IMAGE = SIZE // P
TILES = IMAGES * TILES_IN_IMAGE
HEAD = SIZE // 16
EXPERTS, TOP = 8, 2
H = 512
KH = H // P
REGION = IMAGES * SIZE + P
MAX_TILES = (IMAGES * SIZE * TOP + EXPERTS * (P - 1)) // P
LEAST_TILES = IMAGES * SIZE * TOP // P
ROWS = (EXPERTS + 1) * REGION
EPS_LN, EPS_TOP = 1e-5, 1e-9
GRAY = (0.2989, 0.587, 0.114)
NEVER = -3.0e38

C_ID, C_MASK, C_IOTA, C_BASE, C_SEL, C_TILE = 0, 128, 256, 264, 272, 274
C_UP = C_TILE + MAX_TILES
C_DOWN, C_BEFORE = C_UP + P, C_UP + 2 * P
C_ALL = C_UP + 3 * P


def shape_constants():
    import numpy as np
    c = np.zeros((P, C_ALL), np.float32)
    r = np.arange(P)
    c[:, C_ID:C_ID + P] = np.eye(P)
    c[:, C_UP:C_UP + P] = r[:, None] == r[None, :] - 1
    c[:, C_DOWN:C_DOWN + P] = r[:, None] == r[None, :] + 1
    c[:, C_MASK:C_MASK + P] = np.where(r[:, None] // HEAD == r[None, :] // HEAD, 0.0, NEVER)
    c[:, C_BEFORE:C_BEFORE + P] = r[:, None] < r[None, :]
    c[:, C_IOTA:C_IOTA + EXPERTS] = np.arange(EXPERTS)
    c[:, C_BASE:C_BASE + EXPERTS] = np.arange(EXPERTS) * REGION
    c[:9, C_SEL] = [1, 1, 1, 0, 0, 0, 1, 1, 1]
    c[:9, C_SEL + 1] = [0, 0, 0, 1, 1, 1, 0, 0, 0]
    c[:, C_TILE:C_TILE + MAX_TILES] = np.arange(MAX_TILES)
    return c


def build(nc, x, scharr, wqT, wkT, wvT, bq, bk, bv, wgT, w1T, b1, woT, bo, consts, zeros, out):
    ctx = ExitStack()
    with ctx:
        _build(nc, ctx, x, scharr, wqT, wkT, wvT, bq, bk, bv, wgT, w1T, b1, woT, bo, consts, zeros, out)


def _build(nc, ctx, x, scharr, wqT, wkT, wvT, bq, bk, bv, wgT, w1T, b1, woT, bo, consts, zeros, out):
    ds = bass.ds

    def sb(name, shape, dt=F32):
        return ctx.enter_context(nc.sbuf_tensor(name, shape, dt))

    def overlaid(whole, *parts):
        with nc.sbuf_tensor(whole[0], [P, whole[1]], whole[2]) as tensor:
            pass
        tensors = [sb(name, [P, words], dt) for name, words, dt in parts]
        rest = whole[1] - sum(words for _, words, _ in parts)
        sb(f"{whole[0]}_rest", [P, rest])
        return tensor, *tensors

    def sem(name):
        return ctx.enter_context(nc.semaphore(name))

    rows_in = nc.dram_tensor("rows_in", (ROWS, D), F32, kind="Internal").ap()
    rows_gated = nc.dram_tensor("rows_gated", (2 * MAX_TILES * P, H), F32, kind="Internal").ap()
    resid = nc.dram_tensor("resid", (TILES * P, D), F32, kind="Internal").ap()

    WE = KD * 2 * H
    LAST = (EXPERTS - 1) * WE
    NB = 4
    w1_hi, res_in, top1 = overlaid(("w1_hi", EXPERTS * WE, F32R), ("res_in", TILES * D, F32), ("top1", TILES * H, F32))
    w1_lo, top2, result_all, weighed_all = overlaid(
        ("w1_lo", EXPERTS * WE, F32R), ("top2", TILES * H, F32), ("result", NB * D, F32), ("weighed", NB * H, F32))
    RES_EXPERTS = -(-TILES * D // WE)
    assert TILES * (H + D) <= LAST and TILES * H + NB * (H + D) <= LAST
    result = result_all[:, :].rearrange("p (b d) -> p b d", b=NB)
    weighed = weighed_all[:, :].rearrange("p (b h) -> p b h", b=NB)
    GW = SIZE + 2
    gray_hi = w1_lo[:, LAST:LAST + 2 * GW].rearrange("p (t c) -> p t c", t=2)
    gray_lo = w1_lo[:, LAST + 2 * GW:LAST + 4 * GW].rearrange("p (t c) -> p t c", t=2)
    halo_in = w1_lo[0:9, LAST + 4 * GW:LAST + 4 * GW + 2 * SIZE].rearrange("p (t c) -> p t c", t=2)
    halo_w = w1_hi[0:9, LAST:LAST + 4 * P].rearrange("p (t k o) -> p t k o", t=2, k=2)
    front_w, _, late_1 = overlaid(("front_w", 6 * 2 * P + 2 * 2 * KD * D, F32R), ("below", 2 * KH * D, F32R), ("late_1", 2 * H, F32))
    band = front_w[:, 0:12 * P].rearrange("p (g q o) -> p g q o", g=2, q=6)
    wqk = front_w[:, 12 * P:].rearrange("p (w g k e) -> p w g k e", w=2, g=2, k=KD)
    wv = w1_hi[:, LAST + 4 * P:LAST + 4 * P + 2 * KD * D].rearrange("p (g k e) -> p g k e", g=2, k=KD)
    wqkv = [wqk[:, 0], wqk[:, 1], wv]
    wo_h = front_w[:, 0:2 * KH * D].rearrange("p (g k e) -> p g k e", g=2, k=KH)
    NS = 3
    shared = sb("shared", [P, EXPERTS * 2 * H])
    xs_img = shared[:, 0:3072].rearrange("p (b c t w) -> p b c t w", b=2, c=3, t=2)
    gray = shared[:, 3072:3584].rearrange("p (t w) -> p t w", t=2)
    xn1 = shared[:, 3584:4096].rearrange("p (t w) -> p t w", t=2)
    stage = shared[:, 4096:7168].rearrange("p (b w) -> p b w", b=NS)
    stage_qkv = shared[:, 6656:8192].rearrange("p (w k e) -> p w k e", w=3, k=KD)
    edge = shared[:, 7168:8192].rearrange("p (t k w) -> p t k w", t=2, k=2)
    b1_all = shared[:, :]
    work = sb("work", [P, 5888])
    h_all = work[:, 0:2048].rearrange("p (b t w) -> p b t w", b=4, t=2)
    xn2 = work[:, 2048:3072].rearrange("p (b t w) -> p b t w", b=2, t=2)
    xn2T = work[:, 3072:3584].rearrange("p (k n) -> p k n", k=KD)
    qT = work[:, 3584:4096].rearrange("p (k n) -> p k n", k=KD)
    kT = work[:, 4096:4608].rearrange("p (k n) -> p k n", k=KD)
    v_sb = work[:, 4608:5120].rearrange("p (t w) -> p t w", t=2)
    masked = work[:, 5120:5376].rearrange("p (t w) -> p t w", t=2)
    probs = work[:, 5376:5632].rearrange("p (t w) -> p t w", t=2)
    probsT = work[:, 5632:5888].rearrange("p (t w) -> p t w", t=2)
    band_raw = work[:, 2048:2048 + 6 * P].rearrange("p (q o) -> p q o", q=6)
    late = (work[:, 4608:4608 + 2 * H], late_1[:, :])
    early = work[:, 2816:2816 + 3 * P]
    wo_raw = work[:, 4608:4608 + KH * D].rearrange("p (k e) -> p k e", k=KH)
    e_in = work[:, 0:2 * D].rearrange("p (b d) -> p b d", b=2)
    e_b = work[:, 512:512 + 2 * H].rearrange("p (b h) -> p b h", b=2)
    e_sig = work[:, 1536:1536 + 2 * H].rearrange("p (b h) -> p b h", b=2)
    e_a = work[:, 2560:2560 + 2 * H].rearrange("p (b h) -> p b h", b=2)
    e_out = work[:, 3584:3584 + 2 * H].rearrange("p (b h) -> p b h", b=2)
    xT = sb("xT", [P, 2 * KD * SIZE], F32R)
    xT_f = xT[:, :].rearrange("p (g k n) -> p g k n", g=2, k=KD)
    xT_e = xT[:, :].rearrange("p (b g k n) -> p b g k n", b=2, g=2, k=KD)

    sumT = [a.rearrange("p (g k t) -> p g k t", g=2, k=KH) for a in (front_w[:, 2 * KH * D:2 * KH * D + 2 * H], xT[:, :])]
    cst = sb("cst", [P, C_UP])
    ident = cst[:, C_ID:C_ID + P]
    before = sb("before", [P, P], BF16)
    ones = sb("ones", [P, P], BF16)
    bv_all = sb("bv_all", [P, D])
    bo_all = sb("bo_all", [P, D])
    bqk = sb("bqk", [P, 2 * KD])
    wg_sb = sb("wg_sb", [P, KD, EXPERTS])
    taps = sb("taps", [P, 18])
    htap = sb("htap", [9, 4, 6])
    htap_r = sb("htap_r", [9, 6], F32R)
    stats = sb("stats", [P, 2, 2, 6])
    mv = sb("mv", [P, 2, 2, 2])
    vare = sb("vare", [P, 2, 2])
    rstd = sb("rstd", [P, 2, 2])
    neg_half = sb("neg_half", [P, 2])
    smax = sb("smax", [P, 2])
    nsmax = sb("nsmax", [P, 2])
    ssum = sb("ssum", [P, 2])
    srec = sb("srec", [P, 2])
    gmax = sb("gmax", [P, 2])
    logit = sb("logit", [P, 2, EXPERTS])
    gexp = sb("gexp", [P, 2, EXPERTS])
    gsum = sb("gsum", [P, 2])
    grec = sb("grec", [P, 2])
    gprob = sb("gprob", [P, 2, EXPERTS])
    best = sb("best", [P, 2, 8])
    best_at = sb("best_at", [P, 2, 8], U32)
    best_f = sb("best_f", [P, 2, TOP])
    chosen_all = sb("chosen_all", [P, TILES, TOP, EXPERTS], BF16)
    hit = sb("hit", [P, 2, EXPERTS], BF16)
    earlier = sb("earlier", [P, 3, EXPERTS], BF16)
    den = sb("den", [P, 2])
    weight = sb("weight", [P, TILES * TOP])
    wsum = sb("wsum", [P, 2])
    place = sb("place", [P, 2, EXPERTS])
    placed = sb("placed", [P, 2, TOP, EXPERTS])
    place_f = sb("place_f", [P, 2, TOP])
    place_i = sb("place_i", [P, TILES, TOP], I32)
    gated_i = sb("gated_i", [P, TILES, TOP], I32)
    tiles_i = sb("tiles_i", [P, 2, EXPERTS], I32)
    tiles_f = sb("tiles_f", [P, EXPERTS])
    one8 = sb("one8", [P, EXPERTS])
    ends = sb("ends", [P, EXPERTS])
    shift = sb("shift", [P, EXPERTS])
    shifts = work[:, 4328:4328 + TILES * TOP * EXPERTS].rearrange("p (n e) -> p n e", e=EXPERTS)
    shift_of = work[:, 4296:4328]
    passed, passed_n = (work[0:1, 3072 + n * 512:3072 + n * 512 + MAX_TILES * EXPERTS].rearrange("p (j e) -> p j e", e=EXPERTS)
                        for n in range(2))
    expert_of, start_of, tiles_in, rows_before, need = (work[0:1, 4096 + n * 40:4096 + n * 40 + MAX_TILES] for n in range(5))
    tab_row = sb("tab_row", [1, MAX_TILES], I32)
    tab_w = sb("tab_w", [1, MAX_TILES], I32)
    tab_b = sb("tab_b", [1, MAX_TILES], I32)
    tab_pad = sb("tab_pad", [1, 3], I32)
    of_later = work[0:1, 5680:5683]
    tab_out = work[0:1, 5632:5632 + MAX_TILES].bitcast(I32)
    real_i, real_at = (work[0:1, 5672 + n * 2:5674 + n * 2].bitcast(I32) for n in range(2))
    res_free_at = work[0:1, 5684:5685].bitcast(I32)
    pad_f = sb("pad_f", [1, EXPERTS])
    pad_i = sb("pad_i", [1, EXPERTS], I32)

    bank = [ctx.enter_context(nc.psum_tensor(f"bank{i}", [P, 512], F32)) for i in range(8)]
    ps_conv = bank[0:2]
    ps_xT, ps_q, ps_k, ps_v, ps_s, ps_pv = bank[2:8]
    ps_rank, ps_xn2T, ps_gate, ps_pT = ps_q, ps_k, ps_s, ps_pv
    ps_count = ps_v[:, 0:EXPERTS]
    ps_et = bank[0:2]
    ps_a, ps_b = bank[2:4], bank[4:6]
    ps_ct = bank[6:8]
    ps_y = bank[0:2]

    S = {n: sem(n) for n in (
        "consts_in taps_in halo_taps_in qkv_in small_in regions_zeroed pads_set bf_set "
        "before_made bands_made bands_split halo_made qkv_hi qkv_split band_hi "
        "gray_first gray_made gray_hi_made gray_split conv_done edge_made h_made "
        "mv1_made rstd1_made xn1_made xT_done xT_hi_made xT_split q_done k_done v_done q_made k_made v_made "
        "s_done masked_made probs_made pT_done pT_made pv_done srec_made h2_made mv2_made rstd2_made xn2_made "
        "xn2T_done xn2T_made gate_done logit_made gexp_made hits_made rank_done rank_read places_made "
        "res_made gated_places_made out_rows_made count_done tables_made b1_in wo_in wo_hi wo_split w1_hi_made w1_lo_made "
        "e_T e_hi e_split e_b_done e_a_done e_b_made e_sig_made e_a_read e_out_made "
        "c_res c_first c_sum c_T c_hi c_split c_y c_out dve_step pool_step").split()}
    padded = [sem(f"padded{i}") for i in range(2)]
    x_in = [sem(f"x_in{i}") for i in range(2)]
    late_in = [sem(f"late_in{i}") for i in range(2)]
    halo_moved = [sem(f"halo_moved{i}") for i in range(2)]
    stage_in = [sem(f"stage_in{i}") for i in range(NS)]
    scattered = [sem(f"scattered{i}") for i in range(2)]
    res_stored = [sem(f"res_stored{i}") for i in range(4)]
    e_loaded = [sem(f"e_loaded{i}") for i in range(2)]
    e_stored = [sem(f"e_stored{i}") for i in range(2)]
    c_loaded = [[sem(f"c_loaded{k}_{i}") for i in range(NB)] for k in range(TOP)]
    c_stored = [sem(f"c_stored{i}") for i in range(NB)]

    block = ctx.enter_context(nc.Block())

    STEPS = IMAGES + 3
    CHUNKS = EXPERTS * KD
    BY_POOL = IMAGES + 3
    EARLY = IMAGES

    def live(u):
        return 0 <= u < IMAGES

    def three(k_range):
        return [(g, f, k) for k in k_range for g, f in ((0, 0), (0, 1), (1, 0))]

    def w1_chunk(c):
        return w1T[(c % KD) * P:(c % KD + 1) * P, c // KD, :]

    zero_rows = zeros[0:P * D // H, :].rearrange("a (b d) -> (a b) d", d=D)

    def zero_behind(queue, e):
        r = queue.value_load(pad_i[0:1, e:e + 1], min_val=0, max_val=ROWS - P)
        queue.dma_start(rows_in[ds(r, P), :], zero_rows).then_inc(padded[e // (EXPERTS // 2)], 16)

    def row_of(queue, j):
        return queue.value_load(tab_row[0:1, ds(j, 1)], min_val=0, max_val=ROWS - P)

    def load_rows(queue, r, p):
        queue.dma_start(e_in[:, p, :], rows_in[ds(r, P), :]).then_inc(e_loaded[p], 16)

    def first_rows(queue, j):
        queue.wait_ge(S["tables_made"], 1)
        r = row_of(queue, j)
        pads = queue.value_load(tab_pad[0:1, j:j + 1], min_val=1, max_val=16 * EXPERTS // 2 + 1)
        queue.wait_ge(S["regions_zeroed"], 16 * 2 * (MAX_TILES - LEAST_TILES))
        for n in range(3):
            queue.wait_ge(res_stored[n], 16 * IMAGES // 4)
        queue.wait_ge(padded[0], 16 * EXPERTS // 2)
        for n in range(2):
            queue.wait_ge(scattered[n], 16 * 4 * IMAGES // 2)
        queue.wait_ge(padded[1], pads)
        load_rows(queue, r, j)

    def weight_of(t, k):
        return weight[:, ds(TOP * t + k, 1)]

    @block.sync
    def _(sp):
        def load_image(u):
            if u >= 2:
                sp.wait_ge(S["gray_made"], u - 1)
            sp.dma_start(xs_img[:, u % 2], x[u].rearrange("c (t p) w -> p c t w", p=P)).then_inc(x_in[u % 2], 16)

        sp.dma_start(cst[:, :], consts[:, 0:C_UP]).then_inc(S["consts_in"], 16)
        sp.dma_start(early, consts[:, C_UP:C_ALL]).then_inc(S["consts_in"], 16)
        load_image(0)
        sp.dma_start(stage_qkv[:, 0], wqT.rearrange("(k p) e -> p k e", p=P)).then_inc(S["qkv_in"], 16)
        sp.dma_start(stage_qkv[:, 1], wkT.rearrange("(k p) e -> p k e", p=P)).then_inc(S["qkv_in"], 16)
        sp.dma_start(stage_qkv[:, 2], wvT.rearrange("(k p) e -> p k e", p=P)).then_inc(S["qkv_in"], 16)
        load_image(1)
        def zero_region(n):
            r = EXPERTS * REGION + n * P
            sp.dma_start(rows_in[r:r + P, :], zero_rows).then_inc(S["regions_zeroed"], 16)
            r = (LEAST_TILES + n) * P
            sp.dma_start(rows_gated[r:r + P, :], zeros).then_inc(S["regions_zeroed"], 16)

        def load_b1(experts):
            for e in experts:
                sp.dma_start(b1_all[:, e * 2 * H:(e + 1) * 2 * H], b1[e].partition_broadcast(P)).then_inc(S["b1_in"], 16)

        def load_chunk(c):
            if c == 2:
                sp.wait_ge(S["qkv_split"], 3)
            if c >= NS:
                sp.wait_ge(S["w1_lo_made"], c - NS + 1)
            sp.dma_start(stage[:, c % NS, :], w1_chunk(c)).then_inc(stage_in[c % NS], 16)

        def halo(u):
            sp.wait_ge(S["gray_split"], u + 1)
            if u >= 1:
                sp.wait_ge(S["conv_done"], 2 * u)
            for t, row in ((0, 0), (1, P - 1)):
                for half, parts in ((gray_hi, (0, 3)), (gray_lo, (6,))):
                    src = half[row:row + 1, 1 - t, 0:SIZE]
                    wide = bass.AP(tensor=src.tensor, offset=src.offset, ap=[list(src.ap[0]), [1, 3], [1, SIZE]]).bitcast(F32)
                    for p0 in parts:
                        sp.dma_start(halo_in[p0:p0 + 3, t, :].bitcast(F32), wide).then_inc(halo_moved[t], 16)

        halo(0)
        load_chunk(0)
        load_chunk(1)
        for s in range(STEPS):
            if live(s - 4):
                u = s - 4
                sp.wait_ge(S["res_made"], 2 * (u + 1))
                sp.dma_start(resid[u * SIZE:(u + 1) * SIZE, :].rearrange("(t p) w -> p t w", p=P),
                             h_all[:, u % 4]).then_inc(res_stored[u % 4], 16)
            if live(s + 2):
                load_image(s + 2)
            if live(s + 1):
                halo(s + 1)
            if s + 2 < EARLY:
                load_chunk(s + 2)
            if 1 <= s <= MAX_TILES - LEAST_TILES:
                zero_region(s - 1)
            if s == IMAGES:
                sp.wait_ge(S["xT_done"], IMAGES)
                sp.wait_ge(S["h_made"], 2 * IMAGES)
                sp.wait_ge(S["w1_lo_made"], EARLY)
            if s in (IMAGES, IMAGES + 1):
                sp.wait_ge(scattered[s % 2], 64 * ((s - 4) // 2 + 1))
                load_b1(range(0, EXPERTS // 2) if s == IMAGES else range(EXPERTS // 2, EXPERTS))
        sp.wait_ge(S["pads_set"], 1)
        for e in range(0, EXPERTS, 2):
            zero_behind(sp, e)
        u = IMAGES - 1
        sp.wait_ge(S["res_made"], 2 * (u + 1))
        sp.dma_start(resid[u * SIZE:(u + 1) * SIZE, :].rearrange("(t p) w -> p t w", p=P),
                             h_all[:, u % 4]).then_inc(res_stored[u % 4], 16)
        first_rows(sp, 0)
        def store_rows(j, p):
            r = sp.value_load(tab_out[0:1, ds(j, 1)], min_val=0, max_val=(2 * MAX_TILES - 1) * P)
            sp.wait_ge(S["e_out_made"], j + 1)
            sp.dma_start(rows_gated[ds(r, P), :], e_out[:, p, :]).then_inc(e_stored[p], 16)

        sp.wait_ge(padded[1], 16 * EXPERTS // 2 + 1)
        AHEAD = 4

        def load_next(j, p):
            r = row_of(sp, j)
            sp.wait_ge(S["e_T"], j - 1)
            load_rows(sp, r, p)

        for j in range(2, AHEAD):
            load_next(j, j % 2)
        sp.wait_ge(S["out_rows_made"], 1)
        LOOPED = (MAX_TILES - AHEAD) // 2
        WO_AT = 2 * LOOPED // 3
        for start, end in ((0, WO_AT), (WO_AT, LOOPED)):
            with sp.Fori(start, end) as i:
                for p in range(2):
                    load_next(2 * i + p + AHEAD, p)
                    store_rows(2 * i + p, p)
            if start == 0:
                sp.wait_ge(S["w1_lo_made"], CHUNKS)
                sp.dma_start(wo_raw, woT.rearrange("(k p) e -> p k e", p=P)).then_inc(S["wo_in"], 16)
        for j in range(2 * LOOPED, MAX_TILES):
            if j + AHEAD < MAX_TILES:
                load_next(j + AHEAD, j % 2)
            store_rows(j, j % 2)

        def store_results(q):
            for b in range(NB):
                t = NB * q + b
                sp.wait_ge(S["c_out"], t + 1)
                sp.dma_start(out[ds(t * P, P), :], result[:, b, :]).then_inc(c_stored[b], 16)

        with sp.Fori(0, TILES // NB) as q:
            store_results(q)
        for b in range(NB):
            sp.wait_ge(c_stored[b], 16 * TILES // NB)

    @block.scalar
    def _(act):
        act.dma_start(taps[:, :], scharr.rearrange("k o a b -> (k o a b)").partition_broadcast(P)).then_inc(S["taps_in"], 16)
        for c in range(3):
            with nc.allow_non_contiguous_dma(reason="18 values"):
                act.dma_start(htap[3 * c:3 * c + 3, 0, :], scharr.rearrange("k o a b -> b (k o a)")).then_inc(S["halo_taps_in"], 16)

        def gray_first(u):
            act.wait_ge(x_in[u % 2], 16 * (u // 2 + 1))
            if u >= 1:
                act.wait_ge(S["gray_split"], u)
            act.activation(gray, xs_img[:, u % 2, 0], ACT.Copy, scale=GRAY[0]).then_inc(S["gray_first"], 1)

        def gray_high(u):
            act.wait_ge(S["gray_made"], u + 1)
            if u >= 1:
                act.wait_ge(S["conv_done"], 2 * u)
            act.activation(gray_hi[:, :, 1:1 + SIZE], gray, ACT.Copy).then_inc(S["gray_hi_made"], 1)

        def edges(u, t):
            act.wait_ge(S["conv_done"], 2 * u + t + 1)
            if u >= 1:
                act.wait_ge(S["h_made"], 2 * u + t - 1)
            else:
                act.wait_ge(S["qkv_split"], 3)
            act.activation(edge[:, t], ps_conv[t][:, :].rearrange("p (k w) -> p k w", k=2), ACT.Abs).then_inc(S["edge_made"], 1)

        def split_high(c, staged, ready, loads):
            act.wait_ge(ready, loads)
            act.activation(w1_hi[:, c * 2 * H:(c + 1) * 2 * H], staged, ACT.Copy).then_inc(S["w1_hi_made"], 1)

        def split_late(c):
            split_high(c, late[(c - EARLY) % 2], late_in[(c - EARLY) % 2], 16 * ((c - EARLY) // 2 + 1))

        gray_first(0)
        act.wait_ge(S["bands_made"], 6)
        act.activation(band[:, 0], band_raw, ACT.Copy).then_inc(S["band_hi"], 1)
        gray_high(0)
        act.dma_start(bv_all[:, :], bv.partition_broadcast(P)).then_inc(S["small_in"], 16)
        act.dma_start(bo_all[:, :], bo.partition_broadcast(P)).then_inc(S["small_in"], 16)
        with nc.allow_non_contiguous_dma(reason="256 values each"):
            act.dma_start(bqk[:, 0:KD], bq.rearrange("(k p) -> p k", p=P)).then_inc(S["small_in"], 16)
            act.dma_start(bqk[:, KD:2 * KD], bk.rearrange("(k p) -> p k", p=P)).then_inc(S["small_in"], 16)
            act.dma_start(wg_sb[:, :, :], wgT.rearrange("(k p) e -> p k e", p=P)).then_inc(S["small_in"], 16)
        act.wait_ge(S["qkv_in"], 48)
        for w in range(3):
            act.activation(wqkv[w][:, 0], stage_qkv[:, w], ACT.Copy).then_inc(S["qkv_hi"], 1)

        for s in range(STEPS):
            if live(s + 1):
                gray_first(s + 1)
            if live(s - 1):
                u = s - 1
                act.wait_ge(S["xT_done"], u + 1)
                if u >= 1:
                    act.wait_ge(S["v_done"], u)
                act.activation(xT_f[:, 0], ps_xT[:, :].rearrange("p (k n) -> p k n", k=KD), ACT.Copy)\
                   .then_inc(S["xT_hi_made"], 1)
            if live(s - 2):
                u = s - 2
                act.wait_ge(S["pT_done"], u + 1)
                if u >= 1:
                    act.wait_ge(S["pv_done"], u)
                act.activation(probsT, ps_pT[:, 0:2 * P].rearrange("p (t n) -> p t n", t=2), ACT.Copy)\
                   .then_inc(S["pT_made"], 1)
            if live(s):
                edges(s, 0)
            if live(s):
                edges(s, 1)
            if live(s + 1):
                gray_high(s + 1)
            if live(s - 3):
                u = s - 3
                act.wait_ge(S["logit_made"], u + 1)
                act.activation(gexp[:, :, :], logit[:, :, :], ACT.Exp).then_inc(S["gexp_made"], 1)
            if s == STEPS - 1:
                split_late(EARLY)
                split_late(EARLY + 1)
            if s < EARLY:
                split_high(s, stage[:, s % NS, :], stage_in[s % NS], 16 * (s // NS + 1))
            if live(s - 1):
                u = s - 1
                act.wait_ge(S["small_in"], 80)
                for n, (done, made, ps, dst) in enumerate((("q_done", "q_made", ps_q, qT), ("k_done", "k_made", ps_k, kT))):
                    act.wait_ge(S[done], u + 1)
                    if u >= 1:
                        act.wait_ge(S["s_done"], u)
                    for m in range(KD):
                        act.activation(dst[:, m], ps[:, m * SIZE:(m + 1) * SIZE], ACT.Identity,
                                       bias=bqk[:, n * KD + m:n * KD + m + 1]).then_inc(S[made], 1)
            if live(s - 1):
                u = s - 1
                act.wait_ge(S["masked_made"], u + 1)
                if u >= 1:
                    act.wait_ge(S["pT_done"], u)
                    act.wait_ge(S["srec_made"], u)
                for t in range(2):
                    act.activation(probs[:, t], masked[:, t], ACT.Exp, bias=nsmax[:, t:t + 1],
                                   accum_out=ssum[:, t:t + 1]).then_inc(S["probs_made"], 1)
            if live(s - 2):
                u = s - 2
                act.wait_ge(S["xn2T_done"], u + 1)
                if u >= 1:
                    act.wait_ge(S["gate_done"], u)
                act.activation(xn2T, ps_xn2T[:, :].rearrange("p (k n) -> p k n", k=KD), ACT.Copy)\
                   .then_inc(S["xn2T_made"], 1)

        act.wait_ge(S["pads_set"], 1)
        for e in range(1, EXPERTS, 2):
            zero_behind(act, e)
        first_rows(act, 1)
        act.wait_ge(S["srec_made"], IMAGES)
        act.activation(ssum[:, :], nsmax[:, :], ACT.Sigmoid)

        def e_high(j, p, first=False):
            act.wait_ge(S["e_T"], j + 1)
            if not first:
                act.wait_ge(S["e_a_done"], j - 1)
            act.activation(xT_e[:, p, 0], ps_et[p][:, 0:KD * P].rearrange("p (k n) -> p k n", k=KD), ACT.Copy)\
               .then_inc(S["e_hi"], 1)

        def e_sigmoid(j, p, first=False):
            act.wait_ge(S["e_b_made"], j + 1)
            if not first:
                act.wait_ge(S["e_out_made"], j - 1)
            act.activation(e_sig[:, p], e_b[:, p], ACT.Sigmoid).then_inc(S["e_sig_made"], 1)

        e_high(0, 0, True)
        e_high(1, 1, True)
        for c in range(EARLY + 2, BY_POOL):
            split_late(c)
        act.wait_ge(res_stored[3], 16 * IMAGES // 4)
        e_sigmoid(0, 0, True)
        e_high(2, 0)
        e_sigmoid(1, 1, True)
        def two_tiles(i):
            e_high(2 * i + 1, 1)
            e_sigmoid(2 * i, 0)
            e_high(2 * i + 2, 0)
            e_sigmoid(2 * i + 1, 1)

        with act.Fori(1, MAX_TILES // 2 - 1) as i:
            two_tiles(i)
        act.wait_ge(S["wo_in"], 16)
        act.activation(wo_h[:, 0], wo_raw, ACT.Copy).then_inc(S["wo_hi"], 1)
        two_tiles(MAX_TILES // 2 - 1)
        e_sigmoid(MAX_TILES - 1, 0)

        def c_high(t, p, first=False):
            act.wait_ge(S["c_T"], t + 1)
            if not first:
                act.wait_ge(S["c_y"], t - 1)
            act.activation(sumT[p][:, 0], ps_ct[p][:, :].rearrange("p (k n) -> p k n", k=KH), ACT.Copy)\
               .then_inc(S["c_hi"], 1)

        def c_first(t, b, at16):
            act.wait_ge(c_loaded[0][b], at16)
            act.activation(top1[:, ds(t * H, H)], top1[:, ds(t * H, H)], ACT.Copy, scale=weight_of(t, 0)).then_inc(S["c_first"], 1)

        c_first(0, 0, 16)
        for t in range(NB):
            c_first(t + 1, (t + 1) % NB, 16 * ((t + 1) // NB + 1))
            c_high(t, t % 2, t < 2)
        with act.Fori(1, TILES // NB - 1) as i:
            for b in range(NB):
                t = NB * i + b
                c_first(t + 1, (b + 1) % NB, 16 * i + 16 * ((b + 1) // NB + 1))
                c_high(t, b % 2)
        for t in range(TILES - NB, TILES):
            if t + 1 < TILES:
                c_first(t + 1, (t + 1) % NB, 16 * ((t + 1) // NB + 1))
            c_high(t, t % 2)


    @block.gpsimd
    def _(pool):
        def split_low(c, staged):
            pool.wait_ge(S["w1_hi_made"], c + 1)
            cols = slice(c * 2 * H, (c + 1) * 2 * H)
            pool.tensor_tensor(w1_lo[:, cols], staged, w1_hi[:, cols].bitcast(F32), ALU.subtract)\
                .then_inc(S["w1_lo_made"], 1)

        steps = 0

        def inverse_deviation(norm, u, moments, made):
            nonlocal steps
            pool.wait_ge(S[moments], u + 1)
            pool.tensor_scalar(vare[:, norm], mv[:, norm, :, 1], EPS_LN, None, ALU.add).then_inc(S["pool_step"], 1)
            steps += 1
            pool.wait_ge(S["pool_step"], steps)
            pool.tensor_tensor(rstd[:, norm], vare[:, norm], neg_half[:, :], ALU.pow).then_inc(S[made], 1)

        pool.memset(neg_half[:, :], -0.5).then_inc(S["pool_step"], 1)
        steps += 1
        pool.wait_ge(S["pool_step"], steps)

        def scatter(u):
            pool.wait_ge(S["places_made"], u + 1)
            for t in range(2):
                for k in range(TOP):
                    pool.indirect_dma_start(
                        rows_in, bass.IndirectOffsetOnAxis(ap=place_i[:, 2 * u + t, k:k + 1], axis=0),
                        xn2[:, u % 2, t, :], None).then_inc(scattered[u % 2], 16)

        def load_late(c):
            pool.dma_start(late[(c - EARLY) % 2], w1_chunk(c)).then_inc(late_in[(c - EARLY) % 2], 16)

        for s in range(STEPS):
            if live(s - 4) and live(s - 1):
                scatter(s - 4)
            if live(s - 2):
                inverse_deviation(1, s - 2, "mv2_made", "rstd2_made")
            if s == IMAGES + 1:
                pool.wait_ge(S["pv_done"], IMAGES)
                pool.wait_ge(S["v_done"], IMAGES)
                load_late(EARLY)
                load_late(EARLY + 1)
            if live(s - 3) and not live(s):
                scatter(s - 3)
            if live(s):
                inverse_deviation(0, s, "mv1_made", "rstd1_made")
            if s < EARLY:
                split_low(s, stage[:, s % NS, :])

        for c in range(EARLY, CHUNKS):
            staged = late[(c - EARLY) % 2]
            if c >= BY_POOL:
                pool.wait_ge(late_in[(c - EARLY) % 2], 16 * ((c - EARLY) // 2 + 1))
                pool.tensor_copy(w1_hi[:, c * 2 * H:(c + 1) * 2 * H], staged).then_inc(S["w1_hi_made"], 1)
            split_low(c, staged)
            if c + 2 < CHUNKS:
                pool.wait_ge(S["w1_lo_made"], c + 1)
                if c == EARLY:
                    for p in range(2):
                        pool.wait_ge(e_loaded[p], 16)
                load_late(c + 2)

        pool.wait_ge(S["gated_places_made"], 1)
        freed = pool.value_load(res_free_at[0:1, :], min_val=1, max_val=MAX_TILES)
        for n in range(4):
            pool.wait_ge(res_stored[n], 16 * IMAGES // 4)
        pool.wait_ge(S["e_a_done"], freed)
        pool.tensor_tensor(rstd[:, 0], neg_half[:, :], neg_half[:, :], ALU.add)
        for t in range(TILES):
            pool.dma_start(res_in[:, t * D:(t + 1) * D], resid[t * P:(t + 1) * P, :]).then_inc(S["c_res"], 16)

        counts = [pool.value_load(real_at[0:1, p:p + 1], min_val=16 * (LEAST_TILES // 2), max_val=16 * (MAX_TILES + 1) // 2)
                  for p in range(2)]
        for p in range(2):
            pool.wait_ge(e_stored[p], counts[p])
            pool.tensor_tensor(vare[:, p], neg_half[:, :], neg_half[:, :], ALU.add)

        for t in range(TILES):
            if t >= NB:
                for k in range(TOP):
                    pool.wait_ge(c_loaded[k][t % NB], 16 * (t // NB))
            for k, rows in enumerate((top1, top2)):
                pool.indirect_dma_start(
                    rows[:, t * H:(t + 1) * H], None, rows_gated[0:MAX_TILES * P, :],
                    bass.IndirectOffsetOnAxis(ap=gated_i[:, t, k:k + 1], axis=0)).then_inc(c_loaded[k][t % NB], 16)

    @block.vector
    def _(dve):
        steps = 0

        def mark(ins):
            nonlocal steps
            steps += 1
            ins.then_inc(S["dve_step"], 1)

        def settle():
            dve.wait_ge(S["dve_step"], steps)

        def step(ins):
            mark(ins)
            settle()

        for half in (gray_hi, gray_lo):
            for col in (0, GW - 1):
                dve.memset(half[:, :, col:col + 1].bitcast(F32), 0.0)
        dve.memset(ones[:, :], 1.0).then_inc(padded[1], 1)
        dve.memset(one8[:, :], 1.0)
        dve.memset(earlier[:, :, :], 0.0)
        step(dve.memset(halo_w.bitcast(F32), 0.0))

        dve.wait_ge(S["taps_in"], 16)
        step(dve.tensor_scalar(taps[:, :], taps[:, :], 0.5, None, ALU.mult))
        dve.wait_ge(S["consts_in"], 32)
        for dy, diagonal in ((0, early[:, 0:P]), (1, ident), (2, early[:, P:2 * P])):
            for k in range(2):
                for dx in range(3):
                    w = taps[:, 9 * k + 3 * dy + dx:9 * k + 3 * dy + dx + 1]
                    b = band_raw[:, 3 * k + dx, :]
                    if dy == 0:
                        last = dve.tensor_scalar(b, diagonal, w, None, ALU.mult)
                    else:
                        last = dve.scalar_tensor_tensor(b, diagonal, w, b, ALU.mult, ALU.add)
                    if dy == 2:
                        last.then_inc(S["bands_made"], 1)
            if dy < 2:
                step(last)
        def gray_rest(u):
            dve.wait_ge(x_in[u % 2], 16 * (u // 2 + 1))
            dve.wait_ge(S["gray_first"], u + 1)
            step(dve.scalar_tensor_tensor(gray, xs_img[:, u % 2, 1], GRAY[1], gray, ALU.mult, ALU.add))
            dve.scalar_tensor_tensor(gray, xs_img[:, u % 2, 2], GRAY[2], gray, ALU.mult, ALU.add)\
               .then_inc(S["gray_made"], 1)

        def gray_low(u):
            dve.wait_ge(S["gray_hi_made"], u + 1)
            dve.tensor_tensor(gray_lo[:, :, 1:1 + SIZE], gray, gray_hi[:, :, 1:1 + SIZE].bitcast(F32), ALU.subtract)\
               .then_inc(S["gray_split"], 1)

        gray_rest(0)
        dve.wait_ge(S["band_hi"], 1)
        dve.tensor_tensor(band[:, 1], band_raw, band[:, 0].bitcast(F32), ALU.subtract).then_inc(S["bands_split"], 1)
        gray_low(0)

        dve.wait_ge(S["halo_taps_in"], 48)
        step(dve.tensor_scalar(htap[:, 1], htap[:, 0], 0.5, None, ALU.mult))
        step(dve.tensor_copy(htap_r[:, :], htap[:, 1]))
        step(dve.tensor_tensor(htap[:, 2], htap[:, 1], htap_r[:, :].bitcast(F32), ALU.subtract))
        step(dve.tensor_scalar(htap[:, 2], htap[:, 2], cst[0:9, C_SEL + 1:C_SEL + 2], None, ALU.mult))
        step(dve.scalar_tensor_tensor(htap[:, 3], htap_r[:, :].bitcast(F32), cst[0:9, C_SEL:C_SEL + 1], htap[:, 2],
                                      ALU.mult, ALU.add))
        for t, dy, col in ((0, 2, P - 1), (1, 0, 0)):
            dve.tensor_copy(halo_w[:, t, :, col], htap[:, 3, dy:6:3]).then_inc(S["halo_made"], 1)
        dve.tensor_copy(before[:, :], early[:, 2 * P:3 * P]).then_inc(S["before_made"], 1)

        for w in range(3):
            dve.wait_ge(S["qkv_hi"], w + 1)
            dve.tensor_tensor(wqkv[w][:, 1], stage_qkv[:, w], wqkv[w][:, 0].bitcast(F32), ALU.subtract)\
               .then_inc(S["qkv_split"], 1)

        def sums(norm, rows, t):
            mark(dve.bn_stats(stats[:, norm, t, :], rows[:, t, :]))

        def moments(norm, made):
            settle()
            for t in range(2):
                last = dve.bn_aggr(mv[:, norm, t, :], stats[:, norm, t, :])
            last.then_inc(S[made], 1)

        def normalise(norm, dst, rows, u, have, made):
            dve.wait_ge(S[have], u + 1)
            for t in range(2):
                last = dve.tensor_scalar(dst[:, t, :], rows[:, t, :], mv[:, norm, t, 0:1], rstd[:, norm, t:t + 1],
                                         ALU.subtract, ALU.mult)
            last.then_inc(S[made], 1)

        def edge_sum(u, t):
            dve.wait_ge(S["edge_made"], 2 * u + t + 1)
            if u >= 4:
                dve.wait_ge(res_stored[u % 4], 16 * (u // 4))
            dve.tensor_tensor(h_all[:, u % 4, t], edge[:, t, 0], edge[:, t, 1], ALU.add).then_inc(S["h_made"], 1)

        def topk_logits(u):
            dve.wait_ge(S["gate_done"], u + 1)
            ps = ps_gate[:, 0:2 * EXPERTS].rearrange("p (t e) -> p t e", t=2)
            step(dve.tensor_reduce(gmax[:, :], ps, AX.X, ALU.max))
            dve.tensor_tensor(logit[:, :, :], ps, gmax[:, :].unsqueeze(2).broadcast_to([P, 2, EXPERTS]), ALU.subtract)\
               .then_inc(S["logit_made"], 1)

        def pairs(a, n):
            return a[:, :].unsqueeze(2).broadcast_to([P, 2, n])

        def top_sum(u):
            dve.wait_ge(S["gexp_made"], u + 1)
            mark(dve.tensor_reduce(gsum[:, :], gexp[:, :, :], AX.X, ALU.add))

        def top_reciprocal():
            settle()
            mark(dve.reciprocal(grec[:, :], gsum[:, :]))

        def top_softmax():
            settle()
            mark(dve.tensor_tensor(gprob[:, :, :], gexp[:, :, :], pairs(grec, EXPERTS), ALU.mult))

        def top_best():
            settle()
            for t in range(2):
                last = dve.max(best[:, t, :], gprob[:, t, :])
            mark(last)

        def top_which():
            settle()
            for t in range(2):
                last = dve.max_index(best_at[:, t, :], best[:, t, :], gprob[:, t, :])
            mark(last)
            mark(dve.tensor_tensor(den[:, :], best[:, :, 0], best[:, :, 1], ALU.add))

        def top_which_f():
            settle()
            mark(dve.tensor_copy(best_f[:, :, :], best_at[:, :, 0:TOP]))
            mark(dve.tensor_scalar(den[:, :], den[:, :], EPS_TOP, None, ALU.add))

        def top_chosen(u):
            settle()
            iota = cst[:, C_IOTA:C_IOTA + EXPERTS].unsqueeze(1).unsqueeze(1).broadcast_to([P, 2, TOP, EXPERTS])
            mark(dve.tensor_tensor(chosen_all[:, 2 * u:2 * u + 2], iota,
                                   best_f[:, :, :].unsqueeze(3).broadcast_to([P, 2, TOP, EXPERTS]), ALU.is_equal))
            mark(dve.reciprocal(den[:, :], den[:, :]))

        def top_hit(u):
            if u >= 1:
                dve.wait_ge(S["rank_done"], u)
                mark(dve.tensor_copy(earlier[:, 0, :], earlier[:, 2, :]))
            settle()
            mark(dve.tensor_tensor(hit[:, :, :], chosen_all[:, 2 * u:2 * u + 2, 0, :], chosen_all[:, 2 * u:2 * u + 2, 1, :], ALU.add))
            mark(dve.tensor_tensor(weights_at(u), best[:, :, 0:TOP], pairs(den, TOP), ALU.mult))

        def top_earlier():
            settle()
            mark(dve.tensor_tensor(earlier[:, 1, :], earlier[:, 0, :], hit[:, 0, :], ALU.add))

        def top_all(u):
            settle()
            dve.tensor_tensor(earlier[:, 2, :], earlier[:, 1, :], hit[:, 1, :], ALU.add).then_inc(S["hits_made"], 1)
            w = weights_at(u)
            mark(dve.tensor_tensor(wsum[:, :], w[:, :, 0], w[:, :, 1], ALU.add))

        def weights_at(u):
            return weight[:, 2 * TOP * u:2 * TOP * (u + 1)].rearrange("p (t k) -> p t k", t=2)

        def add_bias(u):
            settle()
            h = h_all[:, u % 4]
            for t in range(2):
                dve.scalar_tensor_tensor(h[:, t], bo_all[:, :], wsum[:, t:t + 1], h[:, t],
                                         ALU.mult, ALU.add).then_inc(S["res_made"], 1)

        def topk_places(u):
            dve.wait_ge(S["rank_done"], u + 1)
            base = cst[:, C_BASE:C_BASE + EXPERTS].unsqueeze(1).broadcast_to([P, 2, EXPERTS])
            dve.tensor_tensor(place[:, :, :], ps_rank[:, 0:2 * EXPERTS].rearrange("p (t e) -> p t e", t=2), base, ALU.add)\
               .then_inc(S["rank_read"], 1)
            dve.wait_ge(S["rank_read"], u + 1)
            step(dve.tensor_tensor(placed[:, :, :, :], chosen_all[:, 2 * u:2 * u + 2],
                                   place[:, :, :].unsqueeze(2).broadcast_to([P, 2, TOP, EXPERTS]), ALU.mult))
            step(dve.tensor_reduce(place_f[:, :, :], placed[:, :, :, :], AX.X, ALU.add))
            dve.tensor_copy(place_i[:, 2 * u:2 * u + 2, :], place_f[:, :, :])\
               .then_inc(S["places_made"], 1)

        for s in range(STEPS):
            new, old, gated = live(s), live(s - 2), live(s - 3)
            h_new, h_old = h_all[:, s % 4], h_all[:, (s - 2) % 4]
            if live(s - 1):
                u = s - 1
                dve.wait_ge(S["xT_hi_made"], u + 1)
                dve.tensor_tensor(xT_f[:, 1], ps_xT[:, :].rearrange("p (k n) -> p k n", k=KD),
                                  xT_f[:, 0].bitcast(F32), ALU.subtract).then_inc(S["xT_split"], 1)
            if live(s + 1):
                gray_rest(s + 1)
            if old:
                dve.wait_ge(S["probs_made"], 2 * (s - 1))
                dve.reciprocal(srec[:, :], ssum[:, :]).then_inc(S["srec_made"], 1)
            if new:
                edge_sum(s, 0)
                edge_sum(s, 1)
            if gated and new:
                topk_logits(s - 3)
            if live(s + 1):
                gray_low(s + 1)
            if old:
                dve.wait_ge(S["srec_made"], s - 1)
                dve.wait_ge(S["pv_done"], s - 1)
                for t in range(2):
                    dve.scalar_tensor_tensor(h_old[:, t], ps_pv[:, t * D:(t + 1) * D], srec[:, t:t + 1],
                                             h_old[:, t], ALU.mult, ALU.add).then_inc(S["h2_made"], 1)
            if gated and new:
                top_sum(s - 3)
            if old:
                for t in range(2):
                    dve.wait_ge(S["h2_made"], 2 * (s - 2) + t + 1)
                    sums(1, h_old, t)
            if gated and new:
                top_reciprocal()
            if old:
                moments(1, "mv2_made")
            if gated and not new:
                topk_logits(s - 3)
                top_sum(s - 3)
                top_reciprocal()
            if old and not live(s - 1):
                if s >= 4:
                    dve.wait_ge(scattered[s % 2], 64 * ((s - 2) // 2))
                normalise(1, xn2[:, s % 2], h_old, s - 2, "rstd2_made", "xn2_made")
            if gated:
                top_softmax()
            if gated:
                top_best()
            if gated:
                top_which()
            if old and live(s - 1):
                if s >= 4:
                    dve.wait_ge(scattered[s % 2], 64 * ((s - 2) // 2))
                normalise(1, xn2[:, s % 2], h_old, s - 2, "rstd2_made", "xn2_made")
            if new:
                dve.wait_ge(S["h_made"], 2 * (s + 1))
                for t in range(2):
                    sums(0, h_new, t)
            if gated:
                top_which_f()
            if new:
                moments(0, "mv1_made")
            if gated:
                top_chosen(s - 3)
            if gated:
                top_hit(s - 3)
                top_earlier()
                top_all(s - 3)
                if not new:
                    topk_places(s - 3)
            if new and not live(s + 1):
                if s >= 1:
                    dve.wait_ge(S["xT_done"], s)
                normalise(0, xn1, h_new, s, "rstd1_made", "xn1_made")
            if live(s - 1):
                u = s - 1
                dve.wait_ge(S["s_done"], u + 1)
                if u >= 1:
                    dve.wait_ge(S["probs_made"], 2 * u)
                for t in range(2):
                    last = dve.tensor_tensor_reduce(masked[:, t], ps_s[:, t * P:(t + 1) * P], cst[:, C_MASK:C_MASK + P],
                                                    1.0, NEVER, ALU.add, ALU.max, smax[:, t:t + 1])
                step(last)
                dve.tensor_scalar(nsmax[:, :], smax[:, :], -1.0, None, ALU.mult).then_inc(S["masked_made"], 1)
            if new and live(s + 1):
                if s >= 1:
                    dve.wait_ge(S["xT_done"], s)
                normalise(0, xn1, h_new, s, "rstd1_made", "xn1_made")
            if gated and s < STEPS - 1:
                add_bias(s - 3)
            if live(s - 1):
                u = s - 1
                dve.wait_ge(S["small_in"], 80)
                dve.wait_ge(S["v_done"], u + 1)
                if u >= 1:
                    dve.wait_ge(S["pv_done"], u)
                dve.tensor_tensor(v_sb, ps_v[:, :].rearrange("p (t e) -> p t e", t=2),
                                  bv_all[:, :].unsqueeze(1).broadcast_to([P, 2, D]), ALU.add).then_inc(S["v_made"], 1)
            if gated and new:
                topk_places(s - 3)

        dve.wait_ge(S["count_done"], 1)
        rows_of_expert = ps_count
        dve.tensor_tensor(pad_f[:, :], rows_of_expert[0:1], cst[0:1, C_BASE:C_BASE + EXPERTS], ALU.add)
        step(dve.tensor_scalar(tiles_i[:, 0], rows_of_expert, float(P - 1), None, ALU.add))
        dve.tensor_copy(pad_i[:, :], pad_f[:, :]).then_inc(S["pads_set"], 1)
        add_bias(IMAGES - 1)
        step(dve.tensor_scalar(tiles_i[:, 1], tiles_i[:, 0], P.bit_length() - 1, None, ALU.logical_shift_right))
        step(dve.tensor_copy(tiles_f[:, :], tiles_i[:, 1]))
        step(dve.tensor_tensor_scan(ends[:, :], one8[:, :], tiles_f[:, :], 0.0, ALU.mult, ALU.add))
        whole = [1, MAX_TILES, EXPERTS]
        tile_no = cst[0:1, C_TILE:C_TILE + MAX_TILES]
        step(dve.tensor_tensor(passed, tile_no.unsqueeze(2).broadcast_to(whole),
                               ends[0:1, :].unsqueeze(1).broadcast_to(whole), ALU.is_ge))
        step(dve.tensor_tensor(passed_n, passed, tiles_f[0:1, :].unsqueeze(1).broadcast_to(whole), ALU.mult))
        step(dve.tensor_reduce(expert_of, passed, AX.X, ALU.add))
        step(dve.tensor_reduce(start_of, passed_n, AX.X, ALU.add))
        step(dve.tensor_tensor(tiles_in, tile_no, start_of, ALU.subtract))
        step(dve.tensor_scalar(rows_before, tiles_in, float(P), None, ALU.mult))
        dve.scalar_tensor_tensor(tab_row[:, :], expert_of, float(REGION), rows_before, ALU.mult, ALU.add)
        mark(dve.tensor_scalar(of_later, expert_of[:, 0:3], float(EXPERTS // 2), None, ALU.is_ge))
        step(dve.tensor_scalar(need, expert_of, float(EXPERTS - 1), float(KD), ALU.min, ALU.mult))
        dve.tensor_scalar(tab_pad[:, :], of_later, float(16 * EXPERTS // 2), 1.0, ALU.mult, ALU.add)
        dve.tensor_scalar(tab_w[:, :], need, float(KD), None, ALU.add)
        dve.tensor_scalar(tab_b[:, :], expert_of, float(EXPERTS - 1), float(2 * H), ALU.min, ALU.mult)\
           .then_inc(S["tables_made"], 1)
        dve.wait_ge(S["tables_made"], 1)

        step(dve.tensor_scalar(start_of, expert_of, float(EXPERTS), float(MAX_TILES * P), ALU.is_ge, ALU.mult))
        dve.scalar_tensor_tensor(tab_out[:, :], tile_no, float(P), start_of, ALU.mult, ALU.add).then_inc(S["out_rows_made"], 1)

        step(dve.tensor_tensor(shift[:, :], ends[:, :], tiles_f[:, :], ALU.subtract))
        step(dve.scalar_tensor_tensor(shift[:, :], shift[:, :], float(P), cst[:, C_BASE:C_BASE + EXPERTS], ALU.mult, ALU.subtract))
        each = [P, TILES * TOP, EXPERTS]
        step(dve.tensor_tensor(shifts, chosen_all[:, :, :, :].rearrange("p t k e -> p (t k) e"),
                               shift[:, :].unsqueeze(1).broadcast_to(each), ALU.mult))
        step(dve.tensor_reduce(shift_of, shifts, AX.X, ALU.add))
        dve.tensor_tensor(gated_i[:, :, :].rearrange("p t k -> p (t k)"), place_i[:, :, :].rearrange("p t k -> p (t k)"),
                          shift_of, ALU.add)
        dve.tensor_scalar(res_free_at, ends[0:1, RES_EXPERTS - 1:RES_EXPERTS], 1.0, None, ALU.max)
        dve.tensor_scalar(real_i[:, 0:1], ends[0:1, EXPERTS - 1:EXPERTS], 1.0, None, ALU.add)
        step(dve.tensor_copy(real_i[:, 1:2], ends[0:1, EXPERTS - 1:EXPERTS]))
        dve.tensor_scalar(real_at[:, :], real_i[:, :], 1, 4, ALU.logical_shift_right, ALU.logical_shift_left)\
           .then_inc(S["gated_places_made"], 1)

        dve.wait_ge(S["b1_in"], 16 * EXPERTS)

        def e_low(j, p):
            dve.wait_ge(S["e_hi"], j + 1)
            dve.tensor_tensor(xT_e[:, p, 1], ps_et[p][:, 0:KD * P].rearrange("p (k n) -> p k n", k=KD),
                              xT_e[:, p, 0].bitcast(F32), ALU.subtract).then_inc(S["e_split"], 1)

        def e_gate(j, p, stored, first=False):
            off = dve.value_load(tab_b[0:1, ds(j, 1)], min_val=0, max_val=(EXPERTS - 1) * 2 * H)
            dve.wait_ge(S["e_b_done"], j + 1)
            if not first:
                dve.wait_ge(S["e_sig_made"], j - 1)
            dve.tensor_tensor(e_b[:, p], ps_b[p][:, :], b1_all[:, ds(off + H, H)], ALU.add).then_inc(S["e_b_made"], 1)
            dve.wait_ge(S["e_a_done"], j + 1)
            dve.tensor_tensor(e_a[:, p], ps_a[p][:, :], b1_all[:, ds(off, H)], ALU.add).then_inc(S["e_a_read"], 1)
            dve.wait_ge(S["e_a_read"], j + 1)
            dve.wait_ge(S["e_sig_made"], j + 1)
            if not first:
                dve.wait_ge(e_stored[p], stored)
            dve.tensor_tensor(e_out[:, p], e_a[:, p], e_sig[:, p], ALU.mult).then_inc(S["e_out_made"], 1)

        e_low(0, 0)
        e_low(1, 1)
        e_gate(0, 0, 0, True)
        e_low(2, 0)
        e_gate(1, 1, 0, True)

        def two_tiles(i):
            e_low(2 * i + 1, 1)
            e_gate(2 * i, 0, 16 * i)
            e_low(2 * i + 2, 0)
            e_gate(2 * i + 1, 1, 16 * i)

        with dve.Fori(1, MAX_TILES // 2 - 1) as i:
            two_tiles(i)
        dve.wait_ge(S["wo_hi"], 1)
        dve.tensor_tensor(wo_h[:, 1], wo_raw, wo_h[:, 0].bitcast(F32), ALU.subtract).then_inc(S["wo_split"], 1)
        two_tiles(MAX_TILES // 2 - 1)
        e_gate(MAX_TILES - 1, 0, 16 * (MAX_TILES // 2))

        def c_sum(t, b, loaded):
            dve.wait_ge(c_loaded[1][b], loaded)
            dve.wait_ge(S["c_first"], t + 1)
            at = ds(t * H, H)
            dve.scalar_tensor_tensor(weighed[:, b], top2[:, at], weight_of(t, 1), top1[:, at], ALU.mult, ALU.add)\
               .then_inc(S["c_sum"], 1)

        def c_low(t, p):
            dve.wait_ge(S["c_hi"], t + 1)
            dve.tensor_tensor(sumT[p][:, 1], ps_ct[p][:, :].rearrange("p (k n) -> p k n", k=KH),
                              sumT[p][:, 0].bitcast(F32), ALU.subtract).then_inc(S["c_split"], 1)

        def c_result(t, b, turn, first=False):
            dve.wait_ge(S["c_y"], t + 1)
            dve.wait_ge(S["c_res"], 16 * TILES)
            if not first:
                dve.wait_ge(c_stored[b], turn - 16)
            dve.tensor_tensor(result[:, b], ps_y[b % 2][:, 0:D], res_in[:, ds(t * D, D)], ALU.add).then_inc(S["c_out"], 1)

        c_sum(0, 0, 16)
        for t in range(NB + 1):
            c_sum(t + 1, (t + 1) % NB, 16 * ((t + 1) // NB + 1))
            c_low(t, t % 2)
            if t >= 1:
                c_result(t - 1, t - 1, 16, True)
        with dve.Fori(1, TILES // NB - 1) as i:
            for b in range(NB):
                t = NB * i + b + 1
                c_sum(t + 1, (b + 2) % NB, 16 * i + 16 * ((b + 2) // NB + 1))
                c_low(t, (b + 1) % 2)
                c_result(t - 1, b, 16 * i + 16)
        for t in range(TILES - NB + 1, TILES):
            if t + 1 < TILES:
                c_sum(t + 1, (t + 1) % NB, 16 * ((t + 1) // NB + 1))
            c_low(t, t % 2)
            c_result(t - 1, (t - 1) % NB, 16 * ((t - 1) // NB + 1))
        c_result(TILES - 1, NB - 1, 16 * (TILES // NB))

    @block.tensor
    def _(pe):
        def conv(u, t):
            pe.wait_ge(S["gray_split"], u + 1)
            if u >= 1:
                pe.wait_ge(S["edge_made"], 2 * u + t - 1)
            for k in range(2):
                dst = ps_conv[t][:, k * SIZE:(k + 1) * SIZE]
                for n, (g, f, dx) in enumerate(three(range(3))):
                    pe.matmul(dst, band[:, g, 3 * k + dx, :], (gray_hi, gray_lo)[f][:, t, dx:dx + SIZE],
                              start=(n == 0), stop=False)
                if k == 0:
                    pe.wait_ge(S["halo_made"], 2)
                    pe.wait_ge(halo_moved[t], 16 * 3 * (u + 1))
                last = pe.matmul(dst, halo_w[:, t, k, :], halo_in[:, t, :], start=False, stop=True)
            last.then_inc(S["conv_done"], 1)

        def project(u, w, ps, done):
            for m in range(KD):
                for n, (g, f, k) in enumerate(three(range(KD))):
                    last = pe.matmul(ps[:, m * SIZE:(m + 1) * SIZE], wqkv[w][:, g, k, m * P:(m + 1) * P],
                                     xT_f[:, f, k, :], start=(n == 0), stop=(n == 3 * KD - 1))
            last.then_inc(S[done], 1)

        def gate(u):
            pe.wait_ge(S["xn2T_made"], u + 1)
            pe.wait_ge(S["masked_made"], min(u + 2, IMAGES))
            for t in range(2):
                for k in range(KD):
                    last = pe.matmul(ps_gate[:, t * EXPERTS:(t + 1) * EXPERTS], xn2T[:, k, t * P:(t + 1) * P],
                                     wg_sb[:, k, :], start=(k == 0), stop=(k == KD - 1))
            last.then_inc(S["gate_done"], 1)

        def attend(u):
            pe.wait_ge(S["pT_made"], u + 1)
            pe.wait_ge(S["v_made"], u + 1)
            for t in range(2):
                last = pe.matmul(ps_pv[:, t * D:(t + 1) * D], probsT[:, t], v_sb[:, t], start=True, stop=True)
            last.then_inc(S["pv_done"], 1)

        def rank(u):
            pe.wait_ge(S["hits_made"], u + 1)
            pe.wait_ge(S["before_made"], 1)
            pe.matmul(ps_rank[:, 0:2 * EXPERTS], before[:, :], hit[:, :, :].rearrange("p t e -> p (t e)"),
                      start=True, stop=False)
            pe.matmul(ps_rank[:, 0:2 * EXPERTS], ones[:, :], earlier[:, 0:2, :].rearrange("p t e -> p (t e)"),
                      start=False, stop=True).then_inc(S["rank_done"], 1)

        pe.wait_ge(S["consts_in"], 32)
        pe.wait_ge(S["bands_split"], 1)
        for s in range(STEPS):
            if live(s):
                conv(s, 0)
            if live(s - 1):
                u = s - 1
                pe.wait_ge(S["xn1_made"], u + 1)
                if u >= 1:
                    pe.wait_ge(S["xT_split"], u)
                for k in range(KD):
                    for t in range(2):
                        last = pe.transpose(ps_xT[:, k * SIZE + t * P:k * SIZE + (t + 1) * P],
                                            xn1[:, t, k * P:(k + 1) * P], ident)
                last.then_inc(S["xT_done"], 1)
            if live(s - 4) and live(s - 1):
                rank(s - 4)
            if live(s - 2):
                u = s - 2
                pe.wait_ge(S["probs_made"], 2 * (u + 1))
                if u >= 1:
                    pe.wait_ge(S["h2_made"], 2 * u)
                for t in range(2):
                    last = pe.transpose(ps_pT[:, t * P:(t + 1) * P], probs[:, t], ident)
                last.then_inc(S["pT_done"], 1)
            if live(s):
                conv(s, 1)
            order = ((gate, s - 3), (attend, s - 2)) if live(s) else ((attend, s - 2), (gate, s - 3))
            for part, u in order:
                if live(u):
                    part(u)
            if live(s - 1):
                u = s - 1
                pe.wait_ge(S["xT_split"], u + 1)
                pe.wait_ge(S["qkv_split"], 3)
                if u >= 3:
                    pe.wait_ge(S["rank_read"], u - 2)
                project(u, 0, ps_q, "q_done")
                if u >= 2:
                    pe.wait_ge(S["xn2T_made"], u - 1)
                project(u, 1, ps_k, "k_done")
                if u >= 1:
                    pe.wait_ge(S["v_made"], u)
                for t in range(2):
                    for n, (g, f, k) in enumerate(three(range(KD))):
                        last = pe.matmul(ps_v[:, t * D:(t + 1) * D], xT_f[:, g, k, t * P:(t + 1) * P],
                                         wqkv[2][:, f, k, :], start=(n == 0), stop=(n == 3 * KD - 1))
                last.then_inc(S["v_done"], 1)
                pe.wait_ge(S["q_made"], KD * (u + 1))
                if not live(s):
                    rank(s - 3)
                pe.wait_ge(S["k_made"], KD * (u + 1))
                if u >= 2:
                    pe.wait_ge(S["logit_made"], u - 1)
                for t in range(2):
                    for m in range(KD):
                        last = pe.matmul(ps_s[:, t * P:(t + 1) * P], qT[:, m, t * P:(t + 1) * P],
                                         kT[:, m, t * P:(t + 1) * P], start=(m == 0), stop=(m == KD - 1))
                last.then_inc(S["s_done"], 1)
            if live(s - 2):
                u = s - 2
                pe.wait_ge(S["xn2_made"], u + 1)
                if live(s - 1):
                    pe.wait_ge(S["k_made"], KD * s)
                for k in range(KD):
                    for t in range(2):
                        last = pe.transpose(ps_xn2T[:, k * SIZE + t * P:k * SIZE + (t + 1) * P],
                                            xn2[:, u % 2, t, k * P:(k + 1) * P], ident)
                last.then_inc(S["xn2T_done"], 1)
            if not live(s - 1) and live(s - 3):
                rank(s - 3)
        pe.matmul(ps_count, ones[:, :], earlier[:, 2, :], start=True, stop=True).then_inc(S["count_done"], 1)

        def e_transpose(j, p, loaded, first=False):
            pe.wait_ge(e_loaded[p], loaded)
            if not first:
                pe.wait_ge(S["e_split"], j - 1)
            for k in range(KD):
                last = pe.transpose(ps_et[p][:, k * P:(k + 1) * P], e_in[:, p, k * P:(k + 1) * P], ident)
            last.then_inc(S["e_T"], 1)

        def chunks_for(j):
            return pe.value_load(tab_w[0:1, ds(j, 1)], min_val=KD, max_val=CHUNKS)

        def e_product(j, p, need, first=False):
            off = (need - KD) * 2 * H
            pe.wait_ge(S["w1_lo_made"], need)
            pe.wait_ge(S["e_split"], j + 1)
            for ps, col, done, read in ((ps_b[p], H, "e_b_done", "e_b_made"), (ps_a[p], 0, "e_a_done", "e_a_read")):
                if not first:
                    pe.wait_ge(S[read], j - 1)
                for n, (g, f, k) in enumerate(three(range(KD))):
                    last = pe.matmul(ps[:, :], xT_e[:, p, g, k, :], (w1_hi, w1_lo)[f][:, ds(off + k * 2 * H + col, H)],
                                     start=(n == 0), stop=(n == 3 * KD - 1))
                last.then_inc(S[done], 1)

        pe.wait_ge(S["tables_made"], 1)
        e_transpose(0, 0, 16, True)
        e_transpose(1, 1, 16, True)
        e_product(0, 0, chunks_for(0), True)
        e_transpose(2, 0, 32)
        e_product(1, 1, chunks_for(1), True)
        with pe.Fori(1, MAX_TILES // 2) as i:
            need = [chunks_for(2 * i + p) for p in range(2)]
            e_transpose(2 * i + 1, 1, 16 * i + 16)
            e_product(2 * i, 0, need[0])
            e_transpose(2 * i + 2, 0, 16 * i + 32)
            e_product(2 * i + 1, 1, need[1])
        e_product(MAX_TILES - 1, 0, chunks_for(MAX_TILES - 1))

        def c_transpose(t, b, p, first=False):
            pe.wait_ge(S["c_sum"], t + 1)
            if not first:
                pe.wait_ge(S["c_split"], t - 1)
            for k in range(KH):
                last = pe.transpose(ps_ct[p][:, k * P:(k + 1) * P], weighed[:, b, k * P:(k + 1) * P], ident)
            last.then_inc(S["c_T"], 1)

        def c_product(t, p, first=False):
            pe.wait_ge(S["c_split"], t + 1)
            if not first:
                pe.wait_ge(S["c_out"], t - 1)
            for n, (g, f, k) in enumerate(three(range(KH))):
                last = pe.matmul(ps_y[p][:, 0:D], sumT[p][:, g, k, :], wo_h[:, f, k, :],
                                 start=(n == 0), stop=(n == 3 * KH - 1))
            last.then_inc(S["c_y"], 1)

        pe.wait_ge(S["wo_split"], 1)
        c_transpose(0, 0, 0, True)
        for t in range(NB):
            c_transpose(t + 1, (t + 1) % NB, (t + 1) % 2, t + 1 < 2)
            c_product(t, t % 2, t < 2)
        with pe.Fori(1, TILES // NB - 1) as i:
            for b in range(NB):
                t = NB * i + b
                c_transpose(t + 1, (b + 1) % NB, (b + 1) % 2)
                c_product(t, b % 2)
        for t in range(TILES - NB, TILES):
            if t + 1 < TILES:
                c_transpose(t + 1, (t + 1) % NB, (t + 1) % 2)
            c_product(t, t % 2)


def kernel(x, L0_tok_scharr, L0_attn_Wq, L0_attn_bq, L0_attn_Wk, L0_attn_bk, L0_attn_Wv, L0_attn_bv,
           L0_ffn_Wg, L0_ffn_W1, L0_ffn_b1, L0_ffn_Wo, L0_ffn_bo):
    import numpy as np
    from concourse import bacc, mybir as mb
    from concourse.bass_utils import run_bass_kernel_spmd

    def laid(a, *axes):
        a = np.asarray(a)
        return np.ascontiguousarray(a.transpose(*axes) if axes else a)

    arrays = {
        "x": laid(x), "scharr": laid(L0_tok_scharr),
        "wqT": laid(L0_attn_Wq, 1, 0), "wkT": laid(L0_attn_Wk, 1, 0), "wvT": laid(L0_attn_Wv, 1, 0),
        "bq": laid(L0_attn_bq), "bk": laid(L0_attn_bk), "bv": laid(L0_attn_bv),
        "wgT": laid(L0_ffn_Wg, 1, 0), "w1T": laid(L0_ffn_W1, 2, 0, 1), "b1": laid(L0_ffn_b1),
        "woT": laid(L0_ffn_Wo, 1, 0), "bo": laid(L0_ffn_bo), "consts": shape_constants(), "zeros": np.zeros((P, H), np.float32),
    }
    nc = bacc.Bacc("TRN2", target_bir_lowering=False, num_devices=1)
    aps = {n: nc.dram_tensor(n, a.shape, mb.dt.from_np(a.dtype), kind="ExternalInput").ap() for n, a in arrays.items()}
    out = nc.dram_tensor("out", (TILES * P, D), mb.dt.float32, kind="ExternalOutput").ap()
    build(nc, out=out, **aps)
    r = run_bass_kernel_spmd(nc, [arrays], core_ids=[0])
    return r.results[0]["out"].reshape(IMAGES, SIZE, D)
```
